# Optimizing a Trainium2 kernel written in Bass

```python
import numpy as np
import jax
import jax.numpy as jnp

def _softmax(x, axis=-1):
    return jax.nn.softmax(x, axis=axis)

def _gelu(x):
    return jax.nn.gelu(x, approximate=True)

def _silu(x):
    return jax.nn.silu(x)

def _sigmoid(x):
    return jax.nn.sigmoid(x)

def _layernorm(x, axis=-1, eps=1e-05):
    m = jnp.mean(x, axis=axis, keepdims=True)
    v = jnp.var(x, axis=axis, keepdims=True)
    return (x - m) / jnp.sqrt(v + eps)

def _scatter_add(tgt, idx, src, axis=0):
    return tgt.at[idx].add(src)

def _segment_sum(src, seg, n):
    return jax.ops.segment_sum(src, seg, n)
kernel_name = 'mk_gps_d1_gnn_r32_b9fa19'

def setup_inputs(seed: int=0):
    np.random.seed(seed)
    _w = jnp.asarray

    def _rec_inputs():
        import jax
        import jax.numpy as jnp
        _gk = jax.random.key(seed)
        x = -0.000202 + 1 * jax.random.normal(jax.random.fold_in(_gk, 1), (3125, 256), jnp.float32)
        src = jax.random.randint(jax.random.fold_in(_gk, 2), (50000,), 0, 3125, jnp.int32)
        dst = jax.random.randint(jax.random.fold_in(_gk, 3), (50000,), 0, 3125, jnp.int32)
        _o = jnp.argsort(dst, stable=True)
        src = src[_o]
        dst = dst[_o]
        return (x, src, dst)
    x, src, dst = _rec_inputs()

    def _L0_gnn_setup():
        import jax, jax.numpy as jnp
        import numpy as np
        N_NODES = 25000
        N_EDGES = 12500
        D_IN = 256
        D_OUT = 256
        HEADS = 8
        HEAD_DIM = D_OUT // HEADS
        NEG_SLOPE = 0.2
        LN_EPS = 1e-05

        def layer_norm(x, g, b):
            mu = jnp.mean(x, axis=-1, keepdims=True)
            var = jnp.mean((x - mu) ** 2, axis=-1, keepdims=True)
            return (x - mu) * jax.lax.rsqrt(var + LN_EPS) * g + b

        def gelu_tanh(x):
            c = np.sqrt(2.0 / np.pi).astype(np.float32)
            return 0.5 * x * (1.0 + jnp.tanh(c * (x + 0.044715 * x ** 3)))
        key = jax.random.key(seed)
        ks = jax.random.split(key, 16)
        s_in = 1.0 / np.sqrt(D_IN)
        s_out = 1.0 / np.sqrt(D_OUT)
        s_ff = 1.0 / np.sqrt(4 * D_OUT)
        return {'x': jax.random.normal(ks[0], (N_NODES, D_IN), jnp.float32), 'edge_index': jax.random.randint(ks[1], (2, N_EDGES), 0, N_NODES, jnp.int64), 'W': jax.random.normal(ks[2], (D_IN, HEADS * HEAD_DIM), jnp.float32) * s_in, 'att_src': jax.random.normal(ks[3], (HEADS, HEAD_DIM), jnp.float32) * s_out, 'att_dst': jax.random.normal(ks[4], (HEADS, HEAD_DIM), jnp.float32) * s_out, 'bias': jnp.zeros((D_OUT,), jnp.float32), 'W_res': jax.random.normal(ks[5], (D_IN, D_OUT), jnp.float32) * s_in, 'ln1_g': jnp.ones((D_IN,), jnp.float32), 'ln1_b': jnp.zeros((D_IN,), jnp.float32), 'ln2_g': jnp.ones((D_OUT,), jnp.float32), 'ln2_b': jnp.zeros((D_OUT,), jnp.float32), 'ffn_w1': jax.random.normal(ks[6], (D_OUT, 4 * D_OUT), jnp.float32) * s_out, 'ffn_b1': jnp.zeros((4 * D_OUT,), jnp.float32), 'ffn_w2': jax.random.normal(ks[7], (4 * D_OUT, D_OUT), jnp.float32) * s_ff, 'ffn_b2': jnp.zeros((D_OUT,), jnp.float32)}
    _L0_gnn_all = _L0_gnn_setup()
    _L0_gnn_in = {k: v for k, v in _L0_gnn_all.items() if k in ('W', 'att_src', 'att_dst', 'bias', 'W_res', 'ln1_g', 'ln1_b', 'ln2_g', 'ln2_b', 'ffn_w1', 'ffn_b1', 'ffn_w2', 'ffn_b2')}
    del _L0_gnn_all

    def _L0_mix_setup():
        import jax, jax.numpy as jnp
        import numpy as np
        DIM = 256
        HEADS = 4
        DIM_HEAD = 32
        NUM_MEM = 4
        HIDDEN = HEADS * DIM_HEAD
        SCALE = DIM_HEAD ** (-0.5)

        def rmsnorm(x, g):
            n = jnp.linalg.norm(x, axis=-1, keepdims=True)
            return x / jnp.maximum(n, 1e-12) * g * x.shape[-1] ** 0.5
        key = jax.random.key(seed)
        ks = jax.random.split(key, 8)
        B, N = (4, 512)
        return {'x': jax.random.normal(ks[0], (B, N, DIM), jnp.float32), 't': jax.random.normal(ks[1], (B,), jnp.float32), 'w_qkv': jax.random.normal(ks[2], (DIM, 3 * HIDDEN), jnp.float32) * 0.02, 'mem_kv': jax.random.normal(ks[3], (2, HEADS, DIM_HEAD, NUM_MEM), jnp.float32), 'w_out': jax.random.normal(ks[4], (HIDDEN, DIM), jnp.float32) * 0.02, 'b_out': jnp.zeros((DIM,), jnp.float32), 'g_out': jnp.ones((DIM,), jnp.float32), 'g_pre': jnp.ones((DIM,), jnp.float32)}
    _L0_mix_all = _L0_mix_setup()
    _L0_mix_in = {k: v for k, v in _L0_mix_all.items() if k in ('t', 'w_qkv', 'mem_kv', 'w_out', 'b_out', 'g_out', 'g_pre')}
    del _L0_mix_all

    def _L0_ffn_setup():
        import jax, jax.numpy as jnp
        import numpy as np
        TOP_K = 2
        LN_EPS = 1e-05
        key = jax.random.key(seed)
        ks = jax.random.split(key, 8)
        B, S, D, E, H = (16, 1024, 256, 8, 1024)
        x = jax.random.normal(ks[0], (B, S, D), dtype=jnp.float32)
        Wr = jax.random.normal(ks[1], (D, E), dtype=jnp.float32) * 0.1
        br = jnp.zeros((E,), dtype=jnp.float32)
        ln_g = jnp.ones((E, D), dtype=jnp.float32)
        ln_b = jnp.zeros((E, D), dtype=jnp.float32)
        W1 = jax.random.normal(ks[2], (E, D, H), dtype=jnp.float32) * (1.0 / np.sqrt(D))
        b1 = jnp.zeros((E, H), dtype=jnp.float32)
        W2 = jax.random.normal(ks[3], (E, H, D), dtype=jnp.float32) * (1.0 / np.sqrt(H))
        b2 = jnp.zeros((E, D), dtype=jnp.float32)
        return {'x': x, 'Wr': Wr, 'br': br, 'ln_g': ln_g, 'ln_b': ln_b, 'W1': W1, 'b1': b1, 'W2': W2, 'b2': b2}
    _L0_ffn_all = _L0_ffn_setup()
    _L0_ffn_in = {k: v for k, v in _L0_ffn_all.items() if k in ('Wr', 'br', 'ln_g', 'ln_b', 'W1', 'b1', 'W2', 'b2')}
    del _L0_ffn_all
    return {'x': x, 'src': src, 'dst': dst, 'L0_gnn_W': _L0_gnn_in['W'], 'L0_gnn_att_src': _L0_gnn_in['att_src'], 'L0_gnn_att_dst': _L0_gnn_in['att_dst'], 'L0_gnn_bias': _L0_gnn_in['bias'], 'L0_gnn_W_res': _L0_gnn_in['W_res'], 'L0_gnn_ln1_g': _L0_gnn_in['ln1_g'], 'L0_gnn_ln1_b': _L0_gnn_in['ln1_b'], 'L0_gnn_ln2_g': _L0_gnn_in['ln2_g'], 'L0_gnn_ln2_b': _L0_gnn_in['ln2_b'], 'L0_gnn_ffn_w1': _L0_gnn_in['ffn_w1'], 'L0_gnn_ffn_b1': _L0_gnn_in['ffn_b1'], 'L0_gnn_ffn_w2': _L0_gnn_in['ffn_w2'], 'L0_gnn_ffn_b2': _L0_gnn_in['ffn_b2'], 'L0_mix_t': _L0_mix_in['t'], 'L0_mix_w_qkv': _L0_mix_in['w_qkv'], 'L0_mix_mem_kv': _L0_mix_in['mem_kv'], 'L0_mix_w_out': _L0_mix_in['w_out'], 'L0_mix_b_out': _L0_mix_in['b_out'], 'L0_mix_g_out': _L0_mix_in['g_out'], 'L0_mix_g_pre': _L0_mix_in['g_pre'], 'L0_ffn_Wr': _L0_ffn_in['Wr'], 'L0_ffn_br': _L0_ffn_in['br'], 'L0_ffn_ln_g': _L0_ffn_in['ln_g'], 'L0_ffn_ln_b': _L0_ffn_in['ln_b'], 'L0_ffn_W1': _L0_ffn_in['W1'], 'L0_ffn_b1': _L0_ffn_in['b1'], 'L0_ffn_W2': _L0_ffn_in['W2'], 'L0_ffn_b2': _L0_ffn_in['b2']}

def reference(x, src, dst, L0_gnn_W, L0_gnn_att_src, L0_gnn_att_dst, L0_gnn_bias, L0_gnn_W_res, L0_gnn_ln1_g, L0_gnn_ln1_b, L0_gnn_ln2_g, L0_gnn_ln2_b, L0_gnn_ffn_w1, L0_gnn_ffn_b1, L0_gnn_ffn_w2, L0_gnn_ffn_b2, L0_mix_t, L0_mix_w_qkv, L0_mix_mem_kv, L0_mix_w_out, L0_mix_b_out, L0_mix_g_out, L0_mix_g_pre, L0_ffn_Wr, L0_ffn_br, L0_ffn_ln_g, L0_ffn_ln_b, L0_ffn_W1, L0_ffn_b1, L0_ffn_W2, L0_ffn_b2):
    import jax
    import jax.numpy as jnp

    def _L0_gnn_ref(x, edge_index, W, att_src, att_dst, bias, W_res, ln1_g, ln1_b, ln2_g, ln2_b, ffn_w1, ffn_b1, ffn_w2, ffn_b2):
        import jax, jax.numpy as jnp
        import numpy as np
        N_NODES = 25000
        N_EDGES = 12500
        D_IN = 256
        D_OUT = 256
        HEADS = 8
        HEAD_DIM = D_OUT // HEADS
        NEG_SLOPE = 0.2
        LN_EPS = 1e-05

        def layer_norm(x, g, b):
            mu = jnp.mean(x, axis=-1, keepdims=True)
            var = jnp.mean((x - mu) ** 2, axis=-1, keepdims=True)
            return (x - mu) * jax.lax.rsqrt(var + LN_EPS) * g + b

        def gelu_tanh(x):
            c = np.sqrt(2.0 / np.pi).astype(np.float32)
            return 0.5 * x * (1.0 + jnp.tanh(c * (x + 0.044715 * x ** 3)))
        N = x.shape[0]
        xn = layer_norm(x, ln1_g, ln1_b)
        loops = jnp.arange(N, dtype=edge_index.dtype)
        src = jnp.concatenate([edge_index[0], loops])
        dst = jnp.concatenate([edge_index[1], loops])
        h = (xn @ W).reshape(N, HEADS, HEAD_DIM)
        a_src = jnp.einsum('nhd,hd->nh', h, att_src)
        a_dst = jnp.einsum('nhd,hd->nh', h, att_dst)
        e = jax.nn.leaky_relu(a_src[src] + a_dst[dst], NEG_SLOPE)
        emax = jax.ops.segment_max(e, dst, num_segments=N)
        ee = jnp.exp(e - emax[dst])
        denom = jax.ops.segment_sum(ee, dst, num_segments=N)
        alpha = ee / denom[dst]
        msg = h[src] * alpha[:, :, None]
        agg = jax.ops.segment_sum(msg, dst, num_segments=N)
        out = agg.reshape(N, HEADS * HEAD_DIM) + xn @ W_res + bias
        out = layer_norm(out, ln2_g, ln2_b)
        ff = gelu_tanh(out @ ffn_w1 + ffn_b1) @ ffn_w2 + ffn_b2
        return out + ff

    def _L0_mix_ref(x, t, w_qkv, mem_kv, w_out, b_out, g_out, g_pre):
        import jax, jax.numpy as jnp
        import numpy as np
        DIM = 256
        HEADS = 4
        DIM_HEAD = 32
        NUM_MEM = 4
        HIDDEN = HEADS * DIM_HEAD
        SCALE = DIM_HEAD ** (-0.5)

        def rmsnorm(x, g):
            n = jnp.linalg.norm(x, axis=-1, keepdims=True)
            return x / jnp.maximum(n, 1e-12) * g * x.shape[-1] ** 0.5
        b, n, c = x.shape
        xn = rmsnorm(x, g_pre)
        qkv = xn @ w_qkv
        q, k, v = jnp.split(qkv, 3, axis=-1)

        def to_heads(z):
            return z.reshape(b, n, HEADS, DIM_HEAD).transpose(0, 2, 3, 1)
        q, k, v = map(to_heads, (q, k, v))
        mk = jnp.broadcast_to(mem_kv[0], (b, HEADS, DIM_HEAD, NUM_MEM))
        mv = jnp.broadcast_to(mem_kv[1], (b, HEADS, DIM_HEAD, NUM_MEM))
        k = jnp.concatenate([mk, k], axis=-1)
        v = jnp.concatenate([mv, v], axis=-1)
        q = jax.nn.softmax(q, axis=-2) * SCALE
        k = jax.nn.softmax(k, axis=-1)
        context = jnp.einsum('bhdn,bhen->bhde', k, v)
        out = jnp.einsum('bhde,bhdn->bhen', context, q)
        out = out.transpose(0, 3, 1, 2).reshape(b, n, HIDDEN)
        out = rmsnorm(out @ w_out + b_out, g_out)
        return out + x

    def _L0_ffn_ref(x, Wr, br, ln_g, ln_b, W1, b1, W2, b2):
        import jax, jax.numpy as jnp
        import numpy as np
        TOP_K = 2
        LN_EPS = 1e-05
        B, S, D = x.shape
        N = B * S
        xt = x.reshape(N, D)
        logits = xt @ Wr + br
        probs = jax.nn.softmax(logits, axis=-1)
        top_p, top_idx = jax.lax.top_k(probs, TOP_K)
        weights = top_p / top_p.sum(axis=-1, keepdims=True)
        mu = xt.mean(axis=-1, keepdims=True)
        var = ((xt - mu) ** 2).mean(axis=-1, keepdims=True)
        xn = (xt - mu) * jax.lax.rsqrt(var + LN_EPS)
        xe = xn[None, :, :] * ln_g[:, None, :] + ln_b[:, None, :]
        h = jax.nn.gelu(jnp.einsum('end,edh->enh', xe, W1) + b1[:, None, :], approximate=False)
        y = jnp.einsum('enh,ehd->end', h, W2) + b2[:, None, :]
        y_tok = jnp.transpose(y, (1, 0, 2))
        sel = jnp.take_along_axis(y_tok, top_idx[:, :, None], axis=1)
        out = (weights[:, :, None] * sel).sum(axis=1)
        return out.reshape(B, S, D)
    edge_index = jnp.stack([src, dst])
    xn = _layernorm(x, axis=-1)
    x = x + _L0_gnn_ref(xn, edge_index, L0_gnn_W, L0_gnn_att_src, L0_gnn_att_dst, L0_gnn_bias, L0_gnn_W_res, L0_gnn_ln1_g, L0_gnn_ln1_b, L0_gnn_ln2_g, L0_gnn_ln2_b, L0_gnn_ffn_w1, L0_gnn_ffn_b1, L0_gnn_ffn_w2, L0_gnn_ffn_b2) + _L0_mix_ref(xn[None], L0_mix_t, L0_mix_w_qkv, L0_mix_mem_kv, L0_mix_w_out, L0_mix_b_out, L0_mix_g_out, L0_mix_g_pre)[0]
    x = x + _L0_ffn_ref(_layernorm(x, axis=-1)[None], L0_ffn_Wr, L0_ffn_br, L0_ffn_ln_g, L0_ffn_ln_b, L0_ffn_W1, L0_ffn_b1, L0_ffn_W2, L0_ffn_b2)[0]
    return x

_drawn_inputs = setup_inputs


def setup_inputs(seed=0):
    import zlib

    import numpy as np

    out = dict(_drawn_inputs(seed))
    spreads = {'L0_gnn_bias': (0.0, 0.1),
     'L0_gnn_ln1_g': (1.0, 0.2),
     'L0_gnn_ln1_b': (0.0, 0.1),
     'L0_gnn_ln2_g': (1.0, 0.2),
     'L0_gnn_ln2_b': (0.0, 0.1),
     'L0_gnn_ffn_b1': (0.0, 0.1),
     'L0_gnn_ffn_b2': (0.0, 0.1),
     'L0_mix_b_out': (0.0, 0.1),
     'L0_mix_g_out': (1.0, 0.2),
     'L0_mix_g_pre': (1.0, 0.6),
     'L0_ffn_br': (0.0, 0.1),
     'L0_ffn_ln_g': (1.0, 0.2),
     'L0_ffn_ln_b': (0.0, 0.39),
     'L0_ffn_b1': (0.0, 0.37),
     'L0_ffn_b2': (0.0, 0.27)}
    factors = {'L0_gnn_att_dst': 3.219, 'L0_mix_w_qkv': 8.0, 'L0_mix_mem_kv': 8.0, 'L0_mix_w_out': 8.0}
    for name, (base, spread) in spreads.items():
        noise = np.random.default_rng([zlib.crc32(name.encode()), seed]).standard_normal(out[name].shape)
        drawn = base * np.exp(spread * noise) if base else spread * noise
        out[name] = jnp.asarray(drawn.astype(out[name].dtype))
    for name, factor in factors.items():
        out[name] = (out[name] * factor).astype(out[name].dtype)
    return out
```

```python
from contextlib import ExitStack

import concourse.bass as bass
from concourse import mybir

P = 128
F32 = mybir.dt.float32
BF16 = mybir.dt.bfloat16
I32 = mybir.dt.int32
ALU = mybir.AluOpType
ACT = mybir.ActivationFunctionType
AX_X = mybir.AxisListType.X
RMAX = bass.bass_isa.ReduceOp.max

N = 3125
E = 50000
D = 256
KT = D // P
TILES = -(-N // P)
NP = TILES * P
FULL = N // P
REST = N - FULL * P
GH, GHD = 8, 32
MH, MHD, MEM = 4, 32, 4
MC = MH * MHD
HID = 1024
HB = HID // P
EXP = 8
TOPK = 2
JG = 4
EG = JG * P
GROUPS = -(-E // EG)
GFULL = E // EG
GREST = E - GFULL * EG
ITEMS = GROUPS + TILES - 1
RING = 3
ROW = D + GH
MOE_TILES = (NP * TOPK - EXP) // P + EXP
NEED = -(-GROUPS // RING) * RING
BLOCK, BLOCK1, GROUP1, SLOT1, SLOT = 0, 5, 10, 17, 19
EPS = 1e-5
SLOPE = 0.2
BIG = 1e30


class Names:
    pass


class Weights:

    def __init__(self, w1h, w1l, w2h, w2l):
        self.w1h, self.w1l, self.w2h, self.w2l = w1h, w1l, w2h, w2l


class Chain:

    def __init__(self, eng, sem, n=0):
        self.eng, self.sem, self.n = eng, sem, n

    def __call__(self, ins):
        self.n = self.n + 1
        ins.then_inc(self.sem, 1)
        self.eng.wait_ge(self.sem, self.n)


def by_pairs(eng, lo, hi, body):
    pairs = (hi - lo) // 2
    if pairs:
        with eng.Fori(0, pairs) as m:
            body(m * 2 + lo, lo % 2)
            body(m * 2 + (lo + 1), (lo + 1) % 2)
    if (hi - lo) % 2:
        body(hi - 1, (hi - 1) % 2)


def by_threes(eng, lo, hi, body):
    assert (hi - lo) % 3 == 0
    with eng.Fori(0, (hi - lo) // 3) as m:
        for s in range(3):
            body(m * 3 + (lo + s), (lo + s) % 3)


def cols(v):
    return v.rearrange("(k p) -> p k", p=P)


def after(eng, sem, n):
    if not (isinstance(n, int) and n <= 0):
        eng.wait_ge(sem, n)


def row_on_all(v):
    return v.rearrange("(a d) -> a d", a=1).to_broadcast([P, v.shape[0]])


def setup_and_nodes(nc, k, a):
    with ExitStack() as own, nc.Block() as block:
        def sb(name, shape, dt=F32):
            return own.enter_context(nc.sbuf_tensor(name, shape, dt))

        def ps(name, shape):
            return own.enter_context(nc.psum_tensor(name, shape, F32))

        def sem(name):
            return own.enter_context(nc.semaphore(name))

        w_hr = sb("w_hr", [P, KT, 2 * D])
        w_qkv = sb("w_qkv", [P, KT, 3 * MC])
        wout = sb("wout", [P, D])
        gbias = sb("gbias", [P, D])
        att = sb("att", [P, 2, D])
        g1c = sb("g1c", [P, 3, KT])
        edge_i = sb("edge_i", [P, 2, EG], I32)
        edge_f = sb("edge_f", [P, 2, EG])
        below = sb("below", [P, TILES])
        edge0 = sb("edge0", [P, GROUPS])
        small = sb("small", [P, P])
        start_g = sb("start_g", [P, 1])
        start_b = sb("start_b", [P, 1])
        cnt_sb = sb("cnt_sb", [P, TILES + 1])
        step_g = sb("step_g", [P, P])
        step_b = sb("step_b", [P, P])
        mask_g = sb("mask_g", [P, 1])
        past0 = sb("past0", [P, 1])
        MOD = -(-P // RING) * RING
        mod3 = sb("mod3", [1, MOD])
        need_f = sb("need_f", [1, NEED])
        weight = sb("weight", [P, 4])
        zero_row = sb("zero_row", [P, D])
        s_zeroed = sem("s_zeroed")
        stats = sb("stats", [P, TILES, 6])
        st_a = sb("st_a", [P, TILES])
        st_b = sb("st_b", [P, TILES])
        st_v = sb("st_v", [P, TILES])
        mean = sb("mean", [P, TILES])
        rstd = sb("rstd", [P, TILES])
        rms = sb("rms", [P, TILES])
        an = sb("an", [P, 2, D])
        bn = sb("bn", [P, 2, D])
        an_t = sb("an_t", [P, 2, KT, P])
        bn_t = sb("bn_t", [P, 2, KT, P])
        prod = sb("prod", [P, 2, D])
        keys = sb("keys", [P, NP])
        vals = sb("vals", [P, TILES, MC + 1])
        gmax = sb("gmax", [P, 2, GH])
        zself = sb("zself", [P, TILES, GH])
        zself2 = sb("zself2", [P, TILES, GH])
        kmax = sb("kmax", [P, 2])
        kexp = sb("kexp", [P, 2, P])
        kexp_t = sb("kexp_t", [P, 2, P])
        head_mask = sb("head_mask", [P, P])
        ctx_n = sb("ctx_n", [P, P])
        ctx_t = sb("ctx_t", [P, P])
        rz = sb("rz", [P, 1])
        qmax = sb("qmax", [P, TILES * MH])
        qsum = sb("qsum", [P, TILES * MH])
        ps_a = [ps(f"ps_a{i}", [P, KT, P]) for i in range(2)]
        ps_b = [ps(f"ps_b{i}", [P, KT, P]) for i in range(2)]
        ps_hr = [ps(f"ps_hr{i}", [P, 2 * D]) for i in range(2)]
        ps_qkv = [ps(f"ps_qkv{i}", [P, 3 * MC]) for i in range(2)]

        s_x, s_w, s_row, s_edge, s_tab = (sem(n) for n in ("s_x", "s_w", "s_row", "s_edge", "s_tab"))
        s_clear, s_iota, s_dstf, s_memkv = (sem(n) for n in ("s_clear", "s_iota", "s_dstf", "s_memkv"))
        s_edge_f, s_edge_t, s_edge_out, s_below, s_cnt, s_steps, s_items = (
            sem(n) for n in ("s_edge_f", "s_edge_t", "s_edge_out", "s_below", "s_cnt", "s_steps", "s_items"))
        s_dve, s_scale, s_an, s_bn, s_ta, s_tb, s_at, s_bt, s_hr, s_qkv, s_hr_out, s_qkv_out = (
            sem(n) for n in ("s_dve", "s_scale", "s_an", "s_bn", "s_ta", "s_tb", "s_at", "s_bt", "s_hr", "s_qkv",
                             "s_hr_out", "s_qkv_out"))
        s_nodes, s_gmax, s_gall, s_zself, s_wself, s_kmax, s_kexp, s_kt, s_kt_out, s_ctx = (
            sem(n) for n in ("s_nodes", "s_gmax", "s_gall", "s_zself", "s_wself", "s_kmax", "s_kexp", "s_kt",
                             "s_kt_out", "s_ctx"))
        s_var, s_root = sem("s_var"), sem("s_root")
        s_ctx_n, s_ctx_t, s_ctx_to, s_cw, s_q0, s_q1, s_act = (
            sem(n) for n in ("s_ctx_n", "s_ctx_t", "s_ctx_to", "s_cw", "s_q0", "s_q1", "s_act"))

        @block.sync
        def _(sp):
            sp.wait_ge(s_clear, 2)
            for n, v in enumerate((a.src, a.dst)):
                sp.dma_start(edge_i[0:GFULL, n, :], v[0:GFULL * EG].rearrange("(g e) -> g e", e=EG)).then_inc(s_edge, 16)
                sp.dma_start(edge_i[GFULL:GROUPS, n, 0:GREST],
                             v[GFULL * EG:E].rearrange("(g e) -> g e", g=1)).then_inc(s_edge, 16)
            sp.wait_ge(s_clear, 3)
            sp.dma_start(k.acc[:, 0:FULL, :], a.x[0:FULL * P, :].rearrange("(t p) d -> p t d", p=P)).then_inc(s_x, 16)
            sp.dma_start(k.acc[0:REST, FULL, :], a.x[FULL * P:N, :]).then_inc(s_x, 16)
            sp.dma_start(w_hr[:, :, 0:D], a.g_W.rearrange("(k p) n -> p k n", p=P)).then_inc(s_w, 16)
            sp.dma_start(w_hr[:, :, D:2 * D], a.g_Wres.rearrange("(k p) n -> p k n", p=P)).then_inc(s_w, 16)
            sp.dma_start(w_qkv[:], a.m_qkv.rearrange("(k p) n -> p k n", p=P)).then_inc(s_w, 16)
            sp.dma_start(wout[:], a.m_wout).then_inc(s_w, 16)
            for n, v in enumerate((a.ln1_g, a.ln1_b, a.m_gpre)):
                sp.dma_start(g1c[:, n, :], cols(v)).then_inc(s_row, 16)
            sp.dma_start(gbias[:], row_on_all(a.g_bias)).then_inc(s_row, 16)
            for n, v in enumerate((a.g_as, a.g_ad)):
                sp.dma_start(att[:, n, :], row_on_all(v.rearrange("h d -> (h d)"))).then_inc(s_row, 16)
            for to, v in ((k.bout, a.m_bout), (k.gout, a.m_gout), (k.g2, a.ln2_g), (k.b2n, a.ln2_b), (k.fb2, a.f_b2)):
                sp.dma_start(to[:], row_on_all(v)).then_inc(s_row, 16)
            sp.wait_ge(s_iota, 9)
            sp.dma_start(k.rows_in.rearrange("(t p) d -> p t d", p=P),
                         zero_row[:].unsqueeze(1).to_broadcast([P, MOE_TILES, D])).then_inc(s_zeroed, 16)
            sp.wait_ge(s_edge_f, 1)
            sp.dma_start(k.dst_f, edge_f[0:GROUPS, 1, :]).then_inc(s_dstf, 16)
            sp.wait_ge(s_qkv_out, TILES)
            sp.dma_start(keys[:, N:N + MEM], a.m_mem[0].rearrange("h d m -> (h d) m")).then_inc(s_memkv, 16)
            sp.dma_start(vals[REST:REST + MEM, FULL, 0:MC], a.m_mem[1].rearrange("h d m -> m (h d)")).then_inc(s_memkv, 16)
            sp.wait_ge(s_nodes, 1)
            sp.dma_start(k.table.rearrange("(t p) r -> p t r", p=P), k.agg[:]).then_inc(s_tab, 16)
            sp.wait_ge(s_tab, 16)
            sp.wait_ge(s_dstf, 16)
            sp.wait_ge(s_zeroed, 16)

        @block.gpsimd
        def _(pool):
            nc.gpsimd.memset(edge_i[:, 0, :], 0).then_inc(s_clear, 1)
            nc.gpsimd.memset(edge_i[:, 1, :], NP + P).then_inc(s_clear, 1)
            nc.gpsimd.memset(k.acc[:, FULL, :], 0.0).then_inc(s_clear, 1)
            nc.gpsimd.iota(k.pidx[:], pattern=[[0, 1]], base=0, channel_multiplier=1,
                           allow_small_or_imprecise_dtypes=True).then_inc(s_iota, 1)
            nc.gpsimd.iota(k.iota_n[:], pattern=[[1, NP]], base=0, channel_multiplier=0,
                           allow_small_or_imprecise_dtypes=True).then_inc(s_iota, 1)
            nc.gpsimd.iota(k.node_id[:], pattern=[[P, TILES]], base=0, channel_multiplier=1,
                           allow_small_or_imprecise_dtypes=True).then_inc(s_iota, 1)
            nc.gpsimd.iota(edge0[:], pattern=[[EG, GROUPS]], base=0, channel_multiplier=0,
                           allow_small_or_imprecise_dtypes=True).then_inc(s_iota, 1)
            nc.gpsimd.iota(mask_g[:], pattern=[[0, 1]], base=0, channel_multiplier=EG,
                           allow_small_or_imprecise_dtypes=True).then_inc(s_iota, 1)
            nc.gpsimd.memset(vals[:, :, MC:MC + 1], 1.0).then_inc(s_iota, 1)
            nc.gpsimd.memset(need_f[:], 0.0).then_inc(s_iota, 1)
            nc.gpsimd.memset(zero_row[:], 0.0).then_inc(s_iota, 1)
            nc.gpsimd.iota(mod3[:].rearrange("p (a b) -> p a b", b=RING), pattern=[[0, MOD // RING], [1, RING]], base=0,
                           channel_multiplier=0, allow_small_or_imprecise_dtypes=True).then_inc(s_iota, 1)
            pool.wait_ge(s_gmax, 1)
            nc.gpsimd.partition_all_reduce(gmax[:, 1, :], gmax[:, 0, :], P, RMAX).then_inc(s_gall, 1)

        def layer_stats(dve, link, src, n):
            def one(t, _):
                nc.vector.bn_stats(stats[:, t, :], src[:, t, :])
            by_pairs(dve, 0, TILES - 1, one)
            link(nc.vector.bn_stats(stats[:, TILES - 1, :], src[:, TILES - 1, :]))
            link(nc.vector.tensor_tensor(st_a[:], stats[:, :, 1], stats[:, :, 4], ALU.subtract))
            link(nc.vector.tensor_tensor(st_a[:], st_a[:], st_a[:], ALU.mult))
            link(nc.vector.tensor_tensor(st_b[:], stats[:, :, 2], stats[:, :, 5], ALU.add))
            link(nc.vector.scalar_tensor_tensor(out=st_v[:], in0=st_a[:], scalar=D / 4.0, in1=st_b[:], op0=ALU.mult,
                                                op1=ALU.add))
            link(nc.vector.tensor_tensor(mean[:], stats[:, :, 1], stats[:, :, 4], ALU.add))
            link(nc.vector.tensor_scalar(mean[:], mean[:], 0.5, None, ALU.mult))
            nc.vector.tensor_scalar(rstd[:], st_v[:], 1.0 / D, EPS, ALU.mult, ALU.add).then_inc(s_var, 1)
            dve.wait_ge(s_root, n)
            link(nc.vector.reciprocal(st_a[:], rstd[:]))
            link(nc.vector.tensor_scalar(st_b[:], st_v[:], 1.0 / D, EPS, ALU.mult, ALU.add))
            link(nc.vector.tensor_tensor(st_b[:], st_b[:], st_a[:], ALU.mult))
            link(nc.vector.tensor_tensor(st_b[:], st_b[:], rstd[:], ALU.add))
            link(nc.vector.reciprocal(rstd[:], st_b[:]))
            link(nc.vector.tensor_scalar(rstd[:], rstd[:], 2.0, None, ALU.mult))

        @block.vector
        def _(dve):
            link = Chain(dve, s_dve)
            link(nc.vector.memset(k.ones[:], 1.0))
            link(nc.vector.memset(head_mask[:], 0.0))
            for h in range(MH):
                link(nc.vector.memset(head_mask[MHD * h:MHD * h + MHD, MHD * h:MHD * h + MHD], float(MHD) ** -0.5))
            dve.wait_ge(s_iota, 9)
            link(nc.vector.tensor_scalar(k.ident[:], k.iota_n[:, 0:P], k.pidx[:, 0:1], None, ALU.is_equal))
            dve.wait_ge(s_edge, 64)
            nc.vector.tensor_copy(edge_f[:], edge_i[:]).then_inc(s_edge_f, 1)
            dve.wait_ge(s_edge_f, 1)
            for b in range(TILES):
                link(nc.vector.tensor_scalar(an[0:GROUPS, :, :].rearrange("p a b -> p (a b)"), edge_f[0:GROUPS, 1, :],
                                             float(P * b), 0.0, ALU.is_lt, ALU.add,
                                             accum_out=below[0:GROUPS, b:b + 1]))
            nc.vector.tensor_copy(small[0:1, 0:1], below[0:1, 0:1]).then_inc(s_below, 1)
            dve.wait_ge(s_edge_t, 1)
            nc.vector.tensor_copy(k.src_i[:], ps_hr[0][:, 0:JG * GROUPS].rearrange("p (j g) -> p j g", j=JG)).then_inc(s_edge_out, 1)
            nc.vector.tensor_copy(k.dst_e[:], ps_hr[1][:, 0:JG * GROUPS].rearrange("p (j g) -> p j g", j=JG)).then_inc(s_edge_out, 1)
            dve.wait_ge(s_cnt, 1)
            link(nc.vector.tensor_copy(cnt_sb[:, 0:TILES], ps_a[0][:, 0, 0:TILES]))
            link(nc.vector.tensor_copy(cnt_sb[0:TILES, TILES:TILES + 1], ps_a[0][0:TILES, 1, 0:1]))
            link(nc.vector.tensor_scalar(small[:, 0:TILES - 1], cnt_sb[:, 1:TILES], mask_g[:, 0:1], 0.0, ALU.is_le,
                                         ALU.add, accum_out=start_g[:]))
            link(nc.vector.tensor_tensor(start_g[:], start_g[:], k.pidx[:], ALU.add))
            link(nc.vector.tensor_scalar(small[0:TILES, 0:GROUPS - 1], edge0[0:TILES, 1:GROUPS],
                                         cnt_sb[0:TILES, TILES:TILES + 1], 0.0, ALU.is_lt, ALU.add,
                                         accum_out=start_b[0:TILES, :]))
            link(nc.vector.tensor_tensor(start_b[0:TILES, :], start_b[0:TILES, :], k.pidx[0:TILES, :], ALU.add))
            link(nc.vector.tensor_scalar(step_g[:], k.iota_n[:, 0:P], start_g[:, 0:1], None, ALU.is_ge))
            link(nc.vector.tensor_scalar(step_b[0:TILES, :], k.iota_n[0:TILES, 0:P], start_b[0:TILES, 0:1], None, ALU.is_ge))
            link(nc.vector.tensor_scalar(past0[:], k.pidx[:], 1.0, None, ALU.is_ge))
            link(nc.vector.tensor_scalar(weight[:, 0:1], ps_a[0][:, 1, 1:2], 0.0, None, ALU.is_equal))
            link(nc.vector.tensor_scalar(weight[:, 0:1], weight[:, 0:1], -float(RING), 1.0, ALU.mult, ALU.add))
            link(nc.vector.tensor_tensor(weight[:, 0:1], weight[:, 0:1], past0[:], ALU.mult))
            link(nc.vector.tensor_scalar(weight[:, 1:2], weight[:, 0:1], float(1 << SLOT1), None, ALU.mult))
            link(nc.vector.scalar_tensor_tensor(out=weight[:, 1:2], in0=past0[:], scalar=float(1 << GROUP1),
                                                in1=weight[:, 1:2], op0=ALU.mult, op1=ALU.add))
            link(nc.vector.tensor_scalar(weight[:, 0:1], weight[:, 0:1], float(1 << SLOT), None, ALU.mult))
            link(nc.vector.tensor_scalar(weight[:, 2:3], past0[:], float(1 << BLOCK1), None, ALU.mult))
            nc.vector.tensor_copy(weight[:, 3:4], past0[:]).then_inc(s_steps, 1)
            dve.wait_ge(s_items, 1)
            link(nc.vector.tensor_copy(k.items[:], ps_a[1][0:1, 0, 0:ITEMS]))
            link(nc.vector.tensor_copy(need_f[0:1, RING:GROUPS], ps_b[1][0:1, 0, 0:GROUPS - RING]))
            nf = need_f[0:1, :].rearrange("p (m s) -> p m s", s=RING)
            link(nc.vector.scalar_tensor_tensor(out=nf[:, :, 1], in0=nf[:, :, 2], scalar=float(1 << 7), in1=nf[:, :, 1],
                                                op0=ALU.mult, op1=ALU.add))
            link(nc.vector.scalar_tensor_tensor(out=nf[:, :, 0], in0=nf[:, :, 1], scalar=float(1 << 7), in1=nf[:, :, 0],
                                                op0=ALU.mult, op1=ALU.add))
            link(nc.vector.tensor_copy(k.need[:], nf[:, :, 0]))

            dve.wait_ge(s_x, 32)
            layer_stats(dve, link, k.acc, 1)

            def norm0(t, _):
                nc.vector.tensor_scalar(k.xn0[:, t, :], k.acc[:, t, :], mean[:, bass.ds(t, 1)], rstd[:, bass.ds(t, 1)],
                                        ALU.subtract, ALU.mult)
            by_pairs(dve, 0, TILES - 1, norm0)
            link(nc.vector.tensor_scalar(k.xn0[:, TILES - 1, :], k.acc[:, TILES - 1, :], mean[:, TILES - 1:TILES],
                                         rstd[:, TILES - 1:TILES], ALU.subtract, ALU.mult))
            layer_stats(dve, link, k.xn0, 2)
            link(nc.vector.tensor_tensor(st_b[:], mean[:], mean[:], ALU.mult))
            nc.vector.scalar_tensor_tensor(out=rms[:], in0=st_b[:], scalar=float(D), in1=st_v[:], op0=ALU.mult,
                                           op1=ALU.add).then_inc(s_var, 1)
            dve.wait_ge(s_root, 3)
            link(nc.vector.tensor_scalar(rms[:], rms[:], 1e-12, None, ALU.max))
            link(nc.vector.reciprocal(rms[:], rms[:]))
            nc.vector.tensor_scalar(rms[:], rms[:], float(D) ** 0.5, None, ALU.mult).then_inc(s_scale, 1)
            dve.wait_ge(s_row, 16 * 11)

            def an_of(i, par):
                after(dve, s_ta, i - 1)
                nc.vector.tensor_scalar(an[:, par, :], k.xn0[:, i, :], mean[:, bass.ds(i, 1)], rstd[:, bass.ds(i, 1)],
                                        ALU.subtract, ALU.mult).then_inc(s_an, 1)

            def node(i, par, ahead=True):
                dve.wait_ge(s_ta, i + 1)
                after(dve, s_hr, i - 1)
                for kt in range(KT):
                    m = nc.vector.tensor_scalar(an_t[:, par, kt, :], ps_a[par][:, kt, :], g1c[:, 0, kt:kt + 1],
                                                g1c[:, 1, kt:kt + 1], ALU.mult, ALU.add)
                m.then_inc(s_at, 1)
                if ahead:
                    an_of(i + 2, par)
                dve.wait_ge(s_hr, i + 1)
                nc.vector.tensor_tensor(k.res[:, i, :], ps_hr[par][:, D:2 * D], gbias[:], ALU.add)
                link(nc.vector.tensor_copy(k.agg[:, i, 0:D], ps_hr[par][:, 0:D]))
                nc.vector.tensor_copy(small[:, 0:1], small[:, 1:2]).then_inc(s_hr_out, 1)
                nc.vector.tensor_tensor(prod[:, 0, :], k.agg[:, i, 0:D], att[:, 0, :], ALU.mult)
                link(nc.vector.tensor_tensor(prod[:, 1, :], k.agg[:, i, 0:D], att[:, 1, :], ALU.mult))
                nc.vector.tensor_reduce(k.agg[:, i, D:ROW], prod[:, 0, :].rearrange("p (h d) -> p h d", h=GH), AX_X, ALU.add)
                link(nc.vector.tensor_reduce(k.node_am[:, i, 0:GH], prod[:, 1, :].rearrange("p (h d) -> p h d", h=GH),
                                             AX_X, ALU.add))

            an_of(0, 0)
            an_of(1, 1)
            node(0, 0)
            node(1, 1)
            base, per = link.n, 3

            def counted(i, par):
                link.n = (i - 2) * per + base
                node(i, par)
            by_pairs(dve, 2, TILES - 2, counted)
            link.n = base + per * (TILES - 4)
            node(TILES - 2, (TILES - 2) % 2, False)
            node(TILES - 1, (TILES - 1) % 2, False)
            nc.vector.tensor_copy(small[:, 0:1], small[:, 1:2]).then_inc(s_nodes, 1)
            nc.vector.tensor_reduce(gmax[:, 0, :], k.agg[:, :, D:ROW].rearrange("p t h -> p h t"), AX_X,
                                    ALU.max).then_inc(s_gmax, 1)
            dve.wait_ge(s_gall, 1)
            link(nc.vector.tensor_tensor(zself[:], k.node_am[:, :, 0:GH],
                                         gmax[:, 1:2, :].to_broadcast([P, TILES, GH]), ALU.add))
            link(nc.vector.scalar_tensor_tensor(out=k.node_am[:, :, GH:2 * GH], in0=zself[:], scalar=SLOPE,
                                                in1=zself[:], op0=ALU.mult, op1=ALU.max))
            link(nc.vector.tensor_tensor(zself2[:], k.node_am[:, :, 0:GH], k.agg[:, :, D:ROW], ALU.add))
            link(nc.vector.scalar_tensor_tensor(out=zself[:], in0=zself2[:], scalar=SLOPE, in1=zself2[:],
                                                op0=ALU.mult, op1=ALU.max))
            nc.vector.tensor_tensor(zself[:], zself[:], k.node_am[:, :, GH:2 * GH], ALU.subtract).then_inc(s_zself, 1)
            dve.wait_ge(s_memkv, 32)
            link(nc.vector.tensor_reduce(kmax[:, 0:1], keys[:, 0:N + MEM], AX_X, ALU.max))
            nc.vector.tensor_scalar(kmax[:, 1:2], kmax[:, 0:1], -1.0, None, ALU.mult).then_inc(s_kmax, 1)
            qv = k.q[:].rearrange("p t (h d) -> p (t h) d", h=MH)
            link(nc.vector.tensor_reduce(qmax[:], qv, AX_X, ALU.max))
            nc.vector.tensor_tensor(qv, qv, qmax[:].unsqueeze(2).to_broadcast([P, TILES * MH, MHD]),
                                    ALU.subtract).then_inc(s_q0, 1)

            def key_tile(i, par):
                dve.wait_ge(s_kt, i + 1)
                after(dve, s_ctx, i - 1)
                nc.vector.tensor_copy(kexp_t[:, par, :], ps_a[par][:, 0, :]).then_inc(s_kt_out, 1)
            key_tile(0, 0)
            key_tile(1, 1)
            by_pairs(dve, 2, TILES, key_tile)
            dve.wait_ge(s_tab, 16)
            dve.wait_ge(s_wself, 1)
            for t0, t1 in ((0, 13), (13, TILES)):
                hv = k.agg[:, t0:t1, 0:D].rearrange("p t (h d) -> p t h d", h=GH)
                link(nc.vector.tensor_tensor(hv, hv, zself2[:, t0:t1, :].unsqueeze(3).to_broadcast([P, t1 - t0, GH, GHD]),
                                             ALU.mult))
            link(nc.vector.tensor_copy(k.agg[:, :, D:ROW], zself2[:]))
            dve.wait_ge(s_ctx, TILES)
            link(nc.vector.reciprocal(rz[:], ps_hr[0][:, MC:MC + 1]))
            nc.vector.scalar_tensor_tensor(out=ctx_n[:], in0=ps_hr[0][:, 0:MC], scalar=rz[:, 0:1], in1=head_mask[:],
                                           op0=ALU.mult, op1=ALU.mult).then_inc(s_ctx_n, 1)
            dve.wait_ge(s_ctx_t, 1)
            nc.vector.tensor_copy(ctx_t[:], ps_a[0][:, 0, :]).then_inc(s_ctx_to, 1)
            dve.wait_ge(s_cw, 1)
            link(nc.vector.tensor_copy(k.cw[:], ps_hr[1][:, 0:D]))
            dve.wait_ge(s_q1, 1)
            link(nc.vector.tensor_reduce(qsum[:], qv, AX_X, ALU.add))
            link(nc.vector.reciprocal(qsum[:], qsum[:]))
            link(nc.vector.tensor_tensor(qv, qv, qsum[:].unsqueeze(2).to_broadcast([P, TILES * MH, MHD]), ALU.mult))

        @block.scalar
        def _(act):
            for n, v in enumerate((rstd, rstd, rms)):
                act.wait_ge(s_var, n + 1)
                nc.scalar.activation(v[:], v[:], ACT.Sqrt).then_inc(s_root, 1)
            act.wait_ge(s_scale, 1)
            act.wait_ge(s_row, 16 * 11)

            def bn_of(i, par):
                after(act, s_tb, i - 1)
                nc.scalar.activation(bn[:, par, :], k.xn0[:, i, :], ACT.Copy, scale=rms[:, bass.ds(i, 1)]).then_inc(s_bn, 1)

            def node(i, par, ahead=True):
                act.wait_ge(s_tb, i + 1)
                after(act, s_qkv, i - 1)
                for kt in range(KT):
                    m = nc.scalar.activation(bn_t[:, par, kt, :], ps_b[par][:, kt, :], ACT.Copy, scale=g1c[:, 2, kt:kt + 1])
                m.then_inc(s_bt, 1)
                if ahead:
                    bn_of(i + 2, par)
                act.wait_ge(s_qkv, i + 1)
                nc.scalar.copy(k.q[:, i, :], ps_qkv[par][:, 0:MC])
                nc.scalar.copy(vals[:, i, 0:MC], ps_qkv[par][:, MC:2 * MC])
                nc.scalar.copy(keys[:, bass.ds(i * P, P)], ps_qkv[par][:, 2 * MC:3 * MC]).then_inc(s_qkv_out, 1)

            bn_of(0, 0)
            bn_of(1, 1)
            node(0, 0)
            node(1, 1)
            by_pairs(act, 2, TILES - 2, node)
            node(TILES - 2, (TILES - 2) % 2, False)
            node(TILES - 1, (TILES - 1) % 2, False)
            act.wait_ge(s_zself, 1)
            nc.scalar.activation(zself2[:], zself[:], ACT.Exp).then_inc(s_wself, 1)
            act.wait_ge(s_kmax, 1)

            def key_exp(i, par):
                after(act, s_kt, i - 1)
                nc.scalar.activation(kexp[:, par, :], keys[:, bass.ds(i * P, P)], ACT.Exp, bias=kmax[:, 1:2]).then_inc(s_kexp, 1)
            key_exp(0, 0)
            key_exp(1, 1)
            by_pairs(act, 2, TILES - 1, key_exp)
            par = (TILES - 1) % 2
            act.wait_ge(s_kt, TILES - 2)
            nc.scalar.activation(kexp[:, par, 0:REST + MEM], keys[:, N - REST:N + MEM], ACT.Exp, bias=kmax[:, 1:2])
            nc.scalar.activation(kexp[:, par, REST + MEM:P], k.ones[:, REST + MEM:P], ACT.Copy, scale=0.0).then_inc(s_kexp, 1)
            act.wait_ge(s_q0, 1)
            qf = k.q[:].rearrange("p t c -> p (t c)")
            nc.scalar.activation(qf, qf, ACT.Exp).then_inc(s_q1, 1)

        @block.tensor
        def _(pe):
            pe.wait_ge(s_edge_f, 1)
            pe.wait_ge(s_below, 1)
            for n in range(2):
                for j in range(JG):
                    m = nc.tensor.transpose(ps_hr[n][:, j * GROUPS:(j + 1) * GROUPS],
                                            edge_f[0:GROUPS, n, j * P:(j + 1) * P], k.ident[0:GROUPS, 0:GROUPS])
            m.then_inc(s_edge_t, 1)
            nc.tensor.matmul(ps_a[0][:, 0, 0:TILES], k.ones[0:GROUPS, :], below[0:GROUPS, :], start=True, stop=True)
            nc.tensor.matmul(ps_a[0][:, 1, 1:2], mod3[0:1, 0:P], k.ones[0:1, 0:1], start=True, stop=True)
            nc.tensor.matmul(ps_a[0][0:TILES, 1, 0:1], below[0:GROUPS, :], k.ones[0:GROUPS, 0:1], start=True,
                             stop=True).then_inc(s_cnt, 1)
            pe.wait_ge(s_steps, 1)
            word = ps_a[1][0:1, 0, :]
            nc.tensor.matmul(word[:, 0:ITEMS], weight[0:GROUPS, 0:1], step_g[0:GROUPS, 0:ITEMS], start=True, stop=False)
            nc.tensor.matmul(word[:, 0:ITEMS], weight[0:GROUPS, 1:2], step_g[0:GROUPS, 1:ITEMS + 1], start=False, stop=False)
            nc.tensor.matmul(word[:, 0:ITEMS], weight[0:TILES, 2:3], step_b[0:TILES, 1:ITEMS + 1], start=False, stop=False)
            nc.tensor.matmul(word[:, 1:ITEMS], weight[0:TILES, 3:4], step_b[0:TILES, 0:ITEMS - 1], start=False, stop=True)
            nc.tensor.matmul(ps_b[1][0:1, 0, 0:GROUPS - RING], start_g[:, 0:1], k.ident[:, 1:1 + GROUPS - RING],
                             start=True, stop=True).then_inc(s_items, 1)
            pe.wait_ge(s_edge_out, 2)
            pe.wait_ge(s_scale, 1)
            pe.wait_ge(s_w, 64)

            def turn(i, par):
                pe.wait_ge(s_an, i + 1)
                after(pe, s_at, i - 1)
                for kt in range(KT):
                    m = nc.tensor.transpose(ps_a[par][:, kt, :], an[:, par, kt * P:(kt + 1) * P], k.ident[:])
                m.then_inc(s_ta, 1)
                pe.wait_ge(s_bn, i + 1)
                after(pe, s_bt, i - 1)
                for kt in range(KT):
                    m = nc.tensor.transpose(ps_b[par][:, kt, :], bn[:, par, kt * P:(kt + 1) * P], k.ident[:])
                m.then_inc(s_tb, 1)

            def products(i, par):
                pe.wait_ge(s_at, i + 1)
                after(pe, s_hr_out, i - 1)
                for kt in range(KT):
                    m = nc.tensor.matmul(ps_hr[par][:], an_t[:, par, kt, :], w_hr[:, kt, :], start=(kt == 0),
                                         stop=(kt == KT - 1))
                m.then_inc(s_hr, 1)
                pe.wait_ge(s_bt, i + 1)
                after(pe, s_qkv_out, i - 1)
                for kt in range(KT):
                    nc.tensor.matmul(ps_qkv[par][:, 0:MC], bn_t[:, par, kt, :], w_qkv[:, kt, 0:MC], start=(kt == 0),
                                     stop=(kt == KT - 1))
                for kt in range(KT):
                    nc.tensor.matmul(ps_qkv[par][:, MC:2 * MC], bn_t[:, par, kt, :], w_qkv[:, kt, 2 * MC:3 * MC],
                                     start=(kt == 0), stop=(kt == KT - 1))
                for kt in range(KT):
                    m = nc.tensor.matmul(ps_qkv[par][:, 2 * MC:3 * MC], w_qkv[:, kt, MC:2 * MC], bn_t[:, par, kt, :],
                                         start=(kt == 0), stop=(kt == KT - 1))
                m.then_inc(s_qkv, 1)

            def node(i, par):
                turn(i + 1, 1 - par)
                products(i, par)

            turn(0, 0)
            node(0, 0)
            node(1, 1)
            by_pairs(pe, 2, TILES - 1, node)
            products(TILES - 1, (TILES - 1) % 2)
            pe.wait_ge(s_hr_out, TILES)
            pe.wait_ge(s_at, TILES)
            pe.wait_ge(s_memkv, 32)

            def key_turn(i, par):
                pe.wait_ge(s_kexp, i + 1)
                after(pe, s_kt_out, i - 1)
                nc.tensor.transpose(ps_a[par][:, 0, :], kexp[:, par, :], k.ident[:]).then_inc(s_kt, 1)

            def context(i, par, first=False, last=False):
                pe.wait_ge(s_kt_out, i + 1)
                nc.tensor.matmul(ps_hr[0][:, 0:MC + 1], kexp_t[:, par, :], vals[:, i, :], start=first,
                                 stop=last).then_inc(s_ctx, 1)
            key_turn(0, 0)
            key_turn(1, 1)
            context(0, 0, first=True)

            def both(i, par):
                key_turn(i + 1, 1 - par)
                context(i, par)
            by_pairs(pe, 1, TILES - 1, both)
            context(TILES - 1, (TILES - 1) % 2, last=True)
            pe.wait_ge(s_ctx_n, 1)
            nc.tensor.transpose(ps_a[0][:, 0, :], ctx_n[:], k.ident[:]).then_inc(s_ctx_t, 1)
            pe.wait_ge(s_ctx_to, 1)
            nc.tensor.matmul(ps_hr[1][:, 0:D], ctx_t[:], wout[:], start=True, stop=True).then_inc(s_cw, 1)


def graph_items(nc, k, a):
    with ExitStack() as own, nc.Block() as block:
        def sb(name, shape, dt=F32):
            return own.enter_context(nc.sbuf_tensor(name, shape, dt))

        def sem(name):
            return own.enter_context(nc.semaphore(name))

        rows = sb("rows", [P, RING, JG, ROW])
        index = sb("index", [P, RING, JG], I32)
        dst_all = sb("dst_all", [P, RING, EG])
        sel = sb("sel", [P, RING, JG, P])
        sel_t = sb("sel_t", [P, RING, EG])
        wx = sb("wx", [P, RING, JG, ROW])
        z = sb("z", [P, RING, 4, JG, GH])
        ps_am = [own.enter_context(nc.psum_tensor(f"ps_am{i}", [P, JG, 2 * GH], F32)) for i in range(RING)]
        ps_sum = [own.enter_context(nc.psum_tensor(f"ps_sum{i}", [P, ROW], F32)) for i in range(RING)]

        s_row = [sem(f"s_row{i}") for i in range(RING)]
        s_dst = [sem(f"s_dst{i}") for i in range(RING)]
        s_turn = {"pool": sem("s_turn_pool"), "sp": sem("s_turn_sp"), "index": sem("s_turn_index")}
        s_index, s_rows_in, s_dst_in = sem("s_index"), sem("s_rows_in"), sem("s_dst_in")
        s_sel, s_am, s_link, s_z, s_w, s_wx, s_sum, s_add = (
            sem(n) for n in ("s_sel", "s_am", "s_link", "s_z", "s_w", "s_wx", "s_sum", "s_add"))

        def groups(eng, name, sems, per, out, issue):
            def passed_on(slot, turn):
                eng.wait_ge(sems[slot], (turn + 1) * per)
                eng.sem_inc(out, 1)

            def turn(m, slots):
                word = eng.value_load(k.need[0:1, bass.ds(m, 1)], min_val=0, max_val=(1 << 21) - 1)
                for slot in range(slots):
                    eng.wait_ge(s_wx, (word >> (7 * slot)) & 127)
                    eng.sem_inc(s_turn[name], 1)
                    issue(m * RING + slot, slot)
                    passed_on((slot - 1) % RING, m - (slot == 0))
            for slot in range(RING):
                issue(slot, slot)
                if slot:
                    passed_on(slot - 1, 0)
            with eng.Fori(0, GROUPS // RING - 1) as m:
                turn(m + 1, RING)
            turn(GROUPS // RING, GROUPS % RING)
            passed_on((GROUPS - 1) % RING, (GROUPS - 1) // RING)

        @block.gpsimd
        def _(pool):
            def gather(g, slot):
                nc.gpsimd.tensor_copy(index[:, slot, :], k.src_i[:, :, g]).then_inc(s_index, 1)
                pool.wait_ge(s_index, g + 1)
                pool.sem_inc(s_turn["index"], 1)
                for j in range(JG):
                    nc.gpsimd.indirect_dma_start(rows[:, slot, j, :], None, k.table, bass.IndirectOffsetOnAxis(
                        ap=index[:, slot, j:j + 1], axis=0)).then_inc(s_row[slot], 16)
            groups(pool, "pool", s_row, 16 * JG, s_rows_in, gather)

        @block.sync
        def _(sp):
            def spread(g, slot):
                sp.dma_start(dst_all[:, slot, :], k.dst_f[bass.ds(g, 1), :].to_broadcast([P, EG])).then_inc(s_dst[slot], 16)
            groups(sp, "sp", s_dst, 16, s_dst_in, spread)

        def item(eng, i):
            return eng.value_load(k.items[0:1, bass.ds(i, 1)], min_val=0, max_val=(1 << 21) - 1)

        def part(eng, word, at, top):
            field = eng.snap((word >> at) & ((1 << top.bit_length()) - 1))
            return nc.s_assert_within(field, min_val=0, max_val=top,
                                      skip_runtime_bounds_check_because="the word is built from fields in range")

        @block.vector
        def _(dve):
            def select(i, s, g, slot, b):
                after(dve, s_sum, i - 2)
                for j in range(JG):
                    nc.vector.tensor_scalar(sel[:, s, j, :], k.iota_n[:, bass.ds(b * P, P)], k.dst_e[:, j, bass.ds(g, 1)],
                                            None, ALU.is_equal)
                dve.wait_ge(s_rows_in, g + 1)
                dve.wait_ge(s_dst_in, g + 1)
                after(dve, s_am, i - 2)
                nc.vector.tensor_scalar(sel_t[:, s, :], dst_all[:, slot, :], k.node_id[:, bass.ds(b, 1)], None,
                                        ALU.is_equal).then_inc(s_sel, 1)

            def logits(i, s, slot, link):
                dve.wait_ge(s_am, i + 1)
                zz = z[:, s]
                link(nc.vector.tensor_tensor(zz[:, 0], rows[:, slot, :, D:ROW], ps_am[s][:, :, 0:GH], ALU.add))
                link(nc.vector.scalar_tensor_tensor(out=zz[:, 1], in0=zz[:, 0], scalar=SLOPE, in1=zz[:, 0], op0=ALU.mult,
                                                    op1=ALU.max))
                link(nc.vector.tensor_tensor(zz[:, 2], zz[:, 1], ps_am[s][:, :, GH:2 * GH], ALU.subtract))
                after(dve, s_w, i - 2)
                nc.vector.tensor_scalar(zz[:, 3], zz[:, 2], 0.0, None, ALU.min).then_inc(s_z, 1)

            def weigh(i, s, slot):
                dve.wait_ge(s_w, i + 1)
                nc.vector.tensor_tensor(
                    wx[:, s, :, 0:D].rearrange("p j (h d) -> p j h d", h=GH),
                    rows[:, slot, :, 0:D].rearrange("p j (h d) -> p j h d", h=GH),
                    wx[:, s, :, D:ROW].unsqueeze(3).to_broadcast([P, JG, GH, GHD]), ALU.mult).then_inc(s_wx, 1)

            def add(i, s, b):
                dve.wait_ge(s_sum, i + 1)
                after(dve, s_add, i)
                nc.vector.tensor_tensor(k.agg[:, b, :], k.agg[:, b, :], ps_sum[s][:], ALU.add).then_inc(s_add, 1)

            def step(i, s, first=False, last=False):
                word = item(dve, i)
                slot = part(dve, word, SLOT, RING - 1)
                logits(i, s, slot, Chain(dve, s_link, i * 3))
                if not last:
                    select(i + 1, (s + 1) % RING, part(dve, word, GROUP1, GROUPS - 1),
                           part(dve, word, SLOT1, RING - 1), part(dve, word, BLOCK1, TILES - 1))
                weigh(i, s, slot)
                if not first:
                    add(i - 1, (s - 1) % RING, part(dve, word, BLOCK, TILES - 1))
            select(0, 0, 0, 0, 0)
            step(0, 0, first=True)
            for i in range(1, RING + 1):
                step(i, i % RING)
            by_threes(dve, RING + 1, ITEMS - 1, step)
            step(ITEMS - 1, (ITEMS - 1) % RING, last=True)
            add(ITEMS - 1, (ITEMS - 1) % RING, TILES - 1)

        @block.scalar
        def _(act):
            def weights(i, s):
                act.wait_ge(s_z, i + 1)
                after(act, s_sum, i - 2)
                nc.scalar.activation(wx[:, s, :, D:ROW], z[:, s, 3], ACT.Exp).then_inc(s_w, 1)
            weights(0, 0)
            for i in range(1, RING + 1):
                weights(i, i % RING)
            by_threes(act, RING + 1, ITEMS - 1, weights)
            weights(ITEMS - 1, (ITEMS - 1) % RING)

        @block.tensor
        def _(pe):
            def shares(i, s, b):
                pe.wait_ge(s_sel, i + 1)
                after(pe, s_z, i - 2)
                for j in range(JG):
                    m = nc.tensor.matmul(ps_am[s][:, j, :], sel_t[:, s, j * P:(j + 1) * P], k.node_am[:, b, :], start=True,
                                         stop=True)
                m.then_inc(s_am, 1)

            def sums(i, s):
                pe.wait_ge(s_wx, i + 1)
                after(pe, s_add, i - 2)
                for j in range(JG):
                    m = nc.tensor.matmul(ps_sum[s][:], sel[:, s, j, :], wx[:, s, j, :], start=(j == 0), stop=(j == JG - 1))
                m.then_inc(s_sum, 1)

            def step(i, s):
                shares(i + 1, (s + 1) % RING, part(pe, item(pe, i), BLOCK1, TILES - 1))
                sums(i, s)
            shares(0, 0, 0)
            step(0, 0)
            for i in range(1, RING + 1):
                step(i, i % RING)
            by_threes(pe, RING + 1, ITEMS - 1, step)
            sums(ITEMS - 1, (ITEMS - 1) % RING)


def feed_forward(nc, sb, ps, sem, n, name, gelu, weights, b1, xin, s_xin, gain):
    f = Names()
    xe = sb(name + "_xe", [P, KT, P])
    xh, xl = (sb(name + v, [P, 2, KT, P], BF16) for v in ("_xh", "_xl"))
    hf = sb(name + "_hf", [P, 2, HB, P])
    hh, hl = (sb(name + v, [P, 2, HB, P], BF16) for v in ("_hh", "_hl"))
    ps_x = ps(name + "_ps_x", [P, KT, P])
    f.ps_h = ps_h = [ps(f"{name}_ps_h{i}", [P, HB, P]) for i in range(2)]
    f.ps_y = [ps(f"{name}_ps_y{i}", [P, D]) for i in range(2)]
    s_turned, s_gained, s_xhi, s_x, s_up, s_gelu, s_hhi, s_h = (
        sem(name + v) for v in ("_turned", "_gained", "_xhi", "_x", "_up", "_gelu", "_hhi", "_h"))
    f.s_down, f.s_y, f.s_turned = sem(name + "_down"), sem(name + "_y"), s_turned

    def turn(pe, i, par):
        pe.wait_ge(s_xin, i + 1)
        after(pe, s_x, i)
        for kt in range(KT):
            m = nc.tensor.transpose(ps_x[:, kt, :], xin[:, par, kt * P:(kt + 1) * P], f.ident)
        m.then_inc(s_turned, 1)

    def up(pe, i, par, w):
        pe.wait_ge(s_x, i + 1)
        after(pe, s_gelu, i - 1)
        for b in range(HB):
            steps = [(w.w1h, xh, kt) for kt in range(KT)] + [(w.w1h, xl, kt) for kt in range(KT)] + [
                (w.w1l, xh, kt) for kt in range(KT)]
            for c, (w1, xx, kt) in enumerate(steps):
                m = nc.tensor.matmul(ps_h[par][:, b, :], w1[:, kt, b, :], xx[:, par, kt, :], start=(c == 0),
                                     stop=(c == len(steps) - 1))
            if b % (HB // 2) == HB // 2 - 1:
                m.then_inc(s_up, 1)

    def down(pe, i, par, w):
        pe.wait_ge(s_h, i + 1)
        after(pe, f.s_y, i - 1)
        steps = [(hx, w2, b) for b in range(HB) for hx, w2 in ((hh, w.w2h), (hh, w.w2l), (hl, w.w2h))]
        for c, (hx, w2, b) in enumerate(steps):
            m = nc.tensor.matmul(f.ps_y[par][:], hx[:, par, b, :], w2[:, b, :], start=(c == 0),
                                 stop=(c == len(steps) - 1))
        m.then_inc(f.s_down, 1)

    def pe_program(pe):
        def step(i, par):
            up(pe, i, par, weights(pe, i))
            turn(pe, i + 1, 1 - par)
            down(pe, i - 1, 1 - par, weights(pe, i - 1))
        turn(pe, 0, 0)
        up(pe, 0, 0, weights(pe, 0))
        turn(pe, 1, 1)
        for i in (1, 2):
            step(i, i % 2)
        by_pairs(pe, 3, n - 1, step)
        up(pe, n - 1, (n - 1) % 2, weights(pe, n - 1))
        down(pe, n - 2, n % 2, weights(pe, n - 2))
        down(pe, n - 1, (n - 1) % 2, weights(pe, n - 1))

    def act_program(act):
        def step(i, par):
            bias = b1(act, i)
            after(act, s_h, i - 1)
            for b in range(HB):
                if b % (HB // 2) == 0:
                    act.wait_ge(s_up, i * 2 + (1 + b // (HB // 2)))
                m = nc.scalar.activation(hf[:, par, b, :], ps_h[par][:, b, :], gelu, bias=bias[:, b:b + 1])
            m.then_inc(s_gelu, 1)
            act.wait_ge(s_gelu, i + 1)
            after(act, f.s_down, i - 1)
            nc.scalar.copy(hh[:, par], hf[:, par]).then_inc(s_hhi, 1)
        for i in range(3):
            step(i, i % 2)
        by_pairs(act, 3, n, step)

    def split_x(dve, i, par):
        dve.wait_ge(s_turned, i + 1)
        after(dve, s_up, i * 2 - 2)
        from_ = ps_x
        if gain is not None:
            g, b = gain(dve, i)
            for kt in range(KT):
                m = nc.vector.tensor_scalar(xe[:, kt, :], ps_x[:, kt, :], g[:, kt:kt + 1], b[:, kt:kt + 1], ALU.mult, ALU.add)
            m.then_inc(s_gained, 1)
            dve.wait_ge(s_gained, i + 1)
            from_ = xe
        nc.vector.tensor_copy(xh[:, par], from_[:]).then_inc(s_xhi, 1)
        dve.wait_ge(s_xhi, i + 1)
        nc.vector.tensor_tensor(xl[:, par], from_[:], xh[:, par], ALU.subtract).then_inc(s_x, 1)

    def split_h(dve, i, par):
        dve.wait_ge(s_hhi, i + 1)
        nc.vector.tensor_tensor(hl[:, par], hf[:, par], hh[:, par], ALU.subtract).then_inc(s_h, 1)

    def dve_program(dve, before, leave):
        def step(i, par, ahead=True):
            if ahead:
                before(i + 2, par)
            split_x(dve, i + 1, 1 - par)
            split_h(dve, i, par)
            leave(i - 1, 1 - par)
        before(0, 0)
        before(1, 1)
        split_x(dve, 0, 0)
        before(2, 0)
        split_x(dve, 1, 1)
        split_h(dve, 0, 0)
        for i in (1, 2):
            step(i, i % 2)
        by_pairs(dve, 3, n - 2, step)
        step(n - 2, n % 2, ahead=False)
        split_h(dve, n - 1, (n - 1) % 2)
        leave(n - 2, n % 2)
        leave(n - 1, (n - 1) % 2)

    f.pe, f.act, f.dve = pe_program, act_program, dve_program
    return f


def row_sums(nc, dve, link, t, src):
    if src is not None:
        def one(i, _):
            nc.vector.bn_stats(t.stats[:, i, :], src[:, i, 0:D])
        by_pairs(dve, 0, TILES - 1, one)
        link(nc.vector.bn_stats(t.stats[:, TILES - 1, :], src[:, TILES - 1, 0:D]))
    link(nc.vector.tensor_tensor(t.a[:], t.stats[:, :, 1], t.stats[:, :, 4], ALU.subtract))
    link(nc.vector.tensor_tensor(t.a[:], t.a[:], t.a[:], ALU.mult))
    link(nc.vector.tensor_tensor(t.b[:], t.stats[:, :, 2], t.stats[:, :, 5], ALU.add))
    link(nc.vector.scalar_tensor_tensor(out=t.sq[:], in0=t.a[:], scalar=D / 4.0, in1=t.b[:], op0=ALU.mult, op1=ALU.add))
    link(nc.vector.tensor_tensor(t.mean[:], t.stats[:, :, 1], t.stats[:, :, 4], ALU.add))
    link(nc.vector.tensor_scalar(t.mean[:], t.mean[:], 0.5, None, ALU.mult))


def row_stats(nc, dve, link, t, src, n):
    row_sums(nc, dve, link, t, src)
    link(nc.vector.tensor_scalar(t.var[:], t.sq[:], 1.0 / D, EPS, ALU.mult, ALU.add))
    nc.vector.tensor_copy(t.root[:], t.var[:]).then_inc(t.s_var, 1)
    dve.wait_ge(t.s_root, n)
    link(nc.vector.reciprocal(t.a[:], t.root[:]))
    link(nc.vector.tensor_tensor(t.a[:], t.a[:], t.var[:], ALU.mult))
    link(nc.vector.tensor_tensor(t.a[:], t.a[:], t.root[:], ALU.add))
    link(nc.vector.reciprocal(t.rstd[:], t.a[:]))
    link(nc.vector.tensor_scalar(t.rstd[:], t.rstd[:], 2.0, None, ALU.mult))


def row_scales(nc, dve, link, t, n):
    link(nc.vector.tensor_tensor(t.b[:], t.mean[:], t.mean[:], ALU.mult))
    nc.vector.scalar_tensor_tensor(out=t.root[:], in0=t.b[:], scalar=float(D), in1=t.sq[:], op0=ALU.mult,
                                   op1=ALU.add).then_inc(t.s_var, 1)
    dve.wait_ge(t.s_root, n)
    link(nc.vector.tensor_scalar(t.root[:], t.root[:], 1e-12, None, ALU.max))
    link(nc.vector.reciprocal(t.scale[:], t.root[:]))
    link(nc.vector.tensor_scalar(t.scale[:], t.scale[:], float(D) ** 0.5, None, ALU.mult))


def roots(nc, act, t, first, count):
    for n in range(first, first + count):
        act.wait_ge(t.s_var, n)
        nc.scalar.activation(t.root[:], t.root[:], ACT.Sqrt).then_inc(t.s_root, 1)


def stat_tiles(sb, sem, name):
    t = Names()
    t.stats = sb(name + "_stats", [P, TILES, 6])
    t.s_var, t.s_root = sem(name + "_s_var"), sem(name + "_s_root")
    t.a, t.b, t.sq, t.var, t.root, t.mean, t.rstd, t.scale = (
        sb(name + "_" + v, [P, TILES]) for v in ("a", "b", "sq", "var", "root", "mean", "rstd", "scale"))
    return t


def nodes_finish(nc, k, a):
    with ExitStack() as own, nc.Block() as block:
        def sb(name, shape, dt=F32):
            return own.enter_context(nc.sbuf_tensor(name, shape, dt))

        def ps(name, shape):
            return own.enter_context(nc.psum_tensor(name, shape, F32))

        def sem(name):
            return own.enter_context(nc.semaphore(name))

        raw1 = sb("raw1", [P, KT, HID])
        raw2 = sb("raw2", [P, HB, D])
        w = Weights(sb("w1h", [P, KT, HB, P], BF16), sb("w1l", [P, KT, HB, P], BF16),
                    sb("w2h", [P, HB, D], BF16), sb("w2l", [P, HB, D], BF16))
        b1 = sb("fb1", [P, HB])
        t = stat_tiles(sb, sem, "fin")
        xin = sb("xin", [P, 2, D])
        rden = sb("rden", [P, TILES, GH])
        s_w, s_whi, s_split, s_link, s_xin, s_base, s_sum = (
            sem(n) for n in ("f_w", "f_whi", "f_split", "f_link", "f_xin", "f_base", "f_sum"))
        s_qcopy, s_qt, s_qt_out, s_mix, s_mix_out = (sem(n) for n in ("f_qcopy", "f_qt", "f_qt_out", "f_mix", "f_mix_out"))
        f = feed_forward(nc, sb, ps, sem, TILES, "g", ACT.Gelu_apprx_tanh, lambda eng, i: w, lambda eng, i: b1, xin, s_xin, None)
        f.ident = k.ident[:]
        ps_mix = f.ps_h
        qs, qt = xin, sb("qt", [P, 2, P])

        @block.sync
        def _(sp):
            sp.dma_start(raw1[:], a.f_w1.rearrange("(k p) h -> p k h", p=P)).then_inc(s_w, 16)
            sp.dma_start(raw2[:], a.f_w2.rearrange("(p b) d -> p b d", b=HB)).then_inc(s_w, 16)
            sp.dma_start(b1[:], a.f_b1.rearrange("(p b) -> p b", b=HB)).then_inc(s_w, 16)

        @block.gpsimd
        def _(pool):
            nc.gpsimd.tensor_tensor(k.acc[:], k.acc[:], k.xn0[:], ALU.add).then_inc(s_base, 1)
            pool.wait_ge(s_base, 1)
            nc.gpsimd.tensor_tensor(k.acc[:], k.acc[:], k.fb2[:].unsqueeze(1).to_broadcast([P, TILES, D]),
                                    ALU.add).then_inc(s_base, 1)

        @block.tensor
        def _(pe):
            def turn(i, par):
                pe.wait_ge(s_qcopy, i + 1)
                after(pe, s_qt_out, i - 1)
                nc.tensor.transpose(f.ps_y[par][:, 0:P], qs[:, par, 0:P], k.ident[:]).then_inc(s_qt, 1)

            def mix(i, par):
                pe.wait_ge(s_qt_out, i + 1)
                after(pe, s_mix_out, i - 1)
                nc.tensor.matmul(ps_mix[par][:, 0:KT, :], qt[:, par, :], k.cw[:], start=True, stop=True).then_inc(s_mix, 1)

            def step(i, par):
                turn(i + 1, 1 - par)
                mix(i, par)
            turn(0, 0)
            step(0, 0)
            step(1, 1)
            by_pairs(pe, 2, TILES - 1, step)
            mix(TILES - 1, (TILES - 1) % 2)
            pe.wait_ge(s_mix_out, TILES)
            pe.wait_ge(s_split, 4)
            f.pe(pe)

        @block.scalar
        def _(act):
            roots(nc, act, t, 1, 1)
            act.wait_ge(s_w, 48)
            nc.scalar.copy(w.w1h[:], raw1[:].rearrange("p k (m b) -> p k b m", b=HB)).then_inc(s_whi, 1)
            nc.scalar.copy(w.w2h[:], raw2[:]).then_inc(s_whi, 1)

            def step(i, par):
                after(act, s_qt, i - 1)
                nc.scalar.copy(qs[:, par, 0:P], k.q[:, i, :]).then_inc(s_qcopy, 1)

            def out(i, par):
                act.wait_ge(s_qt, i + 1)
                after(act, s_mix, i - 1)
                nc.scalar.copy(qt[:, par, :], f.ps_y[par][:, 0:P]).then_inc(s_qt_out, 1)

            def both(i, par):
                step(i + 1, 1 - par)
                out(i, par)
            step(0, 0)
            both(0, 0)
            both(1, 1)
            by_pairs(act, 2, TILES - 1, both)
            out(TILES - 1, (TILES - 1) % 2)
            roots(nc, act, t, 2, 1)
            f.act(act)

        @block.vector
        def _(dve):
            link = Chain(dve, s_link)
            link(nc.vector.reciprocal(rden[:], k.agg[:, :, D:ROW]))
            for t0, t1 in ((0, 13), (13, TILES)):
                hv = k.agg[:, t0:t1, 0:D].rearrange("p t (h d) -> p t h d", h=GH)
                link(nc.vector.tensor_tensor(hv, hv, rden[:, t0:t1, :].unsqueeze(3).to_broadcast([P, t1 - t0, GH, GHD]),
                                             ALU.mult))
            link(nc.vector.tensor_tensor(k.agg[:, :, 0:D], k.agg[:, :, 0:D], k.res[:], ALU.add))
            row_stats(nc, dve, link, t, k.agg, 1)

            def graph_norm(i, _):
                nc.vector.tensor_scalar(k.agg[:, i, 0:D], k.agg[:, i, 0:D], t.mean[:, bass.ds(i, 1)],
                                        t.rstd[:, bass.ds(i, 1)], ALU.subtract, ALU.mult)
            by_pairs(dve, 0, TILES - 1, graph_norm)
            i = TILES - 1
            link(nc.vector.tensor_scalar(k.agg[:, i, 0:D], k.agg[:, i, 0:D], t.mean[:, i:i + 1], t.rstd[:, i:i + 1],
                                         ALU.subtract, ALU.mult))
            dve.wait_ge(s_whi, 2)
            link(nc.vector.tensor_tensor(w.w1l[:], raw1[:].rearrange("p k (m b) -> p k b m", b=HB), w.w1h[:], ALU.subtract))
            nc.vector.tensor_tensor(w.w2l[:], raw2[:], w.w2h[:], ALU.subtract).then_inc(s_split, 4)

            def mixed(i, par):
                dve.wait_ge(s_mix, i + 1)
                nc.vector.tensor_tensor(k.res[:, i, :], ps_mix[par][:, 0:KT, :].rearrange("p a b -> p (a b)"), k.bout[:],
                                        ALU.add).then_inc(s_mix_out, 1)
            by_pairs(dve, 0, TILES, mixed)
            dve.wait_ge(s_mix_out, TILES)
            row_sums(nc, dve, link, t, k.res)
            row_scales(nc, dve, link, t, 2)

            def scaled(i, _):
                nc.vector.scalar_tensor_tensor(out=k.res[:, i, :], in0=k.res[:, i, :], scalar=t.scale[:, bass.ds(i, 1)],
                                               in1=k.gout[:], op0=ALU.mult, op1=ALU.mult)
            by_pairs(dve, 0, TILES - 1, scaled)
            i = TILES - 1
            link(nc.vector.scalar_tensor_tensor(out=k.res[:, i, :], in0=k.res[:, i, :], scalar=t.scale[:, i:i + 1],
                                                in1=k.gout[:], op0=ALU.mult, op1=ALU.mult))
            dve.wait_ge(s_base, 2)
            link(nc.vector.tensor_tensor(k.acc[:], k.acc[:], k.res[:], ALU.add))
            dve.wait_ge(s_qt, TILES)

            base = link.n

            def before(i, par):
                link.n = i * 2 + base
                after(dve, f.s_turned, i - 1)
                link(nc.vector.tensor_tensor(k.agg[:, i, 0:D], k.agg[:, i, 0:D], k.g2[:], ALU.mult))
                nc.vector.tensor_tensor(xin[:, par, :], k.agg[:, i, 0:D], k.b2n[:], ALU.add).then_inc(s_xin, 1)
                dve.wait_ge(s_xin, i + 1)
                link(nc.vector.tensor_tensor(k.acc[:, i, :], k.acc[:, i, :], xin[:, par, :], ALU.add))

            def leave(i, par):
                dve.wait_ge(f.s_down, i + 1)
                nc.vector.tensor_tensor(k.acc[:, i, :], k.acc[:, i, :], f.ps_y[par][:], ALU.add).then_inc(f.s_y, 1)
            f.dve(dve, before, leave)


def route(nc, k, a):
    with ExitStack() as own, nc.Block() as block:
        def sb(name, shape, dt=F32):
            return own.enter_context(nc.sbuf_tensor(name, shape, dt))

        def ps(name, shape):
            return own.enter_context(nc.psum_tensor(name, shape, F32))

        def sem(name):
            return own.enter_context(nc.semaphore(name))

        raw1 = [sb(f"r_raw1{i}", [P, KT, HID]) for i in range(2)]
        raw2 = [sb(f"r_raw2{i}", [P, HB, D]) for i in range(1)]
        wr = sb("wr", [P, KT, EXP])
        br = sb("br", [P, EXP])
        t = stat_tiles(sb, sem, "r1")
        t2 = stat_tiles(sb, sem, "r2")
        xt = sb("xt", [P, 2, D])
        xt_t = sb("xt_t", [P, 2, KT, P])
        xn = sb("xn", [P, 2, D])
        index = sb("r_index", [P, 2, TOPK], I32)
        logit, eq, enc, o1, o2, both, rank, total, incl = (
            sb("r_" + n, [P, TILES, EXP]) for n in ("logit", "eq", "enc", "o1", "o2", "both", "rank", "total", "incl"))
        best = sb("best", [P, 3, TILES])
        rev = sb("rev", [P, EXP])
        lower = sb("lower", [P, P])
        tile_no = sb("tile_no", [P, P])
        per_e = sb("per_e", [P, 6, EXP])
        per_ei = sb("per_ei", [P, EXP], I32)
        cmp = sb("cmp", [1, MOE_TILES, EXP - 1])
        tile_f = sb("tile_f", [1, MOE_TILES])
        place_f = sb("place_f", [P, TILES, TOPK])
        zero = sb("zero", [P, TILES])
        ps_t = [ps(f"r_ps_t{i}", [P, KT, P]) for i in range(2)]
        ps_l = ps("r_ps_l", [P, TILES, EXP])
        ps_r = ps("r_ps_r", [P, TILES, EXP])
        ps_n = ps("r_ps_n", [P, TILES, EXP])

        s_small, s_iota, s_link, s_xt, s_turned, s_xt_t, s_logit, s_exp_in, s_exp, s_both, s_rank = (
            sem(n) for n in ("r_small", "r_iota", "r_link", "r_xt", "r_turned", "r_xt_t", "r_logit", "r_exp_in", "r_exp",
                             "r_both", "r_rank"))
        s_place, s_xn, s_idx, s_pool = sem("r_place"), sem("r_xn"), sem("r_idx"), sem("r_pool")
        s_put = [sem(f"r_put{i}") for i in range(2)]
        s_raw1 = [sem(f"r_s_raw1{i}") for i in range(2)]
        s_raw2 = sem("r_s_raw2")
        s_hi1, s_hi2, s_lo1, s_lo2 = (sem(n) for n in ("r_hi1", "r_hi2", "r_lo1", "r_lo2"))

        @block.sync
        def _(sp):
            sp.dma_start(wr[:], a.e_Wr.rearrange("(k p) e -> p k e", p=P)).then_inc(s_small, 16)
            sp.dma_start(br[:], row_on_all(a.e_br)).then_inc(s_small, 16)

            def load(e, par):
                after(sp, s_lo1, e - 1)
                sp.dma_start(raw1[par][:], a.e_W1[bass.ds(e, 1), :, :].rearrange("e (k p) h -> p (e k) h", p=P)).then_inc(
                    s_raw1[par], 16)
                after(sp, s_lo2, e)
                sp.dma_start(raw2[0][:], a.e_W2[bass.ds(e, 1), :, :].rearrange("e (p b) d -> p (e b) d", b=HB)).then_inc(
                    s_raw2, 16)
            load(0, 0)
            load(1, 1)
            by_pairs(sp, 2, EXP, load)

        @block.gpsimd
        def _(pool):
            nc.gpsimd.iota(tile_no[:], pattern=[[1, P]], base=0, channel_multiplier=0,
                           allow_small_or_imprecise_dtypes=True).then_inc(s_iota, 1)
            nc.gpsimd.iota(rev[:], pattern=[[-1, EXP]], base=EXP, channel_multiplier=0,
                           allow_small_or_imprecise_dtypes=True).then_inc(s_iota, 1)
            nc.gpsimd.memset(zero[:], 0.0).then_inc(s_iota, 1)
            pool.wait_ge(s_place, 1)

            def put(i, par):
                after(pool, s_put[par], i * 16 - 16 * par)
                pool.sem_inc(s_pool, 1)
                nc.gpsimd.tensor_copy(index[:, par, :], k.place_i[:, i, :]).then_inc(s_idx, 1)
                pool.wait_ge(s_idx, i + 1)
                pool.sem_inc(s_pool, 1)
                pool.wait_ge(s_xn, i + 1)
                pool.sem_inc(s_pool, 1)
                for c in range(TOPK):
                    nc.gpsimd.indirect_dma_start(k.rows_in, bass.IndirectOffsetOnAxis(ap=index[:, par, c:c + 1], axis=0),
                                                 xn[:, par, :], None).then_inc(s_put[par], 16)
            put(0, 0)
            put(1, 1)
            by_pairs(pool, 2, TILES, put)
            pool.wait_ge(s_put[0], 32 * (TILES - TILES // 2))
            pool.wait_ge(s_put[1], 32 * (TILES // 2))

        @block.scalar
        def _(act):
            roots(nc, act, t, 1, 1)

            def out(i, par):
                act.wait_ge(s_turned, i + 1)
                after(act, s_logit, i - 1)
                nc.scalar.copy(xt_t[:, par], ps_t[par][:]).then_inc(s_xt_t, 1)
            out(0, 0)
            out(1, 1)
            by_pairs(act, 2, TILES, out)
            roots(nc, act, t2, 1, 1)
            act.wait_ge(s_exp_in, 1)
            nc.scalar.activation(best[:, 2, :], best[:, 2, :], ACT.Exp).then_inc(s_exp, 1)

            def high(e, par):
                act.wait_ge(s_raw1[par], e * 8 + (16 - 8 * par))
                nc.scalar.copy(k.w1[:, e, 0], raw1[par][:].rearrange("p k (m b) -> p k b m", b=HB)).then_inc(s_hi1, 1)
                act.wait_ge(s_raw2, (e + 1) * 16)
                nc.scalar.copy(k.w2[:, e, 0], raw2[0][:]).then_inc(s_hi2, 1)
            by_pairs(act, 0, EXP, high)

        @block.tensor
        def _(pe):
            pe.wait_ge(s_small, 32)

            def turn(i, par):
                pe.wait_ge(s_xt, i + 1)
                after(pe, s_xt_t, i - 1)
                for kt in range(KT):
                    m = nc.tensor.transpose(ps_t[par][:, kt, :], xt[:, par, kt * P:(kt + 1) * P], k.ident[:])
                m.then_inc(s_turned, 1)

            def logits(i, par):
                pe.wait_ge(s_xt_t, i + 1)
                for kt in range(KT):
                    m = nc.tensor.matmul(ps_l[:, i, :], xt_t[:, par, kt, :], wr[:, kt, :], start=(kt == 0),
                                         stop=(kt == KT - 1))
                m.then_inc(s_logit, 1)

            def step(i, par):
                turn(i + 1, 1 - par)
                logits(i, par)
            turn(0, 0)
            step(0, 0)
            step(1, 1)
            by_pairs(pe, 2, TILES - 1, step)
            logits(TILES - 1, (TILES - 1) % 2)
            pe.wait_ge(s_both, 1)
            nc.tensor.matmul(ps_r[:], lower[:], both[:], start=True, stop=True)
            nc.tensor.matmul(ps_n[:], k.ones[:], both[:], start=True, stop=True).then_inc(s_rank, 1)

        @block.vector
        def _(dve):
            link = Chain(dve, s_link)
            row_stats(nc, dve, link, t, k.acc, 1)

            def normed(i, par, to):
                return nc.vector.tensor_scalar(to[:, par, :], k.acc[:, i, :], t.mean[:, bass.ds(i, 1)],
                                               t.rstd[:, bass.ds(i, 1)], ALU.subtract, ALU.mult)

            def tile(i, par):
                after(dve, s_turned, i - 1)
                normed(i, par, xt).then_inc(s_xt, 1)
                dve.wait_ge(s_xt, i + 1)
                nc.vector.bn_stats(t2.stats[:, i, :], xt[:, par, :])
            tile(0, 0)
            tile(1, 1)
            by_pairs(dve, 2, TILES, tile)
            dve.wait_ge(s_iota, 3)
            link(nc.vector.tensor_scalar(lower[:], tile_no[:], k.pidx[:, 0:1], None, ALU.is_gt))
            row_stats(nc, dve, link, t2, None, 1)

            def over_e(v):
                return v.unsqueeze(2).to_broadcast([P, TILES, EXP])

            def over_t(v):
                return v.unsqueeze(1).to_broadcast([P, TILES, EXP])
            dve.wait_ge(s_logit, TILES)
            dve.wait_ge(s_small, 32)
            link(nc.vector.tensor_tensor(logit[:], ps_l[:], over_t(br[:]), ALU.add))
            for c, o in enumerate((o1, o2)):
                link(nc.vector.tensor_reduce(best[:, c, :], logit[:], AX_X, ALU.max))
                link(nc.vector.tensor_tensor(eq[:], logit[:], over_e(best[:, c, :]), ALU.is_equal))
                link(nc.vector.tensor_tensor(enc[:], eq[:], over_t(rev[:]), ALU.mult))
                link(nc.vector.tensor_reduce(best[:, 2, :], enc[:], AX_X, ALU.max))
                link(nc.vector.tensor_tensor(o[:], enc[:], over_e(best[:, 2, :]), ALU.is_equal))
                if c == 0:
                    link(nc.vector.scalar_tensor_tensor(out=logit[:], in0=o[:], scalar=-BIG, in1=logit[:], op0=ALU.mult,
                                                        op1=ALU.add))
            nc.vector.tensor_tensor(both[:], o1[:], o2[:], ALU.add).then_inc(s_both, 1)
            nc.vector.tensor_tensor(best[:, 2, :], best[:, 1, :], best[:, 0, :], ALU.subtract).then_inc(s_exp_in, 1)
            dve.wait_ge(s_exp, 1)
            link(nc.vector.tensor_scalar(best[:, 0, :], best[:, 2, :], 1.0, None, ALU.add))
            link(nc.vector.reciprocal(k.share[:, :, 0], best[:, 0, :]))
            link(nc.vector.tensor_tensor(k.share[:, :, 1], k.share[:, :, 0], best[:, 2, :], ALU.mult))
            dve.wait_ge(s_rank, 1)
            link(nc.vector.tensor_copy(total[:], ps_n[:]))
            for e in range(EXP):
                m = nc.vector.tensor_tensor_scan(incl[:, :, e], total[:, :, e], zero[:], 0.0, ALU.add, ALU.add)
            link(m)
            link(nc.vector.tensor_tensor(rank[:], incl[:], total[:], ALU.subtract))
            link(nc.vector.tensor_tensor(rank[:], rank[:], ps_r[:], ALU.add))
            link(nc.vector.tensor_scalar(per_e[:, 0, :], incl[:, TILES - 1, :], float(P - 1), None, ALU.add))
            link(nc.vector.tensor_copy(per_ei[:], per_e[:, 0, :]))
            link(nc.vector.tensor_scalar(per_ei[:], per_ei[:], P.bit_length() - 1, None, ALU.arith_shift_right))
            link(nc.vector.tensor_copy(per_e[:, 1, :], per_ei[:]))
            link(nc.vector.tensor_tensor_scan(per_e[:, 2, :], per_e[:, 1, :], zero[:, 0:EXP], 0.0, ALU.add, ALU.add))
            link(nc.vector.tensor_tensor(per_e[:, 3, :], per_e[:, 2, :], per_e[:, 1, :], ALU.subtract))
            link(nc.vector.tensor_scalar(per_e[:, 4, :], per_e[:, 3, :], float(P), None, ALU.mult))
            link(nc.vector.tensor_tensor(rank[:], rank[:], over_t(per_e[:, 4, :]), ALU.add))
            for c, o in enumerate((o1, o2)):
                link(nc.vector.tensor_tensor(enc[:], rank[:], o[:], ALU.mult))
                link(nc.vector.tensor_reduce(place_f[:, :, c], enc[:], AX_X, ALU.add))
            nc.vector.tensor_copy(k.place_i[:], place_f[:]).then_inc(s_place, 1)
            link(nc.vector.tensor_tensor(cmp[:], tile_no[0:1, 0:MOE_TILES].unsqueeze(2).to_broadcast([1, MOE_TILES, EXP - 1]),
                                         per_e[0:1, 3, 1:EXP].unsqueeze(1).to_broadcast([1, MOE_TILES, EXP - 1]), ALU.is_ge))
            link(nc.vector.tensor_reduce(tile_f[:], cmp[:], AX_X, ALU.add))
            link(nc.vector.tensor_copy(k.tile_expert[:], tile_f[:]))

            def row(i, par):
                after(dve, s_put[par], i * 16 - 16 * par)
                link(normed(i, par, xt))
                nc.vector.tensor_scalar(xn[:, par, :], xt[:, par, :], t2.mean[:, bass.ds(i, 1)], t2.rstd[:, bass.ds(i, 1)],
                                        ALU.subtract, ALU.mult).then_inc(s_xn, 1)
            dve.wait_ge(s_turned, TILES)
            base = link.n

            def counted(i, par):
                link.n = i + base
                row(i, par)
            for i in range(2):
                counted(i, i)
            by_pairs(dve, 2, TILES, counted)
            link.n = base + TILES

            def low(e, par):
                dve.wait_ge(s_hi1, e + 1)
                nc.vector.tensor_tensor(k.w1[:, e, 1], raw1[par][:].rearrange("p k (m b) -> p k b m", b=HB), k.w1[:, e, 0],
                                        ALU.subtract).then_inc(s_lo1, 1)
                dve.wait_ge(s_hi2, e + 1)
                nc.vector.tensor_tensor(k.w2[:, e, 1], raw2[0][:], k.w2[:, e, 0], ALU.subtract).then_inc(s_lo2, 1)
            by_pairs(dve, 0, EXP, low)


def experts(nc, k, a):
    with ExitStack() as own, nc.Block() as block:
        def sb(name, shape, dt=F32):
            return own.enter_context(nc.sbuf_tensor(name, shape, dt))

        def ps(name, shape):
            return own.enter_context(nc.psum_tensor(name, shape, F32))

        def sem(name):
            return own.enter_context(nc.semaphore(name))

        ln_cols = sb("ln_cols", [P, EXP, 2, KT])
        b1 = sb("e_b1", [P, EXP, HB])
        b2 = sb("e_b2", [P, EXP, D])
        xin = sb("e_xin", [P, 2, D])
        y = sb("e_y", [P, 2, D])
        s_small, s_xin, s_pool = sem("e_small"), sem("e_xin_s"), sem("e_pool")
        s_load = [sem(f"e_load{i}") for i in range(2)]
        s_store = [sem(f"e_store{i}") for i in range(2)]

        def expert(eng, i):
            return eng.value_load(k.tile_expert[0:1, bass.ds(i, 1)], min_val=0, max_val=EXP - 1)

        def weights(pe, i):
            e = expert(pe, i)
            return Weights(k.w1[:, e, 0], k.w1[:, e, 1], k.w2[:, e, 0], k.w2[:, e, 1])

        def gain(dve, i):
            e = expert(dve, i)
            return ln_cols[:, e, 0, :], ln_cols[:, e, 1, :]

        f = feed_forward(nc, sb, ps, sem, MOE_TILES, "e", ACT.Gelu, weights, lambda act, i: b1[:, expert(act, i), :], xin,
                         s_xin, gain)
        f.ident = k.ident[:]

        @block.gpsimd
        def _(pool):
            def landed(i, par):
                pool.wait_ge(s_load[1 - par], i * 8 + 8 * par)
                pool.sem_inc(s_xin, 1)

            def load(i, par):
                after(pool, f.s_turned, i - 1)
                pool.sem_inc(s_pool, 1)
                pool.dma_start(xin[:, par, :], k.rows_in[bass.ds(i * P, P), :]).then_inc(s_load[par], 16)
                if not (isinstance(i, int) and i == 0):
                    landed(i, par)
            load(0, 0)
            load(1, 1)
            by_pairs(pool, 2, MOE_TILES, load)
            landed(MOE_TILES, MOE_TILES % 2)

        @block.sync
        def _(sp):
            for n, v in enumerate((a.e_lng, a.e_lnb)):
                for e in range(EXP):
                    sp.dma_start(ln_cols[:, e, n, :], cols(v[e])).then_inc(s_small, 16)
            sp.dma_start(b1[:], a.e_b1.rearrange("e (p b) -> p e b", b=HB)).then_inc(s_small, 16)
            sp.dma_start(b2[:], a.e_b2.rearrange("e d -> (e d)").rearrange("(a n) -> a n", a=1).to_broadcast([P, EXP * D])
                         ).then_inc(s_small, 16)

            def store(i, par):
                sp.wait_ge(f.s_y, i + 1)
                sp.dma_start(k.rows_out[bass.ds(i * P, P), :], y[:, par, :]).then_inc(s_store[par], 16)
            by_pairs(sp, 0, MOE_TILES, store)
            sp.wait_ge(s_store[0], 16 * (MOE_TILES - MOE_TILES // 2))
            sp.wait_ge(s_store[1], 16 * (MOE_TILES // 2))

        @block.tensor
        def _(pe):
            f.pe(pe)

        @block.scalar
        def _(act):
            act.wait_ge(s_small, 16 * (2 * EXP + 2))
            f.act(act)

        @block.vector
        def _(dve):
            dve.wait_ge(s_small, 16 * (2 * EXP + 2))

            def leave(i, par):
                e = expert(dve, i)
                dve.wait_ge(f.s_down, i + 1)
                after(dve, s_store[par], i * 8 - 8 * par)
                nc.vector.tensor_tensor(y[:, par, :], f.ps_y[par][:], b2[:, e, :], ALU.add).then_inc(f.s_y, 1)
            f.dve(dve, lambda i, par: None, leave)


def combine(nc, k, a):
    with ExitStack() as own, nc.Block() as block:
        def sb(name, shape, dt=F32):
            return own.enter_context(nc.sbuf_tensor(name, shape, dt))

        def sem(name):
            return own.enter_context(nc.semaphore(name))

        got = sb("got", [P, 2, TOPK, D])
        index = sb("c_index", [P, 2, TOPK], I32)
        s_idx, s_got, s_sum, s_out, s_pool, s_first = (
            sem(n) for n in ("c_idx", "c_got", "c_sum", "c_out", "c_pool", "c_first"))
        s_get = [sem(f"c_get{i}") for i in range(2)]

        @block.gpsimd
        def _(pool):
            def landed(i, par):
                pool.wait_ge(s_get[1 - par], i * 16 + 16 * par)
                pool.sem_inc(s_got, 1)

            def get(i, par):
                nc.gpsimd.tensor_copy(index[:, par, :], k.place_i[:, i, :]).then_inc(s_idx, 1)
                pool.wait_ge(s_idx, i + 1)
                pool.sem_inc(s_pool, 1)
                after(pool, s_sum, i - 1)
                pool.sem_inc(s_pool, 1)
                for c in range(TOPK):
                    nc.gpsimd.indirect_dma_start(got[:, par, c, :], None, k.rows_out, bass.IndirectOffsetOnAxis(
                        ap=index[:, par, c:c + 1], axis=0)).then_inc(s_get[par], 16)
                if not (isinstance(i, int) and i == 0):
                    landed(i, par)
            get(0, 0)
            get(1, 1)
            by_pairs(pool, 2, TILES, get)
            landed(TILES, TILES % 2)

        @block.vector
        def _(dve):
            def total(i, par):
                dve.wait_ge(s_got, i + 1)
                nc.vector.scalar_tensor_tensor(out=k.acc[:, i, :], in0=got[:, par, 0, :], scalar=k.share[:, i, 0:1],
                                               in1=k.acc[:, i, :], op0=ALU.mult, op1=ALU.add).then_inc(s_first, 1)
                dve.wait_ge(s_first, i + 1)
                nc.vector.scalar_tensor_tensor(out=k.acc[:, i, :], in0=got[:, par, 1, :], scalar=k.share[:, i, 1:2],
                                               in1=k.acc[:, i, :], op0=ALU.mult, op1=ALU.add).then_inc(s_sum, 1)
            by_pairs(dve, 0, TILES, total)

        @block.sync
        def _(sp):
            def store(i, par):
                sp.wait_ge(s_sum, i + 1)
                sp.dma_start(a.out[bass.ds(i * P, P), :], k.acc[:, i, :]).then_inc(s_out, 16)
            by_pairs(sp, 0, FULL, store)
            sp.wait_ge(s_sum, TILES)
            sp.dma_start(a.out[FULL * P:N, :], k.acc[0:REST, FULL, :]).then_inc(s_out, 16)
            sp.wait_ge(s_out, 16 * TILES)


def gnn_moe_layer(nc, x, src, dst, g_W, g_as, g_ad, g_bias, g_Wres, ln1_g, ln1_b, ln2_g, ln2_b, f_w1, f_b1,
                  f_w2, f_b2, m_qkv, m_mem, m_wout, m_bout, m_gout, m_gpre, e_Wr, e_br, e_lng, e_lnb, e_W1,
                  e_b1, e_W2, e_b2, out, stages=4):
    a = Names()
    a.x = x
    a.src = src
    a.dst = dst
    a.g_W = g_W
    a.g_as = g_as
    a.g_ad = g_ad
    a.g_bias = g_bias
    a.g_Wres = g_Wres
    a.ln1_g = ln1_g
    a.ln1_b = ln1_b
    a.ln2_g = ln2_g
    a.ln2_b = ln2_b
    a.f_w1 = f_w1
    a.f_b1 = f_b1
    a.f_w2 = f_w2
    a.f_b2 = f_b2
    a.m_qkv = m_qkv
    a.m_mem = m_mem
    a.m_wout = m_wout
    a.m_bout = m_bout
    a.m_gout = m_gout
    a.m_gpre = m_gpre
    a.e_Wr = e_Wr
    a.e_br = e_br
    a.e_lng = e_lng
    a.e_lnb = e_lnb
    a.e_W1 = e_W1
    a.e_b1 = e_b1
    a.e_W2 = e_W2
    a.e_b2 = e_b2
    a.out = out
    k = Names()
    with ExitStack() as top, nc.allow_non_contiguous_dma(reason="a few hundred small constants"):
        def keep(stack, name, shape, dt=F32):
            return stack.enter_context(nc.sbuf_tensor(name, shape, dt))

        def scratch(name, shape):
            return nc.dram_tensor(name, shape, F32, kind="Internal").ap()

        k.table = scratch("table", (NP, ROW))
        k.dst_f = scratch("dst_f", (GROUPS, EG))
        k.rows_in = scratch("rows_in", (MOE_TILES * P, D))
        k.rows_out = scratch("rows_out", (MOE_TILES * P, D))
        k.ident = keep(top, "ident", [P, P])
        k.ones = keep(top, "ones", [P, P])
        k.pidx = keep(top, "pidx", [P, 1])
        k.acc = keep(top, "acc", [P, TILES, D])
        with ExitStack() as graph:
            k.agg = keep(graph, "agg", [P, TILES, ROW])
            k.res = keep(graph, "res", [P, TILES, D])
            k.q = keep(graph, "q", [P, TILES, MC])
            k.xn0 = keep(graph, "xn0", [P, TILES, D])
            k.cw = keep(graph, "cw", [P, D])
            k.node_am = keep(graph, "node_am", [P, TILES, 2 * GH])
            k.bout, k.gout, k.g2, k.b2n, k.fb2 = (keep(graph, n, [P, D]) for n in ("bout", "gout", "g2", "b2n", "fb2"))
            k.iota_n = keep(graph, "iota_n", [P, NP])
            k.src_i = keep(graph, "src_i", [P, JG, GROUPS], I32)
            k.dst_e = keep(graph, "dst_e", [P, JG, GROUPS])
            k.node_id = keep(graph, "node_id", [P, TILES])
            k.items = keep(graph, "items", [1, ITEMS], I32)
            k.need = keep(graph, "need", [1, NEED // RING], I32)
            setup_and_nodes(nc, k, a)
            if stages >= 2:
                graph_items(nc, k, a)
            if stages >= 3:
                nodes_finish(nc, k, a)
        if stages >= 4:
            k.w1 = keep(top, "w1", [P, EXP, 2, KT, HB, P], BF16)
            k.w2 = keep(top, "w2", [P, EXP, 2, HB, D], BF16)
            k.place_i = keep(top, "place_i", [P, TILES, TOPK], I32)
            k.share = keep(top, "share", [P, TILES, TOPK])
            k.tile_expert = keep(top, "tile_expert", [1, MOE_TILES], I32)
            route(nc, k, a)
            experts(nc, k, a)
            combine(nc, k, a)


_INS = {
    "x": "x", "src": "src", "dst": "dst", "L0_gnn_W": "g_W", "L0_gnn_att_src": "g_as", "L0_gnn_att_dst": "g_ad",
    "L0_gnn_bias": "g_bias", "L0_gnn_W_res": "g_Wres", "L0_gnn_ln1_g": "ln1_g", "L0_gnn_ln1_b": "ln1_b",
    "L0_gnn_ln2_g": "ln2_g", "L0_gnn_ln2_b": "ln2_b", "L0_gnn_ffn_w1": "f_w1", "L0_gnn_ffn_b1": "f_b1",
    "L0_gnn_ffn_w2": "f_w2", "L0_gnn_ffn_b2": "f_b2", "L0_mix_w_qkv": "m_qkv", "L0_mix_mem_kv": "m_mem",
    "L0_mix_w_out": "m_wout", "L0_mix_b_out": "m_bout", "L0_mix_g_out": "m_gout", "L0_mix_g_pre": "m_gpre",
    "L0_ffn_Wr": "e_Wr", "L0_ffn_br": "e_br", "L0_ffn_ln_g": "e_lng", "L0_ffn_ln_b": "e_lnb", "L0_ffn_W1": "e_W1",
    "L0_ffn_b1": "e_b1", "L0_ffn_W2": "e_W2", "L0_ffn_b2": "e_b2",
}


def kernel(**inputs):
    import numpy as _np
    import concourse.bacc as _bacc
    from concourse import mybir as _mybir
    from concourse.bass_utils import run_bass_kernel_spmd as _run

    nc = _bacc.Bacc("TRN2", target_bir_lowering=False, num_devices=1)
    arrays, args = {}, {}
    for name, short in _INS.items():
        v = _np.ascontiguousarray(inputs[name])
        arrays[f"in_{name}_dram"] = v
        args[short] = nc.dram_tensor(f"in_{name}_dram", v.shape, _mybir.dt.from_np(v.dtype), kind="ExternalInput").ap()
    args["out"] = nc.dram_tensor("out_0_dram", (N, D), F32, kind="ExternalOutput").ap()
    gnn_moe_layer(nc, **args)
    r = _run(nc, [arrays], core_ids=[0])
    return r.results[0]["out_0_dram"]
```

```python
from contextlib import ExitStack

import concourse.bass as bass
from concourse import mybir

P = 128
F32 = mybir.dt.float32
BF16 = mybir.dt.bfloat16
I32 = mybir.dt.int32
ALU = mybir.AluOpType
ACT = mybir.ActivationFunctionType
AX_X = mybir.AxisListType.X
RMAX = bass.bass_isa.ReduceOp.max

N = 3125
E = 50000
D = 256
KT = D // P
TILES = -(-N // P)
NP = TILES * P
FULL = N // P
REST = N - FULL * P
GH, GHD = 8, 32
MH, MHD, MEM = 4, 32, 4
MC = MH * MHD
HID = 1024
HB = HID // P
EXP = 8
TOPK = 2
JG = 4
EG = JG * P
GROUPS = -(-E // EG)
GFULL = E // EG
GREST = E - GFULL * EG
ITEMS = GROUPS + TILES - 1
RING = 3
GRING = 4
UNROLL = 6
ROW = D + GH
WIDE = 2
MP = WIDE * P
MOE_STEPS = (NP * TOPK - EXP) // MP + EXP
EXPERT_BITS = (EXP - 1).bit_length()
LAST, OWN, NEXT = range(3)
NEED_BITS, NEED_PER = ITEMS.bit_length(), GRING
NEED = -(-GROUPS // NEED_PER) * NEED_PER
BACK, FIELDS = 2, 4
BLOCK_BITS = (TILES - 1).bit_length()
WORDS = ITEMS + 2
EPS = 1e-5
SLOPE = 0.2
BIG = 1e30


class Names:
    pass


class Weights:

    def __init__(self, w1h, w1l, w2h, w2l):
        self.w1h, self.w1l, self.w2h, self.w2l = w1h, w1l, w2h, w2l


class Chain:

    def __init__(self, eng, sem, n=0):
        self.eng, self.sem, self.n = eng, sem, n

    def __call__(self, ins):
        self.n = self.n + 1
        ins.then_inc(self.sem, 1)
        self.eng.wait_ge(self.sem, self.n)


def by_pairs(eng, lo, hi, body):
    pairs = (hi - lo) // 2
    if pairs:
        with eng.Fori(0, pairs) as m:
            body(m * 2 + lo, lo % 2)
            body(m * 2 + (lo + 1), (lo + 1) % 2)
    if (hi - lo) % 2:
        body(hi - 1, (hi - 1) % 2)


def by_turns(eng, body):
    assert UNROLL % RING == 0 and (ITEMS - BACK) % UNROLL == 0
    with eng.Fori(1, (ITEMS - BACK) // UNROLL) as m:
        body(m * UNROLL)


def field(nc, eng, word, at, top):
    return within(nc, eng, (word >> at) & ((1 << top.bit_length()) - 1), top)


def within(nc, eng, value, top):
    return nc.s_assert_within(eng.snap(value), min_val=0, max_val=top,
                              skip_runtime_bounds_check_because="the words hold blocks and groups in range")


def cols(v):
    return v.rearrange("(k p) -> p k", p=P)


def after(eng, sem, n):
    if not (isinstance(n, int) and n <= 0):
        eng.wait_ge(sem, n)


def row_on_all(v):
    return v.rearrange("(a d) -> a d", a=1).to_broadcast([P, v.shape[0]])


def setup_and_nodes(nc, k, a):
    with ExitStack() as own, nc.Block() as block:
        def sb(name, shape, dt=F32):
            return own.enter_context(nc.sbuf_tensor(name, shape, dt))

        def ps(name, shape):
            return own.enter_context(nc.psum_tensor(name, shape, F32))

        def sem(name):
            return own.enter_context(nc.semaphore(name))

        w_hr = sb("w_hr", [P, KT, 2 * D])
        w_qkv = sb("w_qkv", [P, KT, 3 * MC])
        wout = sb("wout", [P, D])
        gbias = sb("gbias", [P, D])
        att = sb("att", [P, 2, D])
        g1c = sb("g1c", [P, 3, KT])
        edge_i = sb("edge_i", [P, 2, EG], I32)
        edge_f = sb("edge_f", [P, 2, EG])
        below = sb("below", [P, TILES])
        edge0 = sb("edge0", [P, GROUPS])
        small = sb("small", [P, P])
        start_g = sb("start_g", [P, 1])
        start_b = sb("start_b", [P, 1])
        cnt_sb = sb("cnt_sb", [P, TILES + 1])
        step_b = sb("step_b", [P, P])
        mask_g = sb("mask_g", [P, 1])
        need_f = sb("need_f", [1, NEED])
        need_i = sb("need_i", [1, NEED], I32)
        weight = sb("weight", [P, FIELDS])
        zero_row = sb("zero_row", [P, D])
        s_zeroed = sem("s_zeroed")
        stats = sb("stats", [P, TILES, 6])
        st_a = sb("st_a", [P, TILES])
        st_b = sb("st_b", [P, TILES])
        st_v = sb("st_v", [P, TILES])
        mean = sb("mean", [P, TILES])
        rstd = sb("rstd", [P, TILES])
        rms = sb("rms", [P, TILES])
        an = sb("an", [P, 2, D])
        bn = sb("bn", [P, 2, D])
        an_t = sb("an_t", [P, 2, KT, P])
        bn_t = sb("bn_t", [P, 2, KT, P])
        prod = sb("prod", [P, 2, D])
        keys = sb("keys", [P, NP])
        vals = sb("vals", [P, TILES, MC + 1])
        gmax = sb("gmax", [P, 2, GH])
        zself = sb("zself", [P, TILES, GH])
        zself2 = sb("zself2", [P, TILES, GH])
        kmax = sb("kmax", [P, 2])
        kexp = sb("kexp", [P, 2, P])
        kexp_t = sb("kexp_t", [P, 2, P])
        head_mask = sb("head_mask", [P, P])
        ctx_n = sb("ctx_n", [P, P])
        ctx_t = sb("ctx_t", [P, P])
        rz = sb("rz", [P, 1])
        qmax = sb("qmax", [P, TILES * MH])
        qsum = sb("qsum", [P, TILES * MH])
        ps_a = [ps(f"ps_a{i}", [P, KT, P]) for i in range(2)]
        ps_b = [ps(f"ps_b{i}", [P, KT, P]) for i in range(2)]
        ps_hr = [ps(f"ps_hr{i}", [P, 2 * D]) for i in range(2)]
        ps_qkv = [ps(f"ps_qkv{i}", [P, 3 * MC]) for i in range(2)]

        s_x, s_w, s_row, s_edge, s_tab = (sem(n) for n in ("s_x", "s_w", "s_row", "s_edge", "s_tab"))
        s_clear, s_iota, s_dstf, s_memkv = (sem(n) for n in ("s_clear", "s_iota", "s_dstf", "s_memkv"))
        s_edge_f, s_edge_t, s_edge_out, s_below, s_cnt, s_steps, s_items = (
            sem(n) for n in ("s_edge_f", "s_edge_t", "s_edge_out", "s_below", "s_cnt", "s_steps", "s_items"))
        s_dve, s_scale, s_an, s_bn, s_ta, s_tb, s_at, s_bt, s_hr, s_qkv, s_hr_out, s_qkv_out = (
            sem(n) for n in ("s_dve", "s_scale", "s_an", "s_bn", "s_ta", "s_tb", "s_at", "s_bt", "s_hr", "s_qkv",
                             "s_hr_out", "s_qkv_out"))
        s_nodes, s_gmax, s_gall, s_zself, s_wself, s_kmax, s_kexp, s_kt, s_kt_out, s_ctx = (
            sem(n) for n in ("s_nodes", "s_gmax", "s_gall", "s_zself", "s_wself", "s_kmax", "s_kexp", "s_kt",
                             "s_kt_out", "s_ctx"))
        s_var, s_root = sem("s_var"), sem("s_root")
        s_ctx_n, s_ctx_t, s_ctx_to, s_cw, s_q0, s_q1, s_act = (
            sem(n) for n in ("s_ctx_n", "s_ctx_t", "s_ctx_to", "s_cw", "s_q0", "s_q1", "s_act"))

        @block.sync
        def _(sp):
            sp.wait_ge(s_clear, 2)
            for n, v in enumerate((a.src, a.dst)):
                sp.dma_start(edge_i[0:GFULL, n, :], v[0:GFULL * EG].rearrange("(g e) -> g e", e=EG)).then_inc(s_edge, 16)
                sp.dma_start(edge_i[GFULL:GROUPS, n, 0:GREST],
                             v[GFULL * EG:E].rearrange("(g e) -> g e", g=1)).then_inc(s_edge, 16)
            sp.wait_ge(s_clear, 3)
            sp.dma_start(k.acc[:, 0:FULL, :], a.x[0:FULL * P, :].rearrange("(t p) d -> p t d", p=P)).then_inc(s_x, 16)
            sp.dma_start(k.acc[0:REST, FULL, :], a.x[FULL * P:N, :]).then_inc(s_x, 16)
            sp.dma_start(w_hr[:, :, 0:D], a.g_W.rearrange("(k p) n -> p k n", p=P)).then_inc(s_w, 16)
            sp.dma_start(w_hr[:, :, D:2 * D], a.g_Wres.rearrange("(k p) n -> p k n", p=P)).then_inc(s_w, 16)
            sp.dma_start(w_qkv[:], a.m_qkv.rearrange("(k p) n -> p k n", p=P)).then_inc(s_w, 16)
            sp.dma_start(wout[:], a.m_wout).then_inc(s_w, 16)
            for n, v in enumerate((a.ln1_g, a.ln1_b, a.m_gpre)):
                sp.dma_start(g1c[:, n, :], cols(v)).then_inc(s_row, 16)
            sp.dma_start(gbias[:], row_on_all(a.g_bias)).then_inc(s_row, 16)
            for n, v in enumerate((a.g_as, a.g_ad)):
                sp.dma_start(att[:, n, :], row_on_all(v.rearrange("h d -> (h d)"))).then_inc(s_row, 16)
            for to, v in ((k.bout, a.m_bout), (k.gout, a.m_gout), (k.g2, a.ln2_g), (k.b2n, a.ln2_b), (k.fb2, a.f_b2)):
                sp.dma_start(to[:], row_on_all(v)).then_inc(s_row, 16)
            sp.wait_ge(s_iota, 8)
            sp.dma_start(k.rows_in.rearrange("(t p) d -> p t d", p=P),
                         zero_row[:].unsqueeze(1).to_broadcast([P, MOE_STEPS * WIDE, D])).then_inc(s_zeroed, 16)
            sp.wait_ge(s_edge_f, 1)
            sp.dma_start(k.dst_f, edge_f[0:GROUPS, 1, :]).then_inc(s_dstf, 16)
            sp.wait_ge(s_qkv_out, TILES)
            sp.dma_start(keys[:, N:N + MEM], a.m_mem[0].rearrange("h d m -> (h d) m")).then_inc(s_memkv, 16)
            sp.dma_start(vals[REST:REST + MEM, FULL, 0:MC], a.m_mem[1].rearrange("h d m -> m (h d)")).then_inc(s_memkv, 16)
            sp.wait_ge(s_nodes, 1)
            sp.dma_start(k.table.rearrange("(t p) r -> p t r", p=P), k.agg[:]).then_inc(s_tab, 16)
            sp.wait_ge(s_tab, 16)
            sp.wait_ge(s_dstf, 16)
            sp.wait_ge(s_zeroed, 16)

        @block.gpsimd
        def _(pool):
            nc.gpsimd.memset(edge_i[:, 0, :], 0).then_inc(s_clear, 1)
            nc.gpsimd.memset(edge_i[:, 1, :], NP + P).then_inc(s_clear, 1)
            nc.gpsimd.memset(k.acc[:, FULL, :], 0.0).then_inc(s_clear, 1)
            nc.gpsimd.iota(k.pidx[:], pattern=[[0, 1]], base=0, channel_multiplier=1,
                           allow_small_or_imprecise_dtypes=True).then_inc(s_iota, 1)
            nc.gpsimd.iota(k.iota_n[:], pattern=[[1, NP]], base=0, channel_multiplier=0,
                           allow_small_or_imprecise_dtypes=True).then_inc(s_iota, 1)
            nc.gpsimd.iota(k.node_id[:], pattern=[[P, TILES]], base=0, channel_multiplier=1,
                           allow_small_or_imprecise_dtypes=True).then_inc(s_iota, 1)
            nc.gpsimd.iota(edge0[:], pattern=[[EG, GROUPS]], base=0, channel_multiplier=0,
                           allow_small_or_imprecise_dtypes=True).then_inc(s_iota, 1)
            nc.gpsimd.iota(mask_g[:], pattern=[[0, 1]], base=0, channel_multiplier=EG,
                           allow_small_or_imprecise_dtypes=True).then_inc(s_iota, 1)
            nc.gpsimd.memset(vals[:, :, MC:MC + 1], 1.0).then_inc(s_iota, 1)
            nc.gpsimd.memset(need_f[:], 0.0).then_inc(s_iota, 1)
            nc.gpsimd.memset(zero_row[:], 0.0).then_inc(s_iota, 1)
            pool.wait_ge(s_gmax, 1)
            nc.gpsimd.partition_all_reduce(gmax[:, 1, :], gmax[:, 0, :], P, RMAX).then_inc(s_gall, 1)

        def layer_stats(dve, link, src, n):
            def one(t, _):
                nc.vector.bn_stats(stats[:, t, :], src[:, t, :])
            by_pairs(dve, 0, TILES - 1, one)
            link(nc.vector.bn_stats(stats[:, TILES - 1, :], src[:, TILES - 1, :]))
            link(nc.vector.tensor_tensor(st_a[:], stats[:, :, 1], stats[:, :, 4], ALU.subtract))
            link(nc.vector.tensor_tensor(st_a[:], st_a[:], st_a[:], ALU.mult))
            link(nc.vector.tensor_tensor(st_b[:], stats[:, :, 2], stats[:, :, 5], ALU.add))
            link(nc.vector.scalar_tensor_tensor(out=st_v[:], in0=st_a[:], scalar=D / 4.0, in1=st_b[:], op0=ALU.mult,
                                                op1=ALU.add))
            link(nc.vector.tensor_tensor(mean[:], stats[:, :, 1], stats[:, :, 4], ALU.add))
            link(nc.vector.tensor_scalar(mean[:], mean[:], 0.5, None, ALU.mult))
            nc.vector.tensor_scalar(rstd[:], st_v[:], 1.0 / D, EPS, ALU.mult, ALU.add).then_inc(s_var, 1)
            dve.wait_ge(s_root, n)
            link(nc.vector.reciprocal(st_a[:], rstd[:]))
            link(nc.vector.tensor_scalar(st_b[:], st_v[:], 1.0 / D, EPS, ALU.mult, ALU.add))
            link(nc.vector.tensor_tensor(st_b[:], st_b[:], st_a[:], ALU.mult))
            link(nc.vector.tensor_tensor(st_b[:], st_b[:], rstd[:], ALU.add))
            link(nc.vector.reciprocal(rstd[:], st_b[:]))
            link(nc.vector.tensor_scalar(rstd[:], rstd[:], 2.0, None, ALU.mult))

        @block.vector
        def _(dve):
            link = Chain(dve, s_dve)
            link(nc.vector.memset(k.ones[:], 1.0))
            link(nc.vector.memset(head_mask[:], 0.0))
            for h in range(MH):
                link(nc.vector.memset(head_mask[MHD * h:MHD * h + MHD, MHD * h:MHD * h + MHD], float(MHD) ** -0.5))
            dve.wait_ge(s_iota, 8)
            link(nc.vector.tensor_scalar(k.ident[:], k.iota_n[:, 0:P], k.pidx[:, 0:1], None, ALU.is_equal))
            dve.wait_ge(s_edge, 64)
            nc.vector.tensor_copy(edge_f[:], edge_i[:]).then_inc(s_edge_f, 1)
            dve.wait_ge(s_edge_f, 1)
            for b in range(TILES):
                link(nc.vector.tensor_scalar(an[0:GROUPS, :, :].rearrange("p a b -> p (a b)"), edge_f[0:GROUPS, 1, :],
                                             float(P * b), 0.0, ALU.is_lt, ALU.add,
                                             accum_out=below[0:GROUPS, b:b + 1]))
            nc.vector.tensor_copy(small[0:1, 0:1], below[0:1, 0:1]).then_inc(s_below, 1)
            dve.wait_ge(s_edge_t, 1)
            nc.vector.tensor_copy(k.src_i[:], ps_hr[0][:, 0:JG * GROUPS].rearrange("p (j g) -> p j g", j=JG)).then_inc(s_edge_out, 1)
            nc.vector.tensor_copy(k.dst_e[:], ps_hr[1][:, 0:JG * GROUPS].rearrange("p (j g) -> p j g", j=JG)).then_inc(s_edge_out, 1)
            dve.wait_ge(s_cnt, 1)
            link(nc.vector.tensor_copy(cnt_sb[:, 0:TILES], ps_a[0][:, 0, 0:TILES]))
            link(nc.vector.tensor_copy(cnt_sb[0:TILES, TILES:TILES + 1], ps_a[0][0:TILES, 1, 0:1]))
            link(nc.vector.tensor_scalar(small[:, 0:TILES - 1], cnt_sb[:, 1:TILES], mask_g[:, 0:1], 0.0, ALU.is_le,
                                         ALU.add, accum_out=start_g[:]))
            link(nc.vector.tensor_tensor(start_g[:], start_g[:], k.pidx[:], ALU.add))
            link(nc.vector.tensor_scalar(small[0:TILES, 0:GROUPS - 1], edge0[0:TILES, 1:GROUPS],
                                         cnt_sb[0:TILES, TILES:TILES + 1], 0.0, ALU.is_lt, ALU.add,
                                         accum_out=start_b[0:TILES, :]))
            link(nc.vector.tensor_tensor(start_b[0:TILES, :], start_b[0:TILES, :], k.pidx[0:TILES, :], ALU.add))
            link(nc.vector.tensor_scalar(step_b[0:TILES, :], k.iota_n[0:TILES, 0:P], start_b[0:TILES, 0:1], None, ALU.is_ge))
            link(nc.vector.tensor_scalar(weight[:, 0:1], k.pidx[:], 1.0, None, ALU.is_ge))
            for n in range(1, FIELDS):
                m = nc.vector.tensor_scalar(weight[:, n:n + 1], k.pidx[:], 1.0, float(1 << n * BLOCK_BITS), ALU.is_ge, ALU.mult)
            m.then_inc(s_steps, 1)
            dve.wait_ge(s_items, 1)
            link(nc.vector.tensor_copy(k.items[:], ps_a[1][0:1, 0, 0:WORDS]))
            link(nc.vector.tensor_copy(need_f[0:1, GRING:GROUPS], ps_b[1][0:1, 0, 0:GROUPS - GRING]))
            ni = need_i[0:1, :].rearrange("p (m s) -> p m s", s=NEED_PER)
            link(nc.vector.tensor_copy(need_i[:], need_f[:]))
            for n in range(1, NEED_PER):
                link(nc.vector.tensor_scalar(ni[:, :, n], ni[:, :, n], n * NEED_BITS, None, ALU.logical_shift_left))
                link(nc.vector.tensor_tensor(ni[:, :, 0], ni[:, :, 0], ni[:, :, n], ALU.bitwise_or))
            link(nc.vector.tensor_copy(k.need[:], ni[:, :, 0]))

            dve.wait_ge(s_x, 32)
            layer_stats(dve, link, k.acc, 1)

            def norm0(t, _):
                nc.vector.tensor_scalar(k.xn0[:, t, :], k.acc[:, t, :], mean[:, bass.ds(t, 1)], rstd[:, bass.ds(t, 1)],
                                        ALU.subtract, ALU.mult)
            by_pairs(dve, 0, TILES - 1, norm0)
            link(nc.vector.tensor_scalar(k.xn0[:, TILES - 1, :], k.acc[:, TILES - 1, :], mean[:, TILES - 1:TILES],
                                         rstd[:, TILES - 1:TILES], ALU.subtract, ALU.mult))
            layer_stats(dve, link, k.xn0, 2)
            link(nc.vector.tensor_tensor(st_b[:], mean[:], mean[:], ALU.mult))
            nc.vector.scalar_tensor_tensor(out=rms[:], in0=st_b[:], scalar=float(D), in1=st_v[:], op0=ALU.mult,
                                           op1=ALU.add).then_inc(s_var, 1)
            dve.wait_ge(s_root, 3)
            link(nc.vector.tensor_scalar(rms[:], rms[:], 1e-12, None, ALU.max))
            link(nc.vector.reciprocal(rms[:], rms[:]))
            nc.vector.tensor_scalar(rms[:], rms[:], float(D) ** 0.5, None, ALU.mult).then_inc(s_scale, 1)
            dve.wait_ge(s_row, 16 * 11)

            def an_of(i, par):
                after(dve, s_ta, i - 1)
                nc.vector.tensor_scalar(an[:, par, :], k.xn0[:, i, :], mean[:, bass.ds(i, 1)], rstd[:, bass.ds(i, 1)],
                                        ALU.subtract, ALU.mult).then_inc(s_an, 1)

            def node(i, par, ahead=True):
                dve.wait_ge(s_ta, i + 1)
                after(dve, s_hr, i - 1)
                for kt in range(KT):
                    m = nc.vector.tensor_scalar(an_t[:, par, kt, :], ps_a[par][:, kt, :], g1c[:, 0, kt:kt + 1],
                                                g1c[:, 1, kt:kt + 1], ALU.mult, ALU.add)
                m.then_inc(s_at, 1)
                if ahead:
                    an_of(i + 2, par)
                dve.wait_ge(s_hr, i + 1)
                nc.vector.tensor_tensor(k.res[:, i, :], ps_hr[par][:, D:2 * D], gbias[:], ALU.add)
                link(nc.vector.tensor_copy(k.agg[:, i, 0:D], ps_hr[par][:, 0:D]))
                nc.vector.tensor_copy(small[:, 0:1], small[:, 1:2]).then_inc(s_hr_out, 1)
                nc.vector.tensor_tensor(prod[:, 0, :], k.agg[:, i, 0:D], att[:, 0, :], ALU.mult)
                link(nc.vector.tensor_tensor(prod[:, 1, :], k.agg[:, i, 0:D], att[:, 1, :], ALU.mult))
                nc.vector.tensor_reduce(k.agg[:, i, D:ROW], prod[:, 0, :].rearrange("p (h d) -> p h d", h=GH), AX_X, ALU.add)
                link(nc.vector.tensor_reduce(k.node_am[:, i, 0:GH], prod[:, 1, :].rearrange("p (h d) -> p h d", h=GH),
                                             AX_X, ALU.add))

            an_of(0, 0)
            an_of(1, 1)
            node(0, 0)
            node(1, 1)
            base, per = link.n, 3

            def counted(i, par):
                link.n = (i - 2) * per + base
                node(i, par)
            by_pairs(dve, 2, TILES - 2, counted)
            link.n = base + per * (TILES - 4)
            node(TILES - 2, (TILES - 2) % 2, False)
            node(TILES - 1, (TILES - 1) % 2, False)
            nc.vector.tensor_copy(small[:, 0:1], small[:, 1:2]).then_inc(s_nodes, 1)
            nc.vector.tensor_reduce(gmax[:, 0, :], k.agg[:, :, D:ROW].rearrange("p t h -> p h t"), AX_X,
                                    ALU.max).then_inc(s_gmax, 1)
            dve.wait_ge(s_gall, 1)
            link(nc.vector.tensor_tensor(zself[:], k.node_am[:, :, 0:GH],
                                         gmax[:, 1:2, :].to_broadcast([P, TILES, GH]), ALU.add))
            link(nc.vector.scalar_tensor_tensor(out=k.node_am[:, :, GH:2 * GH], in0=zself[:], scalar=SLOPE,
                                                in1=zself[:], op0=ALU.mult, op1=ALU.max))
            link(nc.vector.tensor_tensor(zself2[:], k.node_am[:, :, 0:GH], k.agg[:, :, D:ROW], ALU.add))
            link(nc.vector.scalar_tensor_tensor(out=zself[:], in0=zself2[:], scalar=SLOPE, in1=zself2[:],
                                                op0=ALU.mult, op1=ALU.max))
            nc.vector.tensor_tensor(zself[:], zself[:], k.node_am[:, :, GH:2 * GH], ALU.subtract).then_inc(s_zself, 1)
            dve.wait_ge(s_memkv, 32)
            link(nc.vector.tensor_reduce(kmax[:, 0:1], keys[:, 0:N + MEM], AX_X, ALU.max))
            nc.vector.tensor_scalar(kmax[:, 1:2], kmax[:, 0:1], -1.0, None, ALU.mult).then_inc(s_kmax, 1)
            qv = k.q[:].rearrange("p t (h d) -> p (t h) d", h=MH)
            link(nc.vector.tensor_reduce(qmax[:], qv, AX_X, ALU.max))
            nc.vector.tensor_tensor(qv, qv, qmax[:].unsqueeze(2).to_broadcast([P, TILES * MH, MHD]),
                                    ALU.subtract).then_inc(s_q0, 1)

            def key_tile(i, par):
                dve.wait_ge(s_kt, i + 1)
                after(dve, s_ctx, i - 1)
                nc.vector.tensor_copy(kexp_t[:, par, :], ps_a[par][:, 0, :]).then_inc(s_kt_out, 1)
            key_tile(0, 0)
            key_tile(1, 1)
            by_pairs(dve, 2, TILES, key_tile)
            dve.wait_ge(s_tab, 16)
            dve.wait_ge(s_wself, 1)
            for t0, t1 in ((0, 13), (13, TILES)):
                hv = k.agg[:, t0:t1, 0:D].rearrange("p t (h d) -> p t h d", h=GH)
                link(nc.vector.tensor_tensor(hv, hv, zself2[:, t0:t1, :].unsqueeze(3).to_broadcast([P, t1 - t0, GH, GHD]),
                                             ALU.mult))
            link(nc.vector.tensor_copy(k.agg[:, :, D:ROW], zself2[:]))
            dve.wait_ge(s_ctx, TILES)
            link(nc.vector.reciprocal(rz[:], ps_hr[0][:, MC:MC + 1]))
            nc.vector.scalar_tensor_tensor(out=ctx_n[:], in0=ps_hr[0][:, 0:MC], scalar=rz[:, 0:1], in1=head_mask[:],
                                           op0=ALU.mult, op1=ALU.mult).then_inc(s_ctx_n, 1)
            dve.wait_ge(s_ctx_t, 1)
            nc.vector.tensor_copy(ctx_t[:], ps_a[0][:, 0, :]).then_inc(s_ctx_to, 1)
            dve.wait_ge(s_cw, 1)
            link(nc.vector.tensor_copy(k.cw[:], ps_hr[1][:, 0:D]))
            dve.wait_ge(s_q1, 1)
            link(nc.vector.tensor_reduce(qsum[:], qv, AX_X, ALU.add))
            link(nc.vector.reciprocal(qsum[:], qsum[:]))
            link(nc.vector.tensor_tensor(qv, qv, qsum[:].unsqueeze(2).to_broadcast([P, TILES * MH, MHD]), ALU.mult))

        @block.scalar
        def _(act):
            for n, v in enumerate((rstd, rstd, rms)):
                act.wait_ge(s_var, n + 1)
                nc.scalar.activation(v[:], v[:], ACT.Sqrt).then_inc(s_root, 1)
            act.wait_ge(s_scale, 1)
            act.wait_ge(s_row, 16 * 11)

            def bn_of(i, par):
                after(act, s_tb, i - 1)
                nc.scalar.activation(bn[:, par, :], k.xn0[:, i, :], ACT.Copy, scale=rms[:, bass.ds(i, 1)]).then_inc(s_bn, 1)

            def node(i, par, ahead=True):
                act.wait_ge(s_tb, i + 1)
                after(act, s_qkv, i - 1)
                for kt in range(KT):
                    m = nc.scalar.activation(bn_t[:, par, kt, :], ps_b[par][:, kt, :], ACT.Copy, scale=g1c[:, 2, kt:kt + 1])
                m.then_inc(s_bt, 1)
                if ahead:
                    bn_of(i + 2, par)
                act.wait_ge(s_qkv, i + 1)
                nc.scalar.copy(k.q[:, i, :], ps_qkv[par][:, 0:MC])
                nc.scalar.copy(vals[:, i, 0:MC], ps_qkv[par][:, MC:2 * MC])
                nc.scalar.copy(keys[:, bass.ds(i * P, P)], ps_qkv[par][:, 2 * MC:3 * MC]).then_inc(s_qkv_out, 1)

            bn_of(0, 0)
            bn_of(1, 1)
            node(0, 0)
            node(1, 1)
            by_pairs(act, 2, TILES - 2, node)
            node(TILES - 2, (TILES - 2) % 2, False)
            node(TILES - 1, (TILES - 1) % 2, False)
            act.wait_ge(s_zself, 1)
            nc.scalar.activation(zself2[:], zself[:], ACT.Exp).then_inc(s_wself, 1)
            act.wait_ge(s_kmax, 1)

            def key_exp(i, par):
                after(act, s_kt, i - 1)
                nc.scalar.activation(kexp[:, par, :], keys[:, bass.ds(i * P, P)], ACT.Exp, bias=kmax[:, 1:2]).then_inc(s_kexp, 1)
            key_exp(0, 0)
            key_exp(1, 1)
            by_pairs(act, 2, TILES - 1, key_exp)
            par = (TILES - 1) % 2
            act.wait_ge(s_kt, TILES - 2)
            nc.scalar.activation(kexp[:, par, 0:REST + MEM], keys[:, N - REST:N + MEM], ACT.Exp, bias=kmax[:, 1:2])
            nc.scalar.activation(kexp[:, par, REST + MEM:P], k.ones[:, REST + MEM:P], ACT.Copy, scale=0.0).then_inc(s_kexp, 1)
            act.wait_ge(s_q0, 1)
            qf = k.q[:].rearrange("p t c -> p (t c)")
            nc.scalar.activation(qf, qf, ACT.Exp).then_inc(s_q1, 1)

        @block.tensor
        def _(pe):
            pe.wait_ge(s_edge_f, 1)
            pe.wait_ge(s_below, 1)
            for n in range(2):
                for j in range(JG):
                    m = nc.tensor.transpose(ps_hr[n][:, j * GROUPS:(j + 1) * GROUPS],
                                            edge_f[0:GROUPS, n, j * P:(j + 1) * P], k.ident[0:GROUPS, 0:GROUPS])
            m.then_inc(s_edge_t, 1)
            nc.tensor.matmul(ps_a[0][:, 0, 0:TILES], k.ones[0:GROUPS, :], below[0:GROUPS, :], start=True, stop=True)
            nc.tensor.matmul(ps_a[0][0:TILES, 1, 0:1], below[0:GROUPS, :], k.ones[0:GROUPS, 0:1], start=True,
                             stop=True).then_inc(s_cnt, 1)
            pe.wait_ge(s_steps, 1)
            word = ps_a[1][0:1, 0, :]
            for n in reversed(range(FIELDS)):
                gap = FIELDS - 1 - n
                nc.tensor.matmul(word[:, gap:WORDS], weight[0:TILES, n:n + 1], step_b[0:TILES, 0:WORDS - gap],
                                 start=(gap == 0), stop=(n == 0))
            nc.tensor.matmul(ps_b[1][0:1, 0, 0:GROUPS - GRING], start_g[:, 0:1], k.ident[:, 1:1 + GROUPS - GRING],
                             start=True, stop=True).then_inc(s_items, 1)
            pe.wait_ge(s_edge_out, 2)
            pe.wait_ge(s_scale, 1)
            pe.wait_ge(s_w, 64)

            def turn(i, par):
                pe.wait_ge(s_an, i + 1)
                after(pe, s_at, i - 1)
                for kt in range(KT):
                    m = nc.tensor.transpose(ps_a[par][:, kt, :], an[:, par, kt * P:(kt + 1) * P], k.ident[:])
                m.then_inc(s_ta, 1)
                pe.wait_ge(s_bn, i + 1)
                after(pe, s_bt, i - 1)
                for kt in range(KT):
                    m = nc.tensor.transpose(ps_b[par][:, kt, :], bn[:, par, kt * P:(kt + 1) * P], k.ident[:])
                m.then_inc(s_tb, 1)

            def products(i, par):
                pe.wait_ge(s_at, i + 1)
                after(pe, s_hr_out, i - 1)
                for kt in range(KT):
                    m = nc.tensor.matmul(ps_hr[par][:], an_t[:, par, kt, :], w_hr[:, kt, :], start=(kt == 0),
                                         stop=(kt == KT - 1))
                m.then_inc(s_hr, 1)
                pe.wait_ge(s_bt, i + 1)
                after(pe, s_qkv_out, i - 1)
                for kt in range(KT):
                    nc.tensor.matmul(ps_qkv[par][:, 0:MC], bn_t[:, par, kt, :], w_qkv[:, kt, 0:MC], start=(kt == 0),
                                     stop=(kt == KT - 1))
                for kt in range(KT):
                    nc.tensor.matmul(ps_qkv[par][:, MC:2 * MC], bn_t[:, par, kt, :], w_qkv[:, kt, 2 * MC:3 * MC],
                                     start=(kt == 0), stop=(kt == KT - 1))
                for kt in range(KT):
                    m = nc.tensor.matmul(ps_qkv[par][:, 2 * MC:3 * MC], w_qkv[:, kt, MC:2 * MC], bn_t[:, par, kt, :],
                                         start=(kt == 0), stop=(kt == KT - 1))
                m.then_inc(s_qkv, 1)

            def node(i, par):
                turn(i + 1, 1 - par)
                products(i, par)

            turn(0, 0)
            node(0, 0)
            node(1, 1)
            by_pairs(pe, 2, TILES - 1, node)
            products(TILES - 1, (TILES - 1) % 2)
            pe.wait_ge(s_hr_out, TILES)
            pe.wait_ge(s_at, TILES)
            pe.wait_ge(s_memkv, 32)

            def key_turn(i, par):
                pe.wait_ge(s_kexp, i + 1)
                after(pe, s_kt_out, i - 1)
                nc.tensor.transpose(ps_a[par][:, 0, :], kexp[:, par, :], k.ident[:]).then_inc(s_kt, 1)

            def context(i, par, first=False, last=False):
                pe.wait_ge(s_kt_out, i + 1)
                nc.tensor.matmul(ps_hr[0][:, 0:MC + 1], kexp_t[:, par, :], vals[:, i, :], start=first,
                                 stop=last).then_inc(s_ctx, 1)
            key_turn(0, 0)
            key_turn(1, 1)
            context(0, 0, first=True)

            def both(i, par):
                key_turn(i + 1, 1 - par)
                context(i, par)
            by_pairs(pe, 1, TILES - 1, both)
            context(TILES - 1, (TILES - 1) % 2, last=True)
            pe.wait_ge(s_ctx_n, 1)
            nc.tensor.transpose(ps_a[0][:, 0, :], ctx_n[:], k.ident[:]).then_inc(s_ctx_t, 1)
            pe.wait_ge(s_ctx_to, 1)
            nc.tensor.matmul(ps_hr[1][:, 0:D], ctx_t[:], wout[:], start=True, stop=True).then_inc(s_cw, 1)


def graph_items(nc, k, a):
    with ExitStack() as own, nc.Block() as block:
        def sb(name, shape, dt=F32):
            return own.enter_context(nc.sbuf_tensor(name, shape, dt))

        def sem(name):
            return own.enter_context(nc.semaphore(name))

        rows = sb("rows", [P, GRING, JG, ROW])
        index = sb("index", [P, GRING, JG], I32)
        dst_all = sb("dst_all", [P, GRING, EG])
        sel = sb("sel", [P, RING, JG, P])
        sel_t = sb("sel_t", [P, RING, EG])
        wx = sb("wx", [P, RING, JG, ROW])
        z = sb("z", [P, RING, 4, JG, GH])
        ps_am = [own.enter_context(nc.psum_tensor(f"ps_am{i}", [P, JG, 2 * GH], F32)) for i in range(RING)]
        ps_sum = [own.enter_context(nc.psum_tensor(f"ps_sum{i}", [P, ROW], F32)) for i in range(RING)]

        s_row = [sem(f"s_row{i}") for i in range(GRING)]
        s_dst = [sem(f"s_dst{i}") for i in range(GRING)]
        s_turn = {"pool": sem("s_turn_pool"), "sp": sem("s_turn_sp"), "index": sem("s_turn_index")}
        s_index, s_rows_in, s_dst_in = sem("s_index"), sem("s_rows_in"), sem("s_dst_in")
        s_sel, s_sel_t, s_abs, s_am, s_link, s_z, s_w, s_wx, s_sum, s_add = (
            sem(n) for n in ("s_sel", "s_sel_t", "s_abs", "s_am", "s_link", "s_z", "s_w", "s_wx", "s_sum", "s_add"))

        def groups(eng, name, issue, landed):
            def turn(m, slots):
                for slot in range(slots):
                    n = slot % NEED_PER
                    if n == 0:
                        word = eng.value_load(k.need[0:1, bass.ds(m * (GRING // NEED_PER) + slot // NEED_PER, 1)], min_val=0,
                                              max_val=(1 << NEED_BITS * NEED_PER) - 1)
                    eng.wait_ge(s_wx, (word >> (NEED_BITS * n)) & ((1 << NEED_BITS) - 1))
                    eng.sem_inc(s_turn[name], 1)
                    issue(m * GRING + slot, slot)
                    landed((slot - 1) % GRING, m - (slot == 0))
            for slot in range(GRING):
                issue(slot, slot)
                if slot:
                    landed(slot - 1, 0)
            with eng.Fori(0, GROUPS // GRING - 1) as m:
                turn(m + 1, GRING)
            turn(GROUPS // GRING, GROUPS % GRING)
            landed((GROUPS - 1) % GRING, (GROUPS - 1) // GRING)

        @block.gpsimd
        def _(pool):
            def gather(g, slot):
                nc.gpsimd.tensor_copy(index[:, slot, :], k.src_i[:, :, g]).then_inc(s_index, 1)
                pool.wait_ge(s_index, g + 1)
                pool.sem_inc(s_turn["index"], 1)
                for j in range(JG):
                    nc.gpsimd.indirect_dma_start(rows[:, slot, j, :], None, k.table, bass.IndirectOffsetOnAxis(
                        ap=index[:, slot, j:j + 1], axis=0)).then_inc(s_row[slot], 16)
            groups(pool, "pool", gather, lambda slot, turn: None)

        @block.sync
        def _(sp):
            def spread(g, slot):
                sp.dma_start(dst_all[:, slot, :], k.dst_f[bass.ds(g, 1), :].to_broadcast([P, EG])).then_inc(s_dst[slot], 16)

            def landed(slot, turn):
                sp.wait_ge(s_dst[slot], (turn + 1) * 16)
                sp.sem_inc(s_dst_in, 1)
                sp.wait_ge(s_row[slot], (turn + 1) * (16 * JG))
                sp.sem_inc(s_rows_in, 1)
            groups(sp, "sp", spread, landed)

        def blocks(eng, i, lo):
            words, found = {}, {}

            def block(n):
                at = (n - lo) // FIELDS
                if at not in words:
                    words[at] = eng.value_load(k.items[0:1, bass.ds(i + (lo + at * FIELDS + BACK + 1), 1)], min_val=0,
                                               max_val=(1 << BLOCK_BITS * FIELDS) - 1)
                if n not in found:
                    found[n] = field(nc, eng, words[at], BLOCK_BITS * ((n - lo) % FIELDS), TILES - 1)
                return found[n]
            return block

        def group(eng, i, b):
            return within(nc, eng, (i - b) & ((1 << GROUPS.bit_length()) - 1), GROUPS - 1)

        @block.vector
        def _(dve):
            def select_t(i, s, g, slot, b):
                dve.wait_ge(s_dst_in, g + 1)
                after(dve, s_am, i - 2)
                nc.vector.tensor_scalar(sel_t[:, s, :], dst_all[:, slot, :], k.node_id[:, bass.ds(b, 1)], None,
                                        ALU.is_equal).then_inc(s_sel_t, 1)

            def weigh(i, s, slot):
                dve.wait_ge(s_w, i + 1)
                nc.vector.tensor_tensor(
                    wx[:, s, :, 0:D].rearrange("p j (h d) -> p j h d", h=GH),
                    rows[:, slot, :, 0:D].rearrange("p j (h d) -> p j h d", h=GH),
                    wx[:, s, :, D:ROW].unsqueeze(3).to_broadcast([P, JG, GH, GHD]), ALU.mult).then_inc(s_wx, 1)

            def add(i, s, b):
                dve.wait_ge(s_sum, i + 1)
                after(dve, s_add, i)
                nc.vector.tensor_tensor(k.agg[:, b, :], k.agg[:, b, :], ps_sum[s][:], ALU.add).then_inc(s_add, 1)

            def step(i, s, b, back=BACK, ahead=True):
                g = group(dve, i, b(0))
                zz = z[:, s]
                dve.wait_ge(s_rows_in, g + 1)
                dve.wait_ge(s_am, i + 1)
                nc.vector.tensor_tensor(zz[:, 0], rows[:, g & (GRING - 1), :, D:ROW], ps_am[s][:, :, 0:GH],
                                        ALU.add).then_inc(s_link, 1)
                dve.wait_ge(s_link, i * 3 + 1)
                nc.vector.scalar_tensor_tensor(out=zz[:, 1], in0=zz[:, 0], scalar=SLOPE, in1=zz[:, 0], op0=ALU.mult,
                                               op1=ALU.max).then_inc(s_link, 1)
                dve.wait_ge(s_link, i * 3 + 2)
                nc.vector.tensor_tensor(zz[:, 2], zz[:, 1], ps_am[s][:, :, GH:2 * GH], ALU.subtract).then_inc(s_link, 1)
                dve.wait_ge(s_link, i * 3 + 3)
                nc.vector.tensor_scalar(zz[:, 3], zz[:, 2], 0.0, None, ALU.min).then_inc(s_z, 1)
                if back:
                    weigh(i - 1, (s - 1) % RING, group(dve, i - 1, b(-1)) & (GRING - 1))
                if back == BACK:
                    add(i - 2, (s - 2) % RING, b(-2))
                if ahead:
                    g = group(dve, i + 2, b(2))
                    select_t(i + 2, (s + 2) % RING, g, g & (GRING - 1), b(2))

            def turn(m):
                b = blocks(dve, m, -BACK)
                for n in range(UNROLL):
                    step(m + n, n % RING, lambda at: b(n + at))
            b = blocks(dve, 0, -1)
            select_t(0, 0, 0, 0, 0)
            g = group(dve, 1, b(1))
            select_t(1, 1, g, g & (GRING - 1), b(1))
            for i in range(UNROLL):
                step(i, i % RING, lambda at: b(i + at), back=min(i, BACK))
            by_turns(dve, turn)
            end = ITEMS - BACK
            b = blocks(dve, end, -BACK)
            for n in range(BACK):
                step(end + n, n, lambda at: b(n + at), ahead=False)
            weigh(end + 1, 1, group(dve, end + 1, b(1)) & (GRING - 1))
            add(end, 0, b(0))
            add(end + 1, 1, TILES - 1)

        @block.scalar
        def _(act):
            def select(i, s, g, b):
                after(act, s_sum, i - 2)
                for j in range(JG):
                    m = nc.scalar.activation(sel[:, s, j, :], k.iota_n[:, bass.ds(b * P, P)], ACT.Abs, scale=-1.0,
                                             bias=k.dst_e[:, j, bass.ds(g, 1)])
                m.then_inc(s_abs, 1)
                act.wait_ge(s_abs, i + 1)
                nc.scalar.activation(sel[:, s], sel[:, s], ACT.Relu, scale=-1.0, bias=k.ones[:, 0:1]).then_inc(s_sel, 1)

            def weights(i, s):
                act.wait_ge(s_z, i + 1)
                nc.scalar.activation(wx[:, s, :, D:ROW], z[:, s, 3], ACT.Exp).then_inc(s_w, 1)

            def step(i, s, b):
                weights(i, s)
                select(i + 2, (s + 2) % RING, group(act, i + 2, b(2)), b(2))

            def turn(m):
                b = blocks(act, m, BACK)
                for n in range(UNROLL):
                    step(m + n, n % RING, lambda at: b(n + at))
            b = blocks(act, 0, 1)
            select(0, 0, 0, 0)
            select(1, 1, group(act, 1, b(1)), b(1))
            for i in range(UNROLL):
                step(i, i % RING, lambda at: b(i + at))
            by_turns(act, turn)
            for i in range(ITEMS - BACK, ITEMS):
                weights(i, i % RING)

        @block.tensor
        def _(pe):
            def shares(i, s, b):
                pe.wait_ge(s_sel_t, i + 1)
                after(pe, s_z, i - 2)
                for j in range(JG):
                    m = nc.tensor.matmul(ps_am[s][:, j, :], sel_t[:, s, j * P:(j + 1) * P], k.node_am[:, b, :], start=True,
                                         stop=True)
                m.then_inc(s_am, 1)

            def sums(i, s):
                pe.wait_ge(s_wx, i + 1)
                pe.wait_ge(s_sel, i + 1)
                after(pe, s_add, i - 2)
                for j in range(JG):
                    m = nc.tensor.matmul(ps_sum[s][:], sel[:, s, j, :], wx[:, s, j, :], start=(j == 0), stop=(j == JG - 1))
                m.then_inc(s_sum, 1)

            def step(i, s, b):
                sums(i - 1, (s - 1) % RING)
                shares(i + 2, (s + 2) % RING, b(2))

            def turn(m):
                b = blocks(pe, m, BACK)
                for n in range(UNROLL):
                    step(m + n, n % RING, lambda at: b(n + at))
            b = blocks(pe, 0, 1)
            shares(0, 0, 0)
            shares(1, 1, b(1))
            shares(2, 2, b(2))
            for i in range(1, UNROLL):
                step(i, i % RING, lambda at: b(i + at))
            by_turns(pe, turn)
            for i in range(ITEMS - BACK - 1, ITEMS):
                sums(i, i % RING)


def feed_forward(nc, sb, ps, sem, n, width, name, gelu, weights, b1, xin, s_xin, gain, words=None):
    f = Names()
    cols_ = width * P
    half = HB // 2
    xe = sb(name + "_xe", [P, KT, cols_])
    xh, xl = (sb(name + v, [P, 2, KT, cols_], BF16) for v in ("_xh", "_xl"))
    hf = sb(name + "_hf", [P, 2, half, cols_])
    hh, hl = (sb(name + v, [P, 2, HB, cols_], BF16) for v in ("_hh", "_hl"))
    ps_x = ps(name + "_ps_x", [P, KT, cols_])
    f.ps_h = ps_h = [ps(f"{name}_ps_h{i}", [P, half, cols_]) for i in range(2)]
    f.ps_y = [ps(f"{name}_ps_y{i}", [P, width, D]) for i in range(2)]
    s_turned, s_gained, s_xhi, s_x, s_up, s_gelu, s_hhi, s_h = (
        sem(name + v) for v in ("_turned", "_gained", "_xhi", "_x", "_up", "_gelu", "_hhi", "_h"))
    f.s_down, f.s_y, f.s_turned = sem(name + "_down"), sem(name + "_y"), s_turned

    def word(eng, i):
        return None if words is None else words(eng, i)

    def turn(pe, i, par):
        pe.wait_ge(s_xin, i + 1)
        after(pe, s_x, i)
        for kt in range(KT):
            for w in range(width):
                m = nc.tensor.transpose(ps_x[:, kt, w * P:(w + 1) * P], xin[:, par, w, kt * P:(kt + 1) * P], f.ident)
        m.then_inc(s_turned, 1)

    def up(pe, i, par, w):
        pe.wait_ge(s_x, i + 1)
        for q in range(2):
            after(pe, s_gelu, i * 2 + (q - 1))
            for b in range(q * half, (q + 1) * half):
                steps = [(w.w1h, xh, kt) for kt in range(KT)] + [(w.w1h, xl, kt) for kt in range(KT)] + [
                    (w.w1l, xh, kt) for kt in range(KT)]
                for c, (w1, xx, kt) in enumerate(steps):
                    m = nc.tensor.matmul(ps_h[q][:, b - q * half, :], w1[:, kt, b, :], xx[:, par, kt, :], start=(c == 0),
                                         stop=(c == len(steps) - 1))
            m.then_inc(s_up, 1)

    def down(pe, i, par, w):
        after(pe, f.s_y, i - 1)
        pe.wait_ge(s_h, i * 2 + 2)
        steps = [(hx, w2, b) for b in range(HB) for hx, w2 in ((hh, w.w2h), (hh, w.w2l), (hl, w.w2h))]
        for v in range(width):
            for c, (hx, w2, b) in enumerate(steps):
                m = nc.tensor.matmul(f.ps_y[par][:, v, :], hx[:, par, b, v * P:(v + 1) * P], w2[:, b, :], start=(c == 0),
                                     stop=(c == len(steps) - 1))
        m.then_inc(f.s_down, 1)

    def pe_program(pe):
        def step(i, par):
            now, last = weights(pe, word(pe, i))
            turn(pe, i + 1, 1 - par)
            up(pe, i, par, now)
            down(pe, i - 1, 1 - par, last)
        turn(pe, 0, 0)
        turn(pe, 1, 1)
        up(pe, 0, 0, weights(pe, word(pe, 0))[0])
        for i in (1, 2):
            step(i, i % 2)
        by_pairs(pe, 3, n - 1, step)
        now, last = weights(pe, word(pe, n - 1))
        up(pe, n - 1, (n - 1) % 2, now)
        down(pe, n - 2, n % 2, last)
        down(pe, n - 1, (n - 1) % 2, now)

    def act_program(act):
        def step(i, par):
            bias = b1(act, word(act, i))
            for q in range(2):
                act.wait_ge(s_up, i * 2 + (1 + q))
                after(act, s_h, i * 2 + (q - 1))
                for b in range(half):
                    m = nc.scalar.activation(hf[:, q, b, :], ps_h[q][:, b, :], gelu, bias=bias[:, q * half + b:q * half + b + 1])
                m.then_inc(s_gelu, 1)
                act.wait_ge(s_gelu, i * 2 + (1 + q))
                if q == 0:
                    after(act, f.s_down, i - 1)
                nc.scalar.copy(hh[:, par, q * half:(q + 1) * half], hf[:, q]).then_inc(s_hhi, 1)
        for i in range(3):
            step(i, i % 2)
        by_pairs(act, 3, n, step)

    def split_x(dve, i, par, w, which=NEXT):
        dve.wait_ge(s_turned, i + 1)
        after(dve, s_up, i * 2 - 2)
        from_ = ps_x
        if gain is not None:
            g, b = gain(dve, w, which)
            for kt in range(KT):
                m = nc.vector.tensor_scalar(xe[:, kt, :], ps_x[:, kt, :], g[:, kt:kt + 1], b[:, kt:kt + 1], ALU.mult, ALU.add)
            m.then_inc(s_gained, 1)
            dve.wait_ge(s_gained, i + 1)
            from_ = xe
        nc.vector.tensor_copy(xh[:, par], from_[:]).then_inc(s_xhi, 1)
        dve.wait_ge(s_xhi, i + 1)
        nc.vector.tensor_tensor(xl[:, par], from_[:], xh[:, par], ALU.subtract).then_inc(s_x, 1)

    def split_h(dve, i, par):
        for q in range(2):
            dve.wait_ge(s_hhi, i * 2 + (1 + q))
            nc.vector.tensor_tensor(hl[:, par, q * half:(q + 1) * half], hf[:, q], hh[:, par, q * half:(q + 1) * half],
                                    ALU.subtract).then_inc(s_h, 1)

    def dve_program(dve, before, leave):
        def step(i, par, ahead=True):
            w = word(dve, i)
            if ahead:
                before(i + 2, par)
            split_x(dve, i + 1, 1 - par, w)
            split_h(dve, i, par)
            leave(i - 1, 1 - par, w, LAST)
        before(0, 0)
        before(1, 1)
        w = word(dve, 0)
        split_x(dve, 0, 0, w, OWN)
        split_x(dve, 1, 1, w)
        before(2, 0)
        split_h(dve, 0, 0)
        for i in (1, 2):
            step(i, i % 2)
        by_pairs(dve, 3, n - 2, step)
        step(n - 2, n % 2, ahead=False)
        w = word(dve, n - 1)
        split_h(dve, n - 1, (n - 1) % 2)
        leave(n - 2, n % 2, w, LAST)
        leave(n - 1, (n - 1) % 2, w, OWN)

    f.pe, f.act, f.dve = pe_program, act_program, dve_program
    return f


def row_sums(nc, dve, link, t, src):
    if src is not None:
        def one(i, _):
            nc.vector.bn_stats(t.stats[:, i, :], src[:, i, 0:D])
        by_pairs(dve, 0, TILES - 1, one)
        link(nc.vector.bn_stats(t.stats[:, TILES - 1, :], src[:, TILES - 1, 0:D]))
    link(nc.vector.tensor_tensor(t.a[:], t.stats[:, :, 1], t.stats[:, :, 4], ALU.subtract))
    link(nc.vector.tensor_tensor(t.a[:], t.a[:], t.a[:], ALU.mult))
    link(nc.vector.tensor_tensor(t.b[:], t.stats[:, :, 2], t.stats[:, :, 5], ALU.add))
    link(nc.vector.scalar_tensor_tensor(out=t.sq[:], in0=t.a[:], scalar=D / 4.0, in1=t.b[:], op0=ALU.mult, op1=ALU.add))
    link(nc.vector.tensor_tensor(t.mean[:], t.stats[:, :, 1], t.stats[:, :, 4], ALU.add))
    link(nc.vector.tensor_scalar(t.mean[:], t.mean[:], 0.5, None, ALU.mult))


def row_stats(nc, dve, link, t, src, n):
    row_sums(nc, dve, link, t, src)
    link(nc.vector.tensor_scalar(t.var[:], t.sq[:], 1.0 / D, EPS, ALU.mult, ALU.add))
    nc.vector.tensor_copy(t.root[:], t.var[:]).then_inc(t.s_var, 1)
    dve.wait_ge(t.s_root, n)
    link(nc.vector.reciprocal(t.a[:], t.root[:]))
    link(nc.vector.tensor_tensor(t.a[:], t.a[:], t.var[:], ALU.mult))
    link(nc.vector.tensor_tensor(t.a[:], t.a[:], t.root[:], ALU.add))
    link(nc.vector.reciprocal(t.rstd[:], t.a[:]))
    link(nc.vector.tensor_scalar(t.rstd[:], t.rstd[:], 2.0, None, ALU.mult))


def roots(nc, act, t, first, count):
    for n in range(first, first + count):
        act.wait_ge(t.s_var, n)
        nc.scalar.activation(t.root[:], t.root[:], ACT.Sqrt).then_inc(t.s_root, 1)


def stat_tiles(sb, sem, name):
    t = Names()
    t.stats = sb(name + "_stats", [P, TILES, 6])
    t.s_var, t.s_root = sem(name + "_s_var"), sem(name + "_s_root")
    t.a, t.b, t.sq, t.var, t.root, t.mean, t.rstd, t.scale = (
        sb(name + "_" + v, [P, TILES]) for v in ("a", "b", "sq", "var", "root", "mean", "rstd", "scale"))
    return t


def nodes_finish(nc, k, a):
    with ExitStack() as own, nc.Block() as block:
        def sb(name, shape, dt=F32):
            return own.enter_context(nc.sbuf_tensor(name, shape, dt))

        def ps(name, shape):
            return own.enter_context(nc.psum_tensor(name, shape, F32))

        def sem(name):
            return own.enter_context(nc.semaphore(name))

        raw1 = sb("raw1", [P, KT, HID])
        raw2 = sb("raw2", [P, HB, D])
        w = Weights(sb("w1h", [P, KT, HB, P], BF16), sb("w1l", [P, KT, HB, P], BF16),
                    sb("w2h", [P, HB, D], BF16), sb("w2l", [P, HB, D], BF16))
        b1 = sb("fb1", [P, HB])
        t = stat_tiles(sb, sem, "fin")
        xin = sb("xin", [P, 2, 1, D])
        rden = sb("rden", [P, TILES, GH])
        squares = sb("squares", [P, 2, D])
        norm = sb("norm", [P, TILES])
        s_w, s_whi, s_split, s_link, s_xin, s_base, s_sum = (
            sem(n) for n in ("f_w", "f_whi", "f_split", "f_link", "f_xin", "f_base", "f_sum"))
        s_qcopy, s_qt, s_qt_out, s_mix, s_mix_out, s_norm, s_acc = (
            sem(n) for n in ("f_qcopy", "f_qt", "f_qt_out", "f_mix", "f_mix_out", "f_norm", "f_acc"))
        f = feed_forward(nc, sb, ps, sem, TILES, 1, "g", ACT.Gelu_apprx_tanh, lambda eng, _: (w, w), lambda eng, _: b1, xin, s_xin, None)
        f.ident = k.ident[:]
        ps_mix = f.ps_h
        qs, qt = xin, sb("qt", [P, 2, P])

        @block.sync
        def _(sp):
            sp.dma_start(raw1[:], a.f_w1.rearrange("(k p) h -> p k h", p=P)).then_inc(s_w, 16)
            sp.dma_start(raw2[:], a.f_w2.rearrange("(p b) d -> p b d", b=HB)).then_inc(s_w, 16)
            sp.dma_start(b1[:], a.f_b1.rearrange("(p b) -> p b", b=HB)).then_inc(s_w, 16)

        @block.gpsimd
        def _(pool):
            nc.gpsimd.tensor_tensor(k.acc[:], k.acc[:], k.xn0[:], ALU.add).then_inc(s_base, 1)
            pool.wait_ge(s_base, 1)
            nc.gpsimd.tensor_tensor(k.acc[:], k.acc[:], k.fb2[:].unsqueeze(1).to_broadcast([P, TILES, D]),
                                    ALU.add).then_inc(s_base, 1)

        @block.tensor
        def _(pe):
            def turn(i, par):
                pe.wait_ge(s_qcopy, i + 1)
                after(pe, s_qt_out, i - 1)
                nc.tensor.transpose(f.ps_y[par][:, 0, 0:P], qs[:, par, 0, 0:P], k.ident[:]).then_inc(s_qt, 1)

            def mix(i, par):
                pe.wait_ge(s_qt_out, i + 1)
                after(pe, s_mix_out, i - 1)
                out = ps_mix[par][:, 0:KT, :]
                nc.tensor.matmul(out, qt[:, par, :], k.cw[:], start=True, stop=False)
                nc.tensor.matmul(out, k.ones[0:1, :], k.bout[0:1, :], start=False, stop=True).then_inc(s_mix, 1)

            def step(i, par):
                turn(i + 1, 1 - par)
                mix(i, par)
            turn(0, 0)
            step(0, 0)
            step(1, 1)
            by_pairs(pe, 2, TILES - 1, step)
            mix(TILES - 1, (TILES - 1) % 2)
            pe.wait_ge(s_mix_out, TILES)
            pe.wait_ge(s_split, 4)
            f.pe(pe)

        @block.scalar
        def _(act):
            def step(i, par):
                after(act, s_qt, i - 1)
                nc.scalar.copy(qs[:, par, 0, 0:P], k.q[:, i, :]).then_inc(s_qcopy, 1)

            def out(i, par):
                act.wait_ge(s_qt, i + 1)
                after(act, s_mix, i - 1)
                nc.scalar.copy(qt[:, par, :], f.ps_y[par][:, 0, 0:P]).then_inc(s_qt_out, 1)

            def mixed(i, par):
                act.wait_ge(s_mix, i + 1)
                rows = ps_mix[par][:, 0:KT, :].rearrange("p a b -> p (a b)")
                nc.scalar.copy(k.xn0[:, i, :], rows)
                after(act, s_mix_out, i - 1)
                nc.scalar.activation(squares[:, par, :], rows, ACT.Square, accum_out=norm[:, bass.ds(i, 1)]).then_inc(s_mix_out, 1)

            def tile(i, par):
                step(i + 1, 1 - par)
                out(i, par)
                mixed(i - 1, 1 - par)
            step(0, 0)
            step(1, 1)
            out(0, 0)
            act.wait_ge(s_base, 1)
            half = TILES // 4 * 2 + 1
            tile(1, 1)
            tile(2, 0)
            by_pairs(act, 3, half, tile)
            roots(nc, act, t, 1, 1)
            act.wait_ge(s_w, 48)
            nc.scalar.copy(w.w1h[:], raw1[:].rearrange("p k (m b) -> p k b m", b=HB)).then_inc(s_whi, 1)
            nc.scalar.copy(w.w2h[:], raw2[:]).then_inc(s_whi, 1)
            by_pairs(act, half, TILES - 1, tile)
            out(TILES - 1, (TILES - 1) % 2)
            mixed(TILES - 2, TILES % 2)
            mixed(TILES - 1, (TILES - 1) % 2)
            act.wait_ge(s_mix_out, TILES)
            nc.scalar.activation(norm[:], norm[:], ACT.Sqrt).then_inc(s_norm, 1)
            f.act(act)

        @block.vector
        def _(dve):
            link = Chain(dve, s_link)
            link(nc.vector.reciprocal(rden[:], k.agg[:, :, D:ROW]))
            for t0, t1 in ((0, 13), (13, TILES)):
                hv = k.agg[:, t0:t1, 0:D].rearrange("p t (h d) -> p t h d", h=GH)
                link(nc.vector.tensor_tensor(hv, hv, rden[:, t0:t1, :].unsqueeze(3).to_broadcast([P, t1 - t0, GH, GHD]),
                                             ALU.mult))
            link(nc.vector.tensor_tensor(k.agg[:, :, 0:D], k.agg[:, :, 0:D], k.res[:], ALU.add))
            row_stats(nc, dve, link, t, k.agg, 1)

            def graph_norm(i, _):
                nc.vector.tensor_scalar(k.agg[:, i, 0:D], k.agg[:, i, 0:D], t.mean[:, bass.ds(i, 1)],
                                        t.rstd[:, bass.ds(i, 1)], ALU.subtract, ALU.mult)
            by_pairs(dve, 0, TILES - 1, graph_norm)
            i = TILES - 1
            link(nc.vector.tensor_scalar(k.agg[:, i, 0:D], k.agg[:, i, 0:D], t.mean[:, i:i + 1], t.rstd[:, i:i + 1],
                                         ALU.subtract, ALU.mult))
            dve.wait_ge(s_whi, 2)
            link(nc.vector.tensor_tensor(w.w1l[:], raw1[:].rearrange("p k (m b) -> p k b m", b=HB), w.w1h[:], ALU.subtract))
            nc.vector.tensor_tensor(w.w2l[:], raw2[:], w.w2h[:], ALU.subtract).then_inc(s_split, 4)

            dve.wait_ge(s_norm, 1)
            link(nc.vector.tensor_scalar(norm[:], norm[:], 1e-12, None, ALU.max))
            link(nc.vector.reciprocal(norm[:], norm[:]))
            link(nc.vector.tensor_scalar(norm[:], norm[:], float(D) ** 0.5, None, ALU.mult))
            dve.wait_ge(s_base, 2)
            dve.wait_ge(s_qt, TILES)

            base = link.n

            def before(i, par):
                link.n = i * 3 + base
                after(dve, f.s_turned, i - 1)
                link(nc.vector.tensor_tensor(k.agg[:, i, 0:D], k.agg[:, i, 0:D], k.g2[:], ALU.mult))
                nc.vector.tensor_tensor(xin[:, par, 0, :], k.agg[:, i, 0:D], k.b2n[:], ALU.add).then_inc(s_xin, 1)
                link(nc.vector.scalar_tensor_tensor(out=k.xn0[:, i, :], in0=k.xn0[:, i, :], scalar=norm[:, bass.ds(i, 1)],
                                                    in1=k.gout[:], op0=ALU.mult, op1=ALU.mult))
                link(nc.vector.tensor_tensor(k.acc[:, i, :], k.acc[:, i, :], k.xn0[:, i, :], ALU.add))
                dve.wait_ge(s_xin, i + 1)
                nc.vector.tensor_tensor(k.acc[:, i, :], k.acc[:, i, :], xin[:, par, 0, :], ALU.add).then_inc(s_acc, 1)

            def leave(i, par, *_):
                dve.wait_ge(f.s_down, i + 1)
                dve.wait_ge(s_acc, i + 1)
                nc.vector.tensor_tensor(k.acc[:, i, :], k.acc[:, i, :], f.ps_y[par][:, 0, :], ALU.add).then_inc(f.s_y, 1)
            f.dve(dve, before, leave)


def route(nc, k, a):
    with ExitStack() as own, nc.Block() as block:
        def sb(name, shape, dt=F32):
            return own.enter_context(nc.sbuf_tensor(name, shape, dt))

        def ps(name, shape):
            return own.enter_context(nc.psum_tensor(name, shape, F32))

        def sem(name):
            return own.enter_context(nc.semaphore(name))

        raw1 = [sb(f"r_raw1{i}", [P, KT, HID]) for i in range(2)]
        raw2 = [sb(f"r_raw2{i}", [P, HB, D]) for i in range(1)]
        wr = sb("wr", [P, KT, EXP])
        br = sb("br", [P, EXP])
        t = stat_tiles(sb, sem, "r1")
        t2 = stat_tiles(sb, sem, "r2")
        xt = sb("xt", [P, 2, D])
        xt_t = sb("xt_t", [P, 2, KT, P])
        xn = sb("xn", [P, 2, D])
        index = sb("r_index", [P, 2, TOPK], I32)
        logit, eq, enc, o1, o2, both, rank, total, incl = (
            sb("r_" + n, [P, TILES, EXP]) for n in ("logit", "eq", "enc", "o1", "o2", "both", "rank", "total", "incl"))
        best = sb("best", [P, 3, TILES])
        rev = sb("rev", [P, EXP])
        lower = sb("lower", [P, P])
        tile_no = sb("tile_no", [P, P])
        per_e = sb("per_e", [P, 6, EXP])
        per_ei = sb("per_ei", [P, EXP], I32)
        cmp = sb("cmp", [1, MOE_STEPS, EXP - 1])
        expert_f = sb("expert_f", [1, MOE_STEPS])
        word_f = sb("word_f", [1, MOE_STEPS])
        place_f = sb("place_f", [P, TILES, TOPK])
        zero = sb("zero", [P, TILES])
        ps_t = [ps(f"r_ps_t{i}", [P, KT, P]) for i in range(2)]
        ps_l = ps("r_ps_l", [P, TILES, EXP])
        ps_r = ps("r_ps_r", [P, TILES, EXP])
        ps_n = ps("r_ps_n", [P, TILES, EXP])

        s_small, s_iota, s_link, s_xt, s_turned, s_xt_t, s_logit, s_exp_in, s_exp, s_both, s_rank = (
            sem(n) for n in ("r_small", "r_iota", "r_link", "r_xt", "r_turned", "r_xt_t", "r_logit", "r_exp_in", "r_exp",
                             "r_both", "r_rank"))
        s_place, s_xn, s_idx, s_pool = sem("r_place"), sem("r_xn"), sem("r_idx"), sem("r_pool")
        s_put = [sem(f"r_put{i}") for i in range(2)]
        s_raw1 = [sem(f"r_s_raw1{i}") for i in range(2)]
        s_raw2 = sem("r_s_raw2")
        s_hi1, s_hi2, s_lo1, s_lo2 = (sem(n) for n in ("r_hi1", "r_hi2", "r_lo1", "r_lo2"))

        @block.sync
        def _(sp):
            sp.dma_start(wr[:], a.e_Wr.rearrange("(k p) e -> p k e", p=P)).then_inc(s_small, 16)
            sp.dma_start(br[:], row_on_all(a.e_br)).then_inc(s_small, 16)

            def load(e, par):
                after(sp, s_lo1, e - 1)
                sp.dma_start(raw1[par][:], a.e_W1[bass.ds(e, 1), :, :].rearrange("e (k p) h -> p (e k) h", p=P)).then_inc(
                    s_raw1[par], 16)
                after(sp, s_lo2, e)
                sp.dma_start(raw2[0][:], a.e_W2[bass.ds(e, 1), :, :].rearrange("e (p b) d -> p (e b) d", b=HB)).then_inc(
                    s_raw2, 16)
            load(0, 0)
            load(1, 1)
            by_pairs(sp, 2, EXP, load)

        @block.gpsimd
        def _(pool):
            nc.gpsimd.iota(tile_no[:], pattern=[[1, P]], base=0, channel_multiplier=0,
                           allow_small_or_imprecise_dtypes=True).then_inc(s_iota, 1)
            nc.gpsimd.iota(rev[:], pattern=[[-1, EXP]], base=EXP, channel_multiplier=0,
                           allow_small_or_imprecise_dtypes=True).then_inc(s_iota, 1)
            nc.gpsimd.memset(zero[:], 0.0).then_inc(s_iota, 1)
            pool.wait_ge(s_place, 1)

            def put(i, par):
                after(pool, s_put[par], i * 16 - 16 * par)
                pool.sem_inc(s_pool, 1)
                nc.gpsimd.tensor_copy(index[:, par, :], k.place_i[:, i, :]).then_inc(s_idx, 1)
                pool.wait_ge(s_idx, i + 1)
                pool.sem_inc(s_pool, 1)
                pool.wait_ge(s_xn, i + 1)
                pool.sem_inc(s_pool, 1)
                for c in range(TOPK):
                    nc.gpsimd.indirect_dma_start(k.rows_in, bass.IndirectOffsetOnAxis(ap=index[:, par, c:c + 1], axis=0),
                                                 xn[:, par, :], None).then_inc(s_put[par], 16)
            put(0, 0)
            put(1, 1)
            by_pairs(pool, 2, TILES, put)
            pool.wait_ge(s_put[0], 32 * (TILES - TILES // 2))
            pool.wait_ge(s_put[1], 32 * (TILES // 2))

        @block.scalar
        def _(act):
            roots(nc, act, t, 1, 1)

            def out(i, par):
                act.wait_ge(s_turned, i + 1)
                after(act, s_logit, i - 1)
                nc.scalar.copy(xt_t[:, par], ps_t[par][:]).then_inc(s_xt_t, 1)
            out(0, 0)
            out(1, 1)
            by_pairs(act, 2, TILES, out)
            roots(nc, act, t2, 1, 1)
            act.wait_ge(s_exp_in, 1)
            nc.scalar.activation(best[:, 2, :], best[:, 2, :], ACT.Exp).then_inc(s_exp, 1)

            def high(e, par):
                act.wait_ge(s_raw1[par], e * 8 + (16 - 8 * par))
                nc.scalar.copy(k.w1[:, e, 0], raw1[par][:].rearrange("p k (m b) -> p k b m", b=HB)).then_inc(s_hi1, 1)
                act.wait_ge(s_raw2, (e + 1) * 16)
                nc.scalar.copy(k.w2[:, e, 0], raw2[0][:]).then_inc(s_hi2, 1)
            by_pairs(act, 0, EXP, high)

        @block.tensor
        def _(pe):
            pe.wait_ge(s_small, 32)

            def turn(i, par):
                pe.wait_ge(s_xt, i + 1)
                after(pe, s_xt_t, i - 1)
                for kt in range(KT):
                    m = nc.tensor.transpose(ps_t[par][:, kt, :], xt[:, par, kt * P:(kt + 1) * P], k.ident[:])
                m.then_inc(s_turned, 1)

            def logits(i, par):
                pe.wait_ge(s_xt_t, i + 1)
                for kt in range(KT):
                    m = nc.tensor.matmul(ps_l[:, i, :], xt_t[:, par, kt, :], wr[:, kt, :], start=(kt == 0),
                                         stop=(kt == KT - 1))
                m.then_inc(s_logit, 1)

            def step(i, par):
                turn(i + 1, 1 - par)
                logits(i, par)
            turn(0, 0)
            step(0, 0)
            step(1, 1)
            by_pairs(pe, 2, TILES - 1, step)
            logits(TILES - 1, (TILES - 1) % 2)
            pe.wait_ge(s_both, 1)
            nc.tensor.matmul(ps_r[:], lower[:], both[:], start=True, stop=True)
            nc.tensor.matmul(ps_n[:], k.ones[:], both[:], start=True, stop=True).then_inc(s_rank, 1)

        @block.vector
        def _(dve):
            link = Chain(dve, s_link)
            row_stats(nc, dve, link, t, k.acc, 1)

            def normed(i, par, to):
                return nc.vector.tensor_scalar(to[:, par, :], k.acc[:, i, :], t.mean[:, bass.ds(i, 1)],
                                               t.rstd[:, bass.ds(i, 1)], ALU.subtract, ALU.mult)

            def tile(i, par):
                after(dve, s_turned, i - 1)
                normed(i, par, xt).then_inc(s_xt, 1)
                dve.wait_ge(s_xt, i + 1)
                nc.vector.bn_stats(t2.stats[:, i, :], xt[:, par, :])
            tile(0, 0)
            tile(1, 1)
            by_pairs(dve, 2, TILES, tile)
            dve.wait_ge(s_iota, 3)
            link(nc.vector.tensor_scalar(lower[:], tile_no[:], k.pidx[:, 0:1], None, ALU.is_gt))
            row_stats(nc, dve, link, t2, None, 1)

            def over_e(v):
                return v.unsqueeze(2).to_broadcast([P, TILES, EXP])

            def over_t(v):
                return v.unsqueeze(1).to_broadcast([P, TILES, EXP])
            dve.wait_ge(s_logit, TILES)
            dve.wait_ge(s_small, 32)
            link(nc.vector.tensor_tensor(logit[:], ps_l[:], over_t(br[:]), ALU.add))
            for c, o in enumerate((o1, o2)):
                link(nc.vector.tensor_reduce(best[:, c, :], logit[:], AX_X, ALU.max))
                link(nc.vector.tensor_tensor(eq[:], logit[:], over_e(best[:, c, :]), ALU.is_equal))
                link(nc.vector.tensor_tensor(enc[:], eq[:], over_t(rev[:]), ALU.mult))
                link(nc.vector.tensor_reduce(best[:, 2, :], enc[:], AX_X, ALU.max))
                link(nc.vector.tensor_tensor(o[:], enc[:], over_e(best[:, 2, :]), ALU.is_equal))
                if c == 0:
                    link(nc.vector.scalar_tensor_tensor(out=logit[:], in0=o[:], scalar=-BIG, in1=logit[:], op0=ALU.mult,
                                                        op1=ALU.add))
            nc.vector.tensor_tensor(both[:], o1[:], o2[:], ALU.add).then_inc(s_both, 1)
            nc.vector.tensor_tensor(best[:, 2, :], best[:, 1, :], best[:, 0, :], ALU.subtract).then_inc(s_exp_in, 1)
            dve.wait_ge(s_exp, 1)
            link(nc.vector.tensor_scalar(best[:, 0, :], best[:, 2, :], 1.0, None, ALU.add))
            link(nc.vector.reciprocal(k.share[:, :, 0], best[:, 0, :]))
            link(nc.vector.tensor_tensor(k.share[:, :, 1], k.share[:, :, 0], best[:, 2, :], ALU.mult))
            dve.wait_ge(s_rank, 1)
            link(nc.vector.tensor_copy(total[:], ps_n[:]))
            for e in range(EXP):
                m = nc.vector.tensor_tensor_scan(incl[:, :, e], total[:, :, e], zero[:], 0.0, ALU.add, ALU.add)
            link(m)
            link(nc.vector.tensor_tensor(rank[:], incl[:], total[:], ALU.subtract))
            link(nc.vector.tensor_tensor(rank[:], rank[:], ps_r[:], ALU.add))
            link(nc.vector.tensor_scalar(per_e[:, 0, :], incl[:, TILES - 1, :], float(MP - 1), None, ALU.add))
            link(nc.vector.tensor_copy(per_ei[:], per_e[:, 0, :]))
            link(nc.vector.tensor_scalar(per_ei[:], per_ei[:], MP.bit_length() - 1, None, ALU.arith_shift_right))
            link(nc.vector.tensor_copy(per_e[:, 1, :], per_ei[:]))
            link(nc.vector.tensor_tensor_scan(per_e[:, 2, :], per_e[:, 1, :], zero[:, 0:EXP], 0.0, ALU.add, ALU.add))
            link(nc.vector.tensor_tensor(per_e[:, 3, :], per_e[:, 2, :], per_e[:, 1, :], ALU.subtract))
            link(nc.vector.tensor_scalar(per_e[:, 4, :], per_e[:, 3, :], float(MP), None, ALU.mult))
            link(nc.vector.tensor_tensor(rank[:], rank[:], over_t(per_e[:, 4, :]), ALU.add))
            for c, o in enumerate((o1, o2)):
                link(nc.vector.tensor_tensor(enc[:], rank[:], o[:], ALU.mult))
                link(nc.vector.tensor_reduce(place_f[:, :, c], enc[:], AX_X, ALU.add))
            nc.vector.tensor_copy(k.place_i[:], place_f[:]).then_inc(s_place, 1)
            link(nc.vector.tensor_tensor(cmp[:], tile_no[0:1, 0:MOE_STEPS].unsqueeze(2).to_broadcast([1, MOE_STEPS, EXP - 1]),
                                         per_e[0:1, 3, 1:EXP].unsqueeze(1).to_broadcast([1, MOE_STEPS, EXP - 1]), ALU.is_ge))
            link(nc.vector.tensor_reduce(expert_f[:], cmp[:], AX_X, ALU.add))
            link(nc.vector.tensor_scalar(word_f[:], expert_f[:], float(1 << EXPERT_BITS), None, ALU.mult))
            link(nc.vector.tensor_tensor(word_f[:, 1:], word_f[:, 1:], expert_f[:, 0:MOE_STEPS - 1], ALU.add))
            link(nc.vector.scalar_tensor_tensor(out=word_f[:, 0:MOE_STEPS - 1], in0=expert_f[:, 1:],
                                                scalar=float(1 << 2 * EXPERT_BITS), in1=word_f[:, 0:MOE_STEPS - 1],
                                                op0=ALU.mult, op1=ALU.add))
            link(nc.vector.tensor_copy(k.step_word[:], word_f[:]))

            def row(i, par):
                after(dve, s_put[par], i * 16 - 16 * par)
                link(normed(i, par, xt))
                nc.vector.tensor_scalar(xn[:, par, :], xt[:, par, :], t2.mean[:, bass.ds(i, 1)], t2.rstd[:, bass.ds(i, 1)],
                                        ALU.subtract, ALU.mult).then_inc(s_xn, 1)
            dve.wait_ge(s_turned, TILES)
            base = link.n
            PER_EXPERT = TILES // EXP
            assert PER_EXPERT >= 2

            def counted(i, par):
                link.n = i + base
                row(i, par)

            def low(e, par):
                dve.wait_ge(s_hi1, e + 1)
                nc.vector.tensor_tensor(k.w1[:, e, 1], raw1[par][:].rearrange("p k (m b) -> p k b m", b=HB), k.w1[:, e, 0],
                                        ALU.subtract).then_inc(s_lo1, 1)
                dve.wait_ge(s_hi2, e + 1)
                nc.vector.tensor_tensor(k.w2[:, e, 1], raw2[0][:], k.w2[:, e, 0], ALU.subtract).then_inc(s_lo2, 1)

            def both_experts(pair, first=0):
                for n in range(first, 2 * PER_EXPERT):
                    counted(pair * (2 * PER_EXPERT) + n, n % 2)
                    if n % PER_EXPERT == PER_EXPERT - 1:
                        low(pair * 2 + n // PER_EXPERT, n // PER_EXPERT)
            counted(0, 0)
            counted(1, 1)
            both_experts(0, 2)
            with dve.Fori(1, EXP // 2) as pair:
                both_experts(pair)
            by_pairs(dve, EXP * PER_EXPERT, TILES, counted)
            link.n = base + TILES


def experts(nc, k, a):
    with ExitStack() as own, nc.Block() as block:
        def sb(name, shape, dt=F32):
            return own.enter_context(nc.sbuf_tensor(name, shape, dt))

        def ps(name, shape):
            return own.enter_context(nc.psum_tensor(name, shape, F32))

        def sem(name):
            return own.enter_context(nc.semaphore(name))

        ln_cols = sb("ln_cols", [P, EXP, 2, KT])
        b1 = sb("e_b1", [P, EXP, HB])
        b2 = sb("e_b2", [P, EXP, D])
        xin = sb("e_xin", [P, 2, WIDE, D])
        y = sb("e_y", [P, 2, WIDE, D])
        s_small, s_xin, s_pool = sem("e_small"), sem("e_xin_s"), sem("e_pool")
        s_load = [sem(f"e_load{i}") for i in range(2)]
        s_store = [sem(f"e_store{i}") for i in range(2)]

        def word(eng, i):
            return eng.value_load(k.step_word[0:1, bass.ds(i, 1)], min_val=0, max_val=(1 << 3 * EXPERT_BITS) - 1)

        def expert(eng, w, which):
            return field(nc, eng, w, which * EXPERT_BITS, EXP - 1)

        def weights(pe, w):
            both = (expert(pe, w, which) for which in (OWN, LAST))
            return tuple(Weights(k.w1[:, e, 0], k.w1[:, e, 1], k.w2[:, e, 0], k.w2[:, e, 1]) for e in both)

        def gain(dve, w, which):
            e = expert(dve, w, which)
            return ln_cols[:, e, 0, :], ln_cols[:, e, 1, :]

        f = feed_forward(nc, sb, ps, sem, MOE_STEPS, WIDE, "e", ACT.Gelu, weights, lambda act, w: b1[:, expert(act, w, OWN), :], xin,
                         s_xin, gain, word)
        f.ident = k.ident[:]

        @block.gpsimd
        def _(pool):
            def landed(i, par):
                pool.wait_ge(s_load[1 - par], i * 8 + 8 * par)
                pool.sem_inc(s_xin, 1)

            def load(i, par):
                after(pool, f.s_turned, i - 1)
                pool.sem_inc(s_pool, 1)
                pool.dma_start(xin[:, par], k.rows_in[bass.ds(i * MP, MP), :].rearrange("(p w) d -> p w d", w=WIDE)).then_inc(s_load[par], 16)
                if not (isinstance(i, int) and i == 0):
                    landed(i, par)
            load(0, 0)
            load(1, 1)
            by_pairs(pool, 2, MOE_STEPS, load)
            landed(MOE_STEPS, MOE_STEPS % 2)

        @block.sync
        def _(sp):
            for n, v in enumerate((a.e_lng, a.e_lnb)):
                for e in range(EXP):
                    sp.dma_start(ln_cols[:, e, n, :], cols(v[e])).then_inc(s_small, 16)
            sp.dma_start(b1[:], a.e_b1.rearrange("e (p b) -> p e b", b=HB)).then_inc(s_small, 16)
            sp.dma_start(b2[:], a.e_b2.rearrange("e d -> (e d)").rearrange("(a n) -> a n", a=1).to_broadcast([P, EXP * D])
                         ).then_inc(s_small, 16)

            def store(i, par):
                sp.wait_ge(f.s_y, i + 1)
                sp.dma_start(k.rows_out[bass.ds(i * MP, MP), :].rearrange("(p w) d -> p w d", w=WIDE), y[:, par]).then_inc(s_store[par], 16)
            by_pairs(sp, 0, MOE_STEPS, store)
            sp.wait_ge(s_store[0], 16 * (MOE_STEPS - MOE_STEPS // 2))
            sp.wait_ge(s_store[1], 16 * (MOE_STEPS // 2))

        @block.tensor
        def _(pe):
            f.pe(pe)

        @block.scalar
        def _(act):
            act.wait_ge(s_small, 16 * (2 * EXP + 2))
            f.act(act)

        @block.vector
        def _(dve):
            dve.wait_ge(s_small, 16 * (2 * EXP + 2))

            def leave(i, par, w, which):
                e = expert(dve, w, which)
                dve.wait_ge(f.s_down, i + 1)
                after(dve, s_store[par], i * 8 - 8 * par)
                nc.vector.tensor_tensor(y[:, par], f.ps_y[par][:], b2[:, e, :].unsqueeze(1).to_broadcast([P, WIDE, D]),
                                        ALU.add).then_inc(f.s_y, 1)
            f.dve(dve, lambda i, par: None, leave)


def combine(nc, k, a):
    with ExitStack() as own, nc.Block() as block:
        def sb(name, shape, dt=F32):
            return own.enter_context(nc.sbuf_tensor(name, shape, dt))

        def sem(name):
            return own.enter_context(nc.semaphore(name))

        got = sb("got", [P, 2, TOPK, D])
        index = sb("c_index", [P, 2, TOPK], I32)
        s_idx, s_got, s_sum, s_out, s_pool, s_first = (
            sem(n) for n in ("c_idx", "c_got", "c_sum", "c_out", "c_pool", "c_first"))
        s_get = [sem(f"c_get{i}") for i in range(2)]

        @block.gpsimd
        def _(pool):
            def landed(i, par):
                pool.wait_ge(s_get[1 - par], i * 16 + 16 * par)
                pool.sem_inc(s_got, 1)

            def get(i, par):
                nc.gpsimd.tensor_copy(index[:, par, :], k.place_i[:, i, :]).then_inc(s_idx, 1)
                pool.wait_ge(s_idx, i + 1)
                pool.sem_inc(s_pool, 1)
                after(pool, s_sum, i - 1)
                pool.sem_inc(s_pool, 1)
                for c in range(TOPK):
                    nc.gpsimd.indirect_dma_start(got[:, par, c, :], None, k.rows_out, bass.IndirectOffsetOnAxis(
                        ap=index[:, par, c:c + 1], axis=0)).then_inc(s_get[par], 16)
                if not (isinstance(i, int) and i == 0):
                    landed(i, par)
            get(0, 0)
            get(1, 1)
            by_pairs(pool, 2, TILES, get)
            landed(TILES, TILES % 2)

        @block.vector
        def _(dve):
            def total(i, par):
                dve.wait_ge(s_got, i + 1)
                nc.vector.scalar_tensor_tensor(out=k.acc[:, i, :], in0=got[:, par, 0, :], scalar=k.share[:, i, 0:1],
                                               in1=k.acc[:, i, :], op0=ALU.mult, op1=ALU.add).then_inc(s_first, 1)
                dve.wait_ge(s_first, i + 1)
                nc.vector.scalar_tensor_tensor(out=k.acc[:, i, :], in0=got[:, par, 1, :], scalar=k.share[:, i, 1:2],
                                               in1=k.acc[:, i, :], op0=ALU.mult, op1=ALU.add).then_inc(s_sum, 1)
            by_pairs(dve, 0, TILES, total)

        @block.sync
        def _(sp):
            def store(i, par):
                sp.wait_ge(s_sum, i + 1)
                sp.dma_start(a.out[bass.ds(i * P, P), :], k.acc[:, i, :]).then_inc(s_out, 16)
            by_pairs(sp, 0, FULL, store)
            sp.wait_ge(s_sum, TILES)
            sp.dma_start(a.out[FULL * P:N, :], k.acc[0:REST, FULL, :]).then_inc(s_out, 16)
            sp.wait_ge(s_out, 16 * TILES)


def gnn_moe_layer(nc, x, src, dst, g_W, g_as, g_ad, g_bias, g_Wres, ln1_g, ln1_b, ln2_g, ln2_b, f_w1, f_b1,
                  f_w2, f_b2, m_qkv, m_mem, m_wout, m_bout, m_gout, m_gpre, e_Wr, e_br, e_lng, e_lnb, e_W1,
                  e_b1, e_W2, e_b2, out, stages=4):
    a = Names()
    a.x = x
    a.src = src
    a.dst = dst
    a.g_W = g_W
    a.g_as = g_as
    a.g_ad = g_ad
    a.g_bias = g_bias
    a.g_Wres = g_Wres
    a.ln1_g = ln1_g
    a.ln1_b = ln1_b
    a.ln2_g = ln2_g
    a.ln2_b = ln2_b
    a.f_w1 = f_w1
    a.f_b1 = f_b1
    a.f_w2 = f_w2
    a.f_b2 = f_b2
    a.m_qkv = m_qkv
    a.m_mem = m_mem
    a.m_wout = m_wout
    a.m_bout = m_bout
    a.m_gout = m_gout
    a.m_gpre = m_gpre
    a.e_Wr = e_Wr
    a.e_br = e_br
    a.e_lng = e_lng
    a.e_lnb = e_lnb
    a.e_W1 = e_W1
    a.e_b1 = e_b1
    a.e_W2 = e_W2
    a.e_b2 = e_b2
    a.out = out
    k = Names()
    with ExitStack() as top, nc.allow_non_contiguous_dma(reason="a few hundred small constants"):
        def keep(stack, name, shape, dt=F32):
            return stack.enter_context(nc.sbuf_tensor(name, shape, dt))

        def scratch(name, shape):
            return nc.dram_tensor(name, shape, F32, kind="Internal").ap()

        k.table = scratch("table", (NP, ROW))
        k.dst_f = scratch("dst_f", (GROUPS, EG))
        k.rows_in = scratch("rows_in", (MOE_STEPS * MP, D))
        k.rows_out = scratch("rows_out", (MOE_STEPS * MP, D))
        k.ident = keep(top, "ident", [P, P])
        k.ones = keep(top, "ones", [P, P])
        k.pidx = keep(top, "pidx", [P, 1])
        k.acc = keep(top, "acc", [P, TILES, D])
        with ExitStack() as graph:
            k.agg = keep(graph, "agg", [P, TILES, ROW])
            k.res = keep(graph, "res", [P, TILES, D])
            k.q = keep(graph, "q", [P, TILES, MC])
            k.xn0 = keep(graph, "xn0", [P, TILES, D])
            k.cw = keep(graph, "cw", [P, D])
            k.node_am = keep(graph, "node_am", [P, TILES, 2 * GH])
            k.bout, k.gout, k.g2, k.b2n, k.fb2 = (keep(graph, n, [P, D]) for n in ("bout", "gout", "g2", "b2n", "fb2"))
            k.iota_n = keep(graph, "iota_n", [P, NP])
            k.src_i = keep(graph, "src_i", [P, JG, GROUPS], I32)
            k.dst_e = keep(graph, "dst_e", [P, JG, GROUPS])
            k.node_id = keep(graph, "node_id", [P, TILES])
            k.items = keep(graph, "items", [1, WORDS], I32)
            k.need = keep(graph, "need", [1, NEED // NEED_PER], I32)
            setup_and_nodes(nc, k, a)
            if stages >= 2:
                graph_items(nc, k, a)
            if stages >= 3:
                nodes_finish(nc, k, a)
        if stages >= 4:
            k.w1 = keep(top, "w1", [P, EXP, 2, KT, HB, P], BF16)
            k.w2 = keep(top, "w2", [P, EXP, 2, HB, D], BF16)
            k.place_i = keep(top, "place_i", [P, TILES, TOPK], I32)
            k.share = keep(top, "share", [P, TILES, TOPK])
            k.step_word = keep(top, "step_word", [1, MOE_STEPS], I32)
            route(nc, k, a)
            experts(nc, k, a)
            combine(nc, k, a)


_INS = {
    "x": "x", "src": "src", "dst": "dst", "L0_gnn_W": "g_W", "L0_gnn_att_src": "g_as", "L0_gnn_att_dst": "g_ad",
    "L0_gnn_bias": "g_bias", "L0_gnn_W_res": "g_Wres", "L0_gnn_ln1_g": "ln1_g", "L0_gnn_ln1_b": "ln1_b",
    "L0_gnn_ln2_g": "ln2_g", "L0_gnn_ln2_b": "ln2_b", "L0_gnn_ffn_w1": "f_w1", "L0_gnn_ffn_b1": "f_b1",
    "L0_gnn_ffn_w2": "f_w2", "L0_gnn_ffn_b2": "f_b2", "L0_mix_w_qkv": "m_qkv", "L0_mix_mem_kv": "m_mem",
    "L0_mix_w_out": "m_wout", "L0_mix_b_out": "m_bout", "L0_mix_g_out": "m_gout", "L0_mix_g_pre": "m_gpre",
    "L0_ffn_Wr": "e_Wr", "L0_ffn_br": "e_br", "L0_ffn_ln_g": "e_lng", "L0_ffn_ln_b": "e_lnb", "L0_ffn_W1": "e_W1",
    "L0_ffn_b1": "e_b1", "L0_ffn_W2": "e_W2", "L0_ffn_b2": "e_b2",
}


def kernel(**inputs):
    import numpy as _np
    import concourse.bacc as _bacc
    from concourse import mybir as _mybir
    from concourse.bass_utils import run_bass_kernel_spmd as _run

    nc = _bacc.Bacc("TRN2", target_bir_lowering=False, num_devices=1)
    arrays, args = {}, {}
    for name, short in _INS.items():
        v = _np.ascontiguousarray(inputs[name])
        arrays[f"in_{name}_dram"] = v
        args[short] = nc.dram_tensor(f"in_{name}_dram", v.shape, _mybir.dt.from_np(v.dtype), kind="ExternalInput").ap()
    args["out"] = nc.dram_tensor("out_0_dram", (N, D), F32, kind="ExternalOutput").ap()
    gnn_moe_layer(nc, **args)
    r = _run(nc, [arrays], core_ids=[0])
    return r.results[0]["out_0_dram"]
```

```python
from contextlib import ExitStack

import concourse.bass as bass
from concourse import mybir

P = 128
F32 = mybir.dt.float32
BF16 = mybir.dt.bfloat16
I32 = mybir.dt.int32
ALU = mybir.AluOpType
ACT = mybir.ActivationFunctionType
AX_X = mybir.AxisListType.X
RMAX = bass.bass_isa.ReduceOp.max

N = 3125
E = 50000
D = 256
KT = D // P
TILES = -(-N // P)
NP = TILES * P
FULL = N // P
REST = N - FULL * P
GH, GHD = 8, 32
MH, MHD, MEM = 4, 32, 4
MC = MH * MHD
HID = 1024
HB = HID // P
EXP = 8
TOPK = 2
JG = 4
EG = JG * P
GROUPS = -(-E // EG)
GFULL = E // EG
GREST = E - GFULL * EG
ITEMS = GROUPS + TILES - 1
RING = 3
GRING = 4
UNROLL = 6
MANY = 6
ROW = D + GH
WIDE = 2
MP = WIDE * P
MOE_STEPS = (NP * TOPK - EXP) // MP + EXP
EXPERT_BITS = (EXP - 1).bit_length()
LAST, OWN, NEXT = range(3)
NEED_BITS, NEED_PER = ITEMS.bit_length(), GRING
NEED = -(-GROUPS // NEED_PER) * NEED_PER
BACK, FIELDS = 2, 4
BLOCK_BITS = (TILES - 1).bit_length()
WORDS = ITEMS + 2
EPS = 1e-5
SLOPE = 0.2
FAR = 60.0
BIG = 1e30


HALF = FULL // 4 * 2


class Names:
    pass


class Weights:

    def __init__(self, w1h, w1l, w2h, w2l):
        self.w1h, self.w1l, self.w2h, self.w2l = w1h, w1l, w2h, w2l


class Chain:

    def __init__(self, eng, sem, n=0):
        self.eng, self.sem, self.n = eng, sem, n

    def __call__(self, ins):
        self.n = self.n + 1
        ins.then_inc(self.sem, 1)
        self.eng.wait_ge(self.sem, self.n)


def by_pairs(eng, lo, hi, body, per=2):
    turns = (hi - lo) // per
    if turns:
        with eng.Fori(0, turns) as m:
            for n in range(per):
                body(m * per + (lo + n), (lo + n) % 2)
    for i in range(lo + turns * per, hi):
        body(i, i % 2)


def by_slots(eng, lo, hi, slots, body):
    turns = (hi - lo) // slots
    with eng.Fori(0, turns) as m:
        for n in range(slots):
            body(m * slots + (lo + n), n)
    for i in range(lo + turns * slots, hi):
        body(i, i % slots)


def by_many(eng, lo, hi, body):
    turns = (hi - lo) // MANY
    with eng.Fori(0, turns) as m:
        for n in range(MANY):
            body(m * MANY + (lo + n))
    for i in range(lo + turns * MANY, hi):
        body(i)


def by_turns(eng, body):
    assert UNROLL % RING == 0 and (ITEMS - BACK) % UNROLL == 0
    with eng.Fori(1, (ITEMS - BACK) // UNROLL) as m:
        body(m * UNROLL)


def field(nc, eng, word, at, top):
    return within(nc, eng, (word >> at) & ((1 << top.bit_length()) - 1), top)


def within(nc, eng, value, top):
    return nc.s_assert_within(eng.snap(value), min_val=0, max_val=top,
                              skip_runtime_bounds_check_because="the words hold blocks and groups in range")


def cols(v):
    return v.rearrange("(k p) -> p k", p=P)


def after(eng, sem, n):
    if not (isinstance(n, int) and n <= 0):
        eng.wait_ge(sem, n)


def row_on_all(v):
    return v.rearrange("(a d) -> a d", a=1).to_broadcast([P, v.shape[0]])


def setup_and_nodes(nc, k, a):
    with ExitStack() as own, nc.Block() as block:
        def sb(name, shape, dt=F32):
            return own.enter_context(nc.sbuf_tensor(name, shape, dt))

        def ps(name, shape):
            return own.enter_context(nc.psum_tensor(name, shape, F32))

        def sem(name):
            return own.enter_context(nc.semaphore(name))

        w_hr = sb("w_hr", [P, KT, 2 * D])
        w_qkv = sb("w_qkv", [P, KT, 3 * MC])
        wout = sb("wout", [P, D])
        gbias = sb("gbias", [P, D])
        att = sb("att", [P, 2, D])
        g1c = sb("g1c", [P, 3, KT])
        edge_i = sb("edge_i", [P, 2, EG], I32)
        edge_f = sb("edge_f", [P, 2, EG])
        below = sb("below", [P, TILES])
        edge0 = sb("edge0", [P, GROUPS])
        small = sb("small", [P, P])
        start_g = sb("start_g", [P, 1])
        start_b = sb("start_b", [P, 1])
        cnt_sb = sb("cnt_sb", [P, TILES + 1])
        step_b = sb("step_b", [P, P])
        mask_g = sb("mask_g", [P, 1])
        need_f = sb("need_f", [1, NEED])
        need_i = sb("need_i", [1, NEED], I32)
        weight = sb("weight", [P, FIELDS])
        zero_row = sb("zero_row", [P, D])
        stats = sb("stats", [P, TILES, 6])
        st_a = sb("st_a", [P, TILES])
        st_b = sb("st_b", [P, TILES])
        st_v = sb("st_v", [P, TILES])
        mean = sb("mean", [P, TILES])
        rstd = sb("rstd", [P, TILES])
        rms = sb("rms", [P, TILES])
        an = sb("an", [P, 2, D])
        bn = sb("bn", [P, 2, D])
        an_t = sb("an_t", [P, 2, KT, P])
        bn_t = sb("bn_t", [P, 2, KT, P])
        prod = sb("prod", [P, 2, 2, D])
        keys = sb("keys", [P, NP])
        vals = sb("vals", [P, TILES, MC + 1])
        gmax = sb("gmax", [P, 2, 2 * GH])
        spread = sb("spread", [1, GH + 1])
        zself = sb("zself", [P, TILES, GH])
        zself2 = sb("zself2", [P, TILES, GH])
        kmax = sb("kmax", [P, 2])
        kexp_both = sb("kexp_both", [P, 4, P])
        kexp, kexp_t = kexp_both[:, 0:2], kexp_both[:, 2:4]
        edge_less = kexp_both[:].rearrange("p a b -> p (a b)")
        head_mask = sb("head_mask", [P, P])
        ctx_n = sb("ctx_n", [P, P])
        ctx_t = sb("ctx_t", [P, P])
        rz = sb("rz", [P, 1])
        qmax = sb("qmax", [P, TILES * MH])
        qsum = sb("qsum", [P, TILES * MH])
        ps_a = [ps(f"ps_a{i}", [P, KT, P]) for i in range(2)]
        ps_b = [ps(f"ps_b{i}", [P, KT, P]) for i in range(2)]
        ps_hr = [ps(f"ps_hr{i}", [P, 2 * D]) for i in range(2)]
        ps_qkv = [ps(f"ps_qkv{i}", [P, 3 * MC]) for i in range(2)]

        s_x2, s_base, s_prod, s_sums, s_less = (sem(n) for n in ("s_x2", "s_base", "s_prod", "s_sums", "s_less"))
        s_x, s_row, s_edge, s_tab = (sem(n) for n in ("s_x", "s_row", "s_edge", "s_tab"))
        s_set, s_dram, s_memkv = (sem(n) for n in ("s_set", "s_dram", "s_memkv"))
        s_edge_f, s_edge_t, s_edge_out, s_cnt, s_steps, s_items = (
            sem(n) for n in ("s_edge_f", "s_edge_t", "s_edge_out", "s_cnt", "s_steps", "s_items"))
        s_dve, s_scale, s_an, s_bn, s_ta, s_tb, s_at, s_bt, s_hr, s_qkv, s_hr_out, s_qkv_out = (
            sem(n) for n in ("s_dve", "s_scale", "s_an", "s_bn", "s_ta", "s_tb", "s_at", "s_bt", "s_hr", "s_qkv",
                             "s_hr_out", "s_qkv_out"))
        s_nodes, s_gmax, s_gall, s_zself, s_wself, s_kmax, s_kexp, s_kt, s_kt_out, s_ctx = (
            sem(n) for n in ("s_nodes", "s_gmax", "s_gall", "s_zself", "s_wself", "s_kmax", "s_kexp", "s_kt",
                             "s_kt_out", "s_ctx"))
        s_var, s_root = sem("s_var"), sem("s_root")
        s_ctx_n, s_ctx_t, s_ctx_to, s_q0, s_q1 = (
            sem(n) for n in ("s_ctx_n", "s_ctx_t", "s_ctx_to", "s_q0", "s_q1"))

        @block.sync
        def _(sp):
            sp.dma_start(k.acc[:, 0:HALF, :], a.x[0:HALF * P, :].rearrange("(t p) d -> p t d", p=P)).then_inc(s_x, 16)
            sp.wait_ge(s_set, 2)
            for n, v in enumerate((a.src, a.dst)):
                sp.dma_start(edge_i[0:GFULL, n, :], v[0:GFULL * EG].rearrange("(g e) -> g e", e=EG)).then_inc(s_edge, 16)
                sp.dma_start(edge_i[GFULL:GROUPS, n, 0:GREST],
                             v[GFULL * EG:E].rearrange("(g e) -> g e", g=1)).then_inc(s_edge, 16)
            sp.wait_ge(s_set, 3)
            sp.dma_start(k.acc[:, HALF:FULL, :], a.x[HALF * P:FULL * P, :].rearrange("(t p) d -> p t d", p=P)).then_inc(s_x2, 16)
            sp.dma_start(k.acc[0:REST, FULL, :], a.x[FULL * P:N, :]).then_inc(s_x2, 16)
            sp.dma_start(w_hr[:, :, 0:D], a.g_W.rearrange("(k p) n -> p k n", p=P)).then_inc(s_row, 16)
            sp.dma_start(w_hr[:, :, D:2 * D], a.g_Wres.rearrange("(k p) n -> p k n", p=P)).then_inc(s_row, 16)
            sp.dma_start(w_qkv[:], a.m_qkv.rearrange("(k p) n -> p k n", p=P)).then_inc(s_row, 16)
            sp.dma_start(wout[:], a.m_wout).then_inc(s_row, 16)
            for n, v in enumerate((a.ln1_g, a.ln1_b, a.m_gpre)):
                sp.dma_start(g1c[:, n, :], cols(v)).then_inc(s_row, 16)
            sp.dma_start(gbias[:], row_on_all(a.g_bias)).then_inc(s_row, 16)
            for n, v in enumerate((a.g_as, a.g_ad)):
                sp.dma_start(att[:, n, :], row_on_all(v.rearrange("h d -> (h d)"))).then_inc(s_row, 16)
            for to, v in ((k.bout, a.m_bout), (k.gout, a.m_gout), (k.g2, a.ln2_g), (k.b2n, a.ln2_b), (k.fb2, a.f_b2)):
                sp.dma_start(to[:], row_on_all(v)).then_inc(s_row, 16)
            sp.wait_ge(s_set, 11)
            sp.dma_start(k.rows_in.rearrange("(t p) d -> p t d", p=P),
                         zero_row[:].unsqueeze(1).to_broadcast([P, MOE_STEPS * WIDE, D])).then_inc(s_dram, 16)
            sp.wait_ge(s_edge_f, 1)
            sp.dma_start(k.dst_f, edge_f[0:GROUPS, 1, :]).then_inc(s_dram, 16)
            sp.wait_ge(s_qkv_out, TILES)
            sp.dma_start(keys[:, N:N + MEM], a.m_mem[0].rearrange("h d m -> (h d) m")).then_inc(s_memkv, 16)
            sp.dma_start(vals[REST:REST + MEM, FULL, 0:MC], a.m_mem[1].rearrange("h d m -> m (h d)")).then_inc(s_memkv, 16)
            sp.wait_ge(s_nodes, 1)
            sp.dma_start(k.table.rearrange("(t p) r -> p t r", p=P), k.agg[:]).then_inc(s_tab, 16)
            sp.wait_ge(s_tab, 16)
            sp.wait_ge(s_dram, 32)

        @block.gpsimd
        def _(pool):
            nc.gpsimd.memset(edge_i[:, 0, :], 0).then_inc(s_set, 1)
            nc.gpsimd.memset(edge_i[:, 1, :], NP + P).then_inc(s_set, 1)
            nc.gpsimd.memset(k.acc[:, FULL, :], 0.0).then_inc(s_set, 1)
            nc.gpsimd.iota(k.pidx[:], pattern=[[0, 1]], base=0, channel_multiplier=1,
                           allow_small_or_imprecise_dtypes=True).then_inc(s_set, 1)
            nc.gpsimd.iota(k.iota_n[:], pattern=[[1, NP]], base=0, channel_multiplier=0,
                           allow_small_or_imprecise_dtypes=True).then_inc(s_set, 1)
            nc.gpsimd.iota(k.node_id[:], pattern=[[P, TILES]], base=0, channel_multiplier=1,
                           allow_small_or_imprecise_dtypes=True).then_inc(s_set, 1)
            nc.gpsimd.iota(edge0[:], pattern=[[EG, GROUPS]], base=0, channel_multiplier=0,
                           allow_small_or_imprecise_dtypes=True).then_inc(s_set, 1)
            nc.gpsimd.iota(mask_g[:], pattern=[[0, 1]], base=0, channel_multiplier=EG,
                           allow_small_or_imprecise_dtypes=True).then_inc(s_set, 1)
            nc.gpsimd.memset(vals[:, :, MC:MC + 1], 1.0).then_inc(s_set, 1)
            nc.gpsimd.memset(need_f[:], 0.0).then_inc(s_set, 1)
            nc.gpsimd.memset(zero_row[:], 0.0).then_inc(s_set, 1)
            pool.wait_ge(s_scale, 1)
            pool.wait_ge(s_row, 16 * 15)

            def shares(i, par):
                nc.gpsimd.tensor_tensor(k.acc[:, i, :], k.acc[:, i, :], k.xn0[:, i, :], ALU.add).then_inc(s_base, 1)
                pool.wait_ge(s_hr_out, i + 1)
                pool.sem_inc(k.s_passed, 1)
                after(pool, s_sums, i - 1)
                pool.sem_inc(k.s_passed, 1)
                nc.gpsimd.tensor_tensor(prod[:, par, 0, :], k.agg[:, i, 0:D], att[:, 0, :], ALU.mult)
                nc.gpsimd.tensor_tensor(prod[:, par, 1, :], k.agg[:, i, 0:D], att[:, 1, :], ALU.mult).then_inc(s_prod, 1)
                pool.wait_ge(s_base, i + 1)
                pool.sem_inc(k.s_passed, 1)
                nc.gpsimd.tensor_tensor(k.acc[:, i, :], k.acc[:, i, :], k.fb2[:], ALU.add)
            shares(0, 0)
            shares(1, 1)
            by_pairs(pool, 2, TILES, shares)
            pool.wait_ge(s_gmax, 1)
            nc.gpsimd.partition_all_reduce(gmax[:, 1, :], gmax[:, 0, :], P, RMAX).then_inc(s_gall, 1)

        def layer_stats(dve, link, src, n):
            def one(t):
                nc.vector.bn_stats(stats[:, t, :], src[:, t, :])
            by_many(dve, 0, HALF, one)
            if n == 1:
                dve.wait_ge(s_x2, 32)
            by_many(dve, HALF, TILES - 1, one)
            link(nc.vector.bn_stats(stats[:, TILES - 1, :], src[:, TILES - 1, :]))
            link(nc.vector.tensor_tensor(st_a[:], stats[:, :, 1], stats[:, :, 4], ALU.subtract))
            link(nc.vector.tensor_tensor(st_a[:], st_a[:], st_a[:], ALU.mult))
            link(nc.vector.tensor_tensor(st_b[:], stats[:, :, 2], stats[:, :, 5], ALU.add))
            link(nc.vector.scalar_tensor_tensor(out=st_v[:], in0=st_a[:], scalar=D / 4.0, in1=st_b[:], op0=ALU.mult,
                                                op1=ALU.add))
            link(nc.vector.tensor_tensor(mean[:], stats[:, :, 1], stats[:, :, 4], ALU.add))
            link(nc.vector.tensor_scalar(mean[:], mean[:], 0.5, None, ALU.mult))
            nc.vector.tensor_scalar(rstd[:], st_v[:], 1.0 / D, EPS, ALU.mult, ALU.add).then_inc(s_var, 1)
            dve.wait_ge(s_root, n)
            link(nc.vector.reciprocal(st_a[:], rstd[:]))
            link(nc.vector.tensor_scalar(st_b[:], st_v[:], 1.0 / D, EPS, ALU.mult, ALU.add))
            link(nc.vector.tensor_tensor(st_b[:], st_b[:], st_a[:], ALU.mult))
            link(nc.vector.tensor_tensor(st_b[:], st_b[:], rstd[:], ALU.add))
            link(nc.vector.reciprocal(rstd[:], st_b[:]))
            link(nc.vector.tensor_scalar(rstd[:], rstd[:], 2.0, None, ALU.mult))

        @block.vector
        def _(dve):
            link = Chain(dve, s_dve)
            link(nc.vector.memset(k.ones[:], 1.0))
            link(nc.vector.memset(head_mask[:], 0.0))
            for h in range(MH):
                link(nc.vector.memset(head_mask[MHD * h:MHD * h + MHD, MHD * h:MHD * h + MHD], float(MHD) ** -0.5))
            dve.wait_ge(s_x, 16)
            layer_stats(dve, link, k.acc, 1)

            def norm0(t):
                nc.vector.tensor_scalar(k.xn0[:, t, :], k.acc[:, t, :], mean[:, bass.ds(t, 1)], rstd[:, bass.ds(t, 1)],
                                        ALU.subtract, ALU.mult)
            by_many(dve, 0, TILES - 1, norm0)
            link(nc.vector.tensor_scalar(k.xn0[:, TILES - 1, :], k.acc[:, TILES - 1, :], mean[:, TILES - 1:TILES],
                                         rstd[:, TILES - 1:TILES], ALU.subtract, ALU.mult))
            layer_stats(dve, link, k.xn0, 2)
            link(nc.vector.tensor_tensor(st_b[:], mean[:], mean[:], ALU.mult))
            nc.vector.scalar_tensor_tensor(out=rms[:], in0=st_b[:], scalar=float(D), in1=st_v[:], op0=ALU.mult,
                                           op1=ALU.add).then_inc(s_var, 1)
            dve.wait_ge(s_root, 3)
            link(nc.vector.tensor_scalar(rms[:], rms[:], 1e-12, None, ALU.max))
            link(nc.vector.reciprocal(rms[:], rms[:]))
            nc.vector.tensor_scalar(rms[:], rms[:], float(D) ** 0.5, None, ALU.mult).then_inc(s_scale, 1)
            dve.wait_ge(s_set, 11)
            link(nc.vector.tensor_scalar(k.ident[:], k.iota_n[:, 0:P], k.pidx[:, 0:1], None, ALU.is_equal))
            dve.wait_ge(s_edge, 64)
            nc.vector.tensor_copy(edge_f[:], edge_i[:]).then_inc(s_edge_f, 1)
            dve.wait_ge(s_edge_f, 1)
            dve.wait_ge(s_edge_t, 1)
            nc.vector.tensor_copy(k.src_i[:], ps_hr[0][:, 0:JG * GROUPS].rearrange("p (j g) -> p j g", j=JG)).then_inc(s_edge_out, 1)
            nc.vector.tensor_copy(k.dst_e[:], ps_hr[1][:, 0:JG * GROUPS].rearrange("p (j g) -> p j g", j=JG)).then_inc(s_edge_out, 1)
            dve.wait_ge(s_row, 16 * 15)

            def an_of(i, par):
                after(dve, s_ta, i - 1)
                nc.vector.tensor_scalar(an[:, par, :], k.xn0[:, i, :], mean[:, bass.ds(i, 1)], rstd[:, bass.ds(i, 1)],
                                        ALU.subtract, ALU.mult).then_inc(s_an, 1)

            def gained(i, par, ahead=True):
                dve.wait_ge(s_ta, i + 1)
                after(dve, s_hr, i - 1)
                for kt in range(KT):
                    m = nc.vector.tensor_scalar(an_t[:, par, kt, :], ps_a[par][:, kt, :], g1c[:, 0, kt:kt + 1],
                                                g1c[:, 1, kt:kt + 1], ALU.mult, ALU.add)
                m.then_inc(s_at, 1)
                if ahead:
                    an_of(i + 2, par)

            def node(i, par):
                dve.wait_ge(s_hr, i + 1)
                nc.vector.tensor_tensor(k.res[:, i, :], ps_hr[par][:, D:2 * D], gbias[:], ALU.add)
                nc.vector.tensor_copy(k.agg[:, i, 0:D], ps_hr[par][:, 0:D]).then_inc(s_hr_out, 1)
                after(dve, s_less, i)
                nc.vector.tensor_scalar(edge_less[0:GROUPS, :], edge_f[0:GROUPS, 1, :], k.iota_n[0:GROUPS, bass.ds(i * P, 1)],
                                        0.0, ALU.is_lt, ALU.add, accum_out=below[0:GROUPS, bass.ds(i, 1)]).then_inc(s_less, 1)

            def sums(i, par):
                dve.wait_ge(s_prod, i + 1)
                for n, to in enumerate((k.agg[:, i, D:ROW], k.node_am[:, i, 0:GH])):
                    m = nc.vector.tensor_reduce(to, prod[:, par, n, :].rearrange("p (h d) -> p h d", h=GH), AX_X, ALU.add)
                m.then_inc(s_sums, 1)

            def both(i, par, ahead=True):
                if ahead is not None:
                    gained(i + 1, 1 - par, ahead)
                node(i, par)
                if not (isinstance(i, int) and i == 0):
                    sums(i - 1, 1 - par)
            an_of(0, 0)
            an_of(1, 1)
            gained(0, 0)
            both(0, 0)
            both(1, 1)
            by_pairs(dve, 2, TILES - 3, both)
            both(TILES - 3, (TILES - 3) % 2, False)
            both(TILES - 2, (TILES - 2) % 2, False)
            both(TILES - 1, (TILES - 1) % 2, None)
            sums(TILES - 1, (TILES - 1) % 2)
            dve.wait_ge(s_sums, TILES)
            dve.wait_ge(s_less, TILES)
            nc.vector.tensor_copy(small[:, P - 2:P - 1], k.ones[:, 0:1]).then_inc(s_nodes, 1)
            by_head = k.agg[:, :, D:ROW].rearrange("p t h -> p h t")
            link(nc.vector.tensor_reduce(gmax[:, 0, GH:2 * GH], by_head, AX_X, ALU.min))
            nc.vector.tensor_scalar(gmax[:, 0, GH:2 * GH], gmax[:, 0, GH:2 * GH], -1.0, None, ALU.mult)
            link(nc.vector.tensor_reduce(gmax[:, 0, 0:GH], by_head, AX_X, ALU.max))
            nc.vector.tensor_copy(small[:, P - 3:P - 2], k.ones[:, 0:1]).then_inc(s_gmax, 1)
            dve.wait_ge(s_cnt, 1)
            link(nc.vector.tensor_copy(cnt_sb[:, 0:TILES], ps_b[0][:, 0, 0:TILES]))
            link(nc.vector.tensor_copy(cnt_sb[0:TILES, TILES:TILES + 1], ps_b[0][0:TILES, 1, 0:1]))
            link(nc.vector.tensor_scalar(small[:, 0:TILES - 1], cnt_sb[:, 1:TILES], mask_g[:, 0:1], 0.0, ALU.is_le,
                                         ALU.add, accum_out=start_g[:]))
            link(nc.vector.tensor_tensor(start_g[:], start_g[:], k.pidx[:], ALU.add))
            link(nc.vector.tensor_scalar(small[0:TILES, 0:GROUPS - 1], edge0[0:TILES, 1:GROUPS],
                                         cnt_sb[0:TILES, TILES:TILES + 1], 0.0, ALU.is_lt, ALU.add,
                                         accum_out=start_b[0:TILES, :]))
            link(nc.vector.tensor_tensor(start_b[0:TILES, :], start_b[0:TILES, :], k.pidx[0:TILES, :], ALU.add))
            link(nc.vector.tensor_scalar(step_b[0:TILES, :], k.iota_n[0:TILES, 0:P], start_b[0:TILES, 0:1], None, ALU.is_ge))
            link(nc.vector.tensor_scalar(weight[:, 0:1], k.pidx[:], 1.0, None, ALU.is_ge))
            for n in range(1, FIELDS):
                m = nc.vector.tensor_scalar(weight[:, n:n + 1], k.pidx[:], 1.0, float(1 << n * BLOCK_BITS), ALU.is_ge, ALU.mult)
            m.then_inc(s_steps, 1)
            dve.wait_ge(s_gall, 1)
            link(nc.vector.tensor_tensor(spread[:, 0:GH], gmax[0:1, 1, 0:GH], gmax[0:1, 1, GH:2 * GH], ALU.add))
            link(nc.vector.tensor_reduce(spread[:, GH:GH + 1], spread[:, 0:GH], AX_X, ALU.max))
            link(nc.vector.tensor_scalar(spread[:, 0:1], spread[:, GH:GH + 1], FAR, None, ALU.is_gt))
            link(nc.vector.tensor_copy(k.far[:], spread[:, 0:1]))
            link(nc.vector.tensor_tensor(zself[:], k.node_am[:, :, 0:GH],
                                         gmax[:, 1:2, 0:GH].to_broadcast([P, TILES, GH]), ALU.add))
            link(nc.vector.scalar_tensor_tensor(out=k.node_am[:, :, GH:2 * GH], in0=zself[:], scalar=SLOPE,
                                                in1=zself[:], op0=ALU.mult, op1=ALU.max))
            link(nc.vector.tensor_tensor(zself2[:], k.node_am[:, :, 0:GH], k.agg[:, :, D:ROW], ALU.add))
            link(nc.vector.scalar_tensor_tensor(out=zself[:], in0=zself2[:], scalar=SLOPE, in1=zself2[:],
                                                op0=ALU.mult, op1=ALU.max))
            nc.vector.tensor_tensor(zself[:], zself[:], k.node_am[:, :, GH:2 * GH], ALU.subtract).then_inc(s_zself, 1)
            dve.wait_ge(s_memkv, 32)
            link(nc.vector.tensor_reduce(kmax[:, 0:1], keys[:, 0:N + MEM], AX_X, ALU.max))
            nc.vector.tensor_scalar(kmax[:, 1:2], kmax[:, 0:1], -1.0, None, ALU.mult).then_inc(s_kmax, 1)
            qv = k.q[:].rearrange("p t (h d) -> p (t h) d", h=MH)
            link(nc.vector.tensor_reduce(qmax[:], qv, AX_X, ALU.max))
            nc.vector.tensor_tensor(qv, qv, qmax[:].unsqueeze(2).to_broadcast([P, TILES * MH, MHD]),
                                    ALU.subtract).then_inc(s_q0, 1)

            dve.wait_ge(s_items, 1)
            link(nc.vector.tensor_copy(k.items[:], ps_b[1][0:1, 0, 0:WORDS]))
            link(nc.vector.tensor_copy(need_f[0:1, GRING:GROUPS], ps_b[1][0:1, 1, 0:GROUPS - GRING]))
            ni = need_i[0:1, :].rearrange("p (m s) -> p m s", s=NEED_PER)
            link(nc.vector.tensor_copy(need_i[:], need_f[:]))
            for n in range(1, NEED_PER):
                link(nc.vector.tensor_scalar(ni[:, :, n], ni[:, :, n], n * NEED_BITS, None, ALU.logical_shift_left))
                link(nc.vector.tensor_tensor(ni[:, :, 0], ni[:, :, 0], ni[:, :, n], ALU.bitwise_or))
            link(nc.vector.tensor_copy(k.need[:], ni[:, :, 0]))

            dve.wait_ge(s_tab, 16)
            dve.wait_ge(s_wself, 1)
            for t0, t1 in ((0, 13), (13, TILES)):
                hv = k.agg[:, t0:t1, 0:D].rearrange("p t (h d) -> p t h d", h=GH)
                link(nc.vector.tensor_tensor(hv, hv, zself2[:, t0:t1, :].unsqueeze(3).to_broadcast([P, t1 - t0, GH, GHD]),
                                             ALU.mult))
            link(nc.vector.tensor_copy(k.agg[:, :, D:ROW], zself2[:]))
            dve.wait_ge(s_q1, 1)
            link(nc.vector.tensor_reduce(qsum[:], qv, AX_X, ALU.add))
            link(nc.vector.reciprocal(qsum[:], qsum[:]))
            link(nc.vector.tensor_tensor(qv, qv, qsum[:].unsqueeze(2).to_broadcast([P, TILES * MH, MHD]), ALU.mult))
            dve.wait_ge(s_ctx, TILES)
            link(nc.vector.reciprocal(rz[:], ps_hr[0][:, MC:MC + 1]))
            nc.vector.scalar_tensor_tensor(out=ctx_n[:], in0=ps_hr[0][:, 0:MC], scalar=rz[:, 0:1], in1=head_mask[:],
                                           op0=ALU.mult, op1=ALU.mult).then_inc(s_ctx_n, 1)
            dve.wait_ge(s_ctx_t, 1)
            nc.vector.tensor_copy(ctx_t[:], ps_a[0][:, 0, :]).then_inc(s_ctx_to, 1)
            dve.wait_ge(s_ctx_t, 2)
            link(nc.vector.tensor_copy(k.cw[:], ps_hr[1][:, 0:D]))
            link(nc.vector.tensor_tensor(k.cw[0:MHD, :], k.cw[0:MHD, :], k.bout[0:MHD, :], ALU.add))

        @block.scalar
        def _(act):
            for n, v in enumerate((rstd, rstd, rms)):
                act.wait_ge(s_var, n + 1)
                nc.scalar.activation(v[:], v[:], ACT.Sqrt).then_inc(s_root, 1)
            act.wait_ge(s_scale, 1)
            act.wait_ge(s_row, 16 * 15)

            def bn_of(i, par):
                after(act, s_tb, i - 1)
                nc.scalar.activation(bn[:, par, :], k.xn0[:, i, :], ACT.Copy, scale=rms[:, bass.ds(i, 1)]).then_inc(s_bn, 1)

            def gained(i, par, ahead=True):
                act.wait_ge(s_tb, i + 1)
                after(act, s_qkv, i - 1)
                for kt in range(KT):
                    m = nc.scalar.activation(bn_t[:, par, kt, :], ps_b[par][:, kt, :], ACT.Copy, scale=g1c[:, 2, kt:kt + 1])
                m.then_inc(s_bt, 1)
                if ahead:
                    bn_of(i + 2, par)

            def node(i, par):
                act.wait_ge(s_qkv, i + 1)
                nc.scalar.copy(k.q[:, i, :], ps_qkv[par][:, 0:MC])
                nc.scalar.copy(vals[:, i, 0:MC], ps_qkv[par][:, MC:2 * MC])
                nc.scalar.copy(keys[:, bass.ds(i * P, P)], ps_qkv[par][:, 2 * MC:3 * MC]).then_inc(s_qkv_out, 1)

            def both(i, par):
                gained(i + 1, 1 - par)
                node(i, par)
            bn_of(0, 0)
            bn_of(1, 1)
            gained(0, 0)
            both(0, 0)
            both(1, 1)
            by_pairs(act, 2, TILES - 3, both)
            for i in range(TILES - 3, TILES):
                if i + 1 < TILES:
                    gained(i + 1, (i + 1) % 2, False)
                node(i, i % 2)
            act.wait_ge(s_zself, 1)
            nc.scalar.activation(zself2[:], zself[:], ACT.Exp).then_inc(s_wself, 1)
            act.wait_ge(s_kmax, 1)

            def key_exp(i, par):
                after(act, s_kt, i - 1)
                nc.scalar.activation(kexp[:, par, :], keys[:, bass.ds(i * P, P)], ACT.Exp, bias=kmax[:, 1:2]).then_inc(s_kexp, 1)

            def key_out(i, par):
                act.wait_ge(s_kt, i + 1)
                after(act, s_ctx, i - 1)
                nc.scalar.copy(kexp_t[:, par, :], ps_a[par][:, 0, :]).then_inc(s_kt_out, 1)

            def key_tile(i, par):
                key_exp(i + 1, 1 - par)
                key_out(i, par)
            key_exp(0, 0)
            key_tile(0, 0)
            key_tile(1, 1)
            by_pairs(act, 2, HALF, key_tile)
            act.wait_ge(s_q0, 1)
            qf = k.q[:].rearrange("p t c -> p (t c)")
            nc.scalar.activation(qf, qf, ACT.Exp).then_inc(s_q1, 1)
            by_pairs(act, HALF, TILES - 2, key_tile)
            par = (TILES - 1) % 2
            act.wait_ge(s_kt, TILES - 2)
            nc.scalar.activation(kexp[:, par, 0:REST + MEM], keys[:, N - REST:N + MEM], ACT.Exp, bias=kmax[:, 1:2])
            nc.scalar.activation(kexp[:, par, REST + MEM:P], k.ones[:, REST + MEM:P], ACT.Copy, scale=0.0).then_inc(s_kexp, 1)
            key_out(TILES - 2, TILES % 2)
            key_out(TILES - 1, par)

        @block.tensor
        def _(pe):
            pe.wait_ge(s_edge_f, 1)
            for n in range(2):
                for j in range(JG):
                    m = nc.tensor.transpose(ps_hr[n][:, j * GROUPS:(j + 1) * GROUPS],
                                            edge_f[0:GROUPS, n, j * P:(j + 1) * P], k.ident[0:GROUPS, 0:GROUPS])
            m.then_inc(s_edge_t, 1)
            pe.wait_ge(s_edge_out, 2)
            pe.wait_ge(s_scale, 1)
            pe.wait_ge(s_row, 16 * 15)

            def turn(i, par):
                pe.wait_ge(s_an, i + 1)
                after(pe, s_at, i - 1)
                for kt in range(KT):
                    m = nc.tensor.transpose(ps_a[par][:, kt, :], an[:, par, kt * P:(kt + 1) * P], k.ident[:])
                m.then_inc(s_ta, 1)
                pe.wait_ge(s_bn, i + 1)
                after(pe, s_bt, i - 1)
                for kt in range(KT):
                    m = nc.tensor.transpose(ps_b[par][:, kt, :], bn[:, par, kt * P:(kt + 1) * P], k.ident[:])
                m.then_inc(s_tb, 1)

            def products(i, par):
                pe.wait_ge(s_at, i + 1)
                after(pe, s_hr_out, i - 1)
                for kt in range(KT):
                    m = nc.tensor.matmul(ps_hr[par][:], an_t[:, par, kt, :], w_hr[:, kt, :], start=(kt == 0),
                                         stop=(kt == KT - 1))
                m.then_inc(s_hr, 1)
                pe.wait_ge(s_bt, i + 1)
                after(pe, s_qkv_out, i - 1)
                for kt in range(KT):
                    nc.tensor.matmul(ps_qkv[par][:, 0:MC], bn_t[:, par, kt, :], w_qkv[:, kt, 0:MC], start=(kt == 0),
                                     stop=(kt == KT - 1))
                for kt in range(KT):
                    nc.tensor.matmul(ps_qkv[par][:, MC:2 * MC], bn_t[:, par, kt, :], w_qkv[:, kt, 2 * MC:3 * MC],
                                     start=(kt == 0), stop=(kt == KT - 1))
                for kt in range(KT):
                    m = nc.tensor.matmul(ps_qkv[par][:, 2 * MC:3 * MC], w_qkv[:, kt, MC:2 * MC], bn_t[:, par, kt, :],
                                         start=(kt == 0), stop=(kt == KT - 1))
                m.then_inc(s_qkv, 1)

            def node(i, par):
                turn(i + 1, 1 - par)
                products(i, par)

            turn(0, 0)
            node(0, 0)
            node(1, 1)
            by_pairs(pe, 2, TILES - 1, node)
            products(TILES - 1, (TILES - 1) % 2)
            pe.wait_ge(s_nodes, 1)
            pe.wait_ge(s_bt, TILES)
            nc.tensor.matmul(ps_b[0][:, 0, 0:TILES], k.ones[0:GROUPS, :], below[0:GROUPS, :], start=True, stop=True)
            nc.tensor.matmul(ps_b[0][0:TILES, 1, 0:1], below[0:GROUPS, :], k.ones[0:GROUPS, 0:1], start=True,
                             stop=True).then_inc(s_cnt, 1)
            pe.wait_ge(s_steps, 1)
            word = ps_b[1][0:1, 0, :]
            for n in reversed(range(FIELDS)):
                gap = FIELDS - 1 - n
                nc.tensor.matmul(word[:, gap:WORDS], weight[0:TILES, n:n + 1], step_b[0:TILES, 0:WORDS - gap],
                                 start=(gap == 0), stop=(n == 0))
            nc.tensor.matmul(ps_b[1][0:1, 1, 0:GROUPS - GRING], start_g[:, 0:1], k.ident[:, 1:1 + GROUPS - GRING],
                             start=True, stop=True).then_inc(s_items, 1)
            pe.wait_ge(s_hr_out, TILES)
            pe.wait_ge(s_at, TILES)
            pe.wait_ge(s_memkv, 32)

            def key_turn(i, par):
                pe.wait_ge(s_kexp, i + 1)
                after(pe, s_kt_out, i - 1)
                nc.tensor.transpose(ps_a[par][:, 0, :], kexp[:, par, :], k.ident[:]).then_inc(s_kt, 1)

            def context(i, par, first=False, last=False):
                pe.wait_ge(s_kt_out, i + 1)
                nc.tensor.matmul(ps_hr[0][:, 0:MC + 1], kexp_t[:, par, :], vals[:, i, :], start=first,
                                 stop=last).then_inc(s_ctx, 1)
            key_turn(0, 0)
            key_turn(1, 1)
            context(0, 0, first=True)

            def both(i, par):
                key_turn(i + 1, 1 - par)
                context(i, par)
            by_pairs(pe, 1, TILES - 1, both)
            context(TILES - 1, (TILES - 1) % 2, last=True)
            pe.wait_ge(s_ctx_n, 1)
            nc.tensor.transpose(ps_a[0][:, 0, :], ctx_n[:], k.ident[:]).then_inc(s_ctx_t, 1)
            pe.wait_ge(s_ctx_to, 1)
            nc.tensor.matmul(ps_hr[1][:, 0:D], ctx_t[:], wout[:], start=True, stop=True).then_inc(s_ctx_t, 1)


def exact_maxima(nc, k, a):
    with ExitStack() as own, nc.Block() as block:
        def sb(name, shape, dt=F32):
            return own.enter_context(nc.sbuf_tensor(name, shape, dt))

        def sem(name):
            return own.enter_context(nc.semaphore(name))

        rows = sb("x_rows", [P, JG, ROW])
        index = sb("x_index", [P, JG], I32)
        dst_all = sb("x_dst_all", [P, EG])
        outside = sb("x_outside", [P, EG])
        masked = sb("x_masked", [P, EG])
        item_max = sb("x_item_max", [P, GH])
        top = sb("x_top", [P, TILES, GH])
        z = sb("x_z", [P, TILES, GH])
        ps_src = [own.enter_context(nc.psum_tensor(f"x_ps_src{i}", [P, EG], F32)) for i in range(2)]
        s_table, s_rows, s_dst, s_index, s_src, s_taken, s_item, s_link, s_z, s_w = (
            sem("x_" + n) for n in ("table", "rows", "dst", "index", "src", "taken", "item", "link", "z", "w"))

        def where_far(eng):
            return eng.If(eng.value_load(k.far[0:1, 0:1], min_val=0, max_val=1) > 0)

        def block_of(eng, i):
            word = eng.value_load(k.items[0:1, bass.ds(i + 1, 1)], min_val=0, max_val=(1 << BLOCK_BITS * FIELDS) - 1)
            return field(nc, eng, word, BACK * BLOCK_BITS, TILES - 1)

        def group_of(eng, i):
            return within(nc, eng, (i - block_of(eng, i)) & ((1 << GROUPS.bit_length()) - 1), GROUPS - 1)

        @block.sync
        def _(sp):
            with where_far(sp):
                sp.dma_start(k.agg[:], k.table.rearrange("(t p) r -> p t r", p=P)).then_inc(s_table, 16)
                with sp.Fori(0, ITEMS) as i:
                    sp.wait_ge(s_item, i)
                    sp.dma_start(dst_all[:], k.dst_f[bass.ds(group_of(sp, i), 1), :].to_broadcast([P, EG])).then_inc(s_dst, 16)

        @block.gpsimd
        def _(pool):
            with where_far(pool):
                with pool.Fori(0, ITEMS) as i:
                    g = group_of(pool, i)
                    pool.wait_ge(s_item, i)
                    pool.sem_inc(k.s_passed, 1)
                    nc.gpsimd.tensor_copy(index[:], k.src_i[:, :, g]).then_inc(s_index, 1)
                    pool.wait_ge(s_index, i + 1)
                    pool.sem_inc(k.s_passed, 1)
                    for j in range(JG):
                        nc.gpsimd.indirect_dma_start(rows[:, j, :], None, k.table, bass.IndirectOffsetOnAxis(
                            ap=index[:, j:j + 1], axis=0)).then_inc(s_rows, 16)

        @block.tensor
        def _(pe):
            with where_far(pe):
                with pe.Fori(0, ITEMS) as i:
                    pe.wait_ge(s_rows, i * (16 * JG) + 16 * JG)
                    for h in range(GH):
                        pe.wait_ge(s_taken, i * GH + h)
                        for j in range(JG):
                            m = nc.tensor.matmul(ps_src[h % 2][:, j * P:(j + 1) * P],
                                                 rows[:, j, D + h:D + h + 1].to_broadcast([P, P]), k.ident[:],
                                                 start=True, stop=True)
                        m.then_inc(s_src, 1)

        @block.vector
        def _(dve):
            with where_far(dve):
                dve.wait_ge(s_table, 16)
                link = Chain(dve, s_link)
                link(nc.vector.tensor_copy(top[:], k.agg[:, :, D:ROW]))
                base, per = link.n, 2 + GH
                with dve.Fori(0, ITEMS) as i:
                    b = block_of(dve, i)
                    link.n = i * per + base
                    dve.wait_ge(s_dst, i * 16 + 16)
                    link(nc.vector.tensor_scalar(outside[:], dst_all[:], k.node_id[:, bass.ds(b, 1)], None, ALU.is_equal))
                    link(nc.vector.tensor_scalar(outside[:], outside[:], BIG, -BIG, ALU.mult, ALU.add))
                    for h in range(GH):
                        dve.wait_ge(s_src, i * GH + (h + 1))
                        nc.vector.tensor_tensor(masked[:], ps_src[h % 2][:], outside[:], ALU.add).then_inc(s_taken, 1)
                        dve.wait_ge(s_taken, i * GH + (h + 1))
                        link(nc.vector.tensor_reduce(item_max[:, h:h + 1], masked[:], AX_X, ALU.max))
                    nc.vector.tensor_tensor(top[:, b, :], top[:, b, :], item_max[:], ALU.max).then_inc(s_item, 1)
                    dve.wait_ge(s_item, i + 1)
                link.n = base + per * ITEMS
                am, bound = k.node_am[:, :, 0:GH], k.node_am[:, :, GH:2 * GH]
                link(nc.vector.tensor_tensor(z[:], am, top[:], ALU.add))
                link(nc.vector.scalar_tensor_tensor(out=bound, in0=z[:], scalar=SLOPE, in1=z[:], op0=ALU.mult, op1=ALU.max))
                link(nc.vector.tensor_tensor(z[:], am, k.agg[:, :, D:ROW], ALU.add))
                link(nc.vector.scalar_tensor_tensor(out=top[:], in0=z[:], scalar=SLOPE, in1=z[:], op0=ALU.mult, op1=ALU.max))
                nc.vector.tensor_tensor(z[:], top[:], bound, ALU.subtract).then_inc(s_z, 1)
                dve.wait_ge(s_w, 1)
                for t0, t1 in ((0, 13), (13, TILES)):
                    hv = k.agg[:, t0:t1, 0:D].rearrange("p t (h d) -> p t h d", h=GH)
                    link(nc.vector.tensor_tensor(hv, hv, top[:, t0:t1, :].unsqueeze(3).to_broadcast([P, t1 - t0, GH, GHD]),
                                                 ALU.mult))
                link(nc.vector.tensor_copy(k.agg[:, :, D:ROW], top[:]))

        @block.scalar
        def _(act):
            with where_far(act):
                act.wait_ge(s_z, 1)
                nc.scalar.activation(top[:], z[:], ACT.Exp).then_inc(s_w, 1)


def graph_items(nc, k, a):
    with ExitStack() as own, nc.Block() as block:
        def sb(name, shape, dt=F32):
            return own.enter_context(nc.sbuf_tensor(name, shape, dt))

        def sem(name):
            return own.enter_context(nc.semaphore(name))

        rows = sb("rows", [P, GRING, JG, ROW])
        index = sb("index", [P, 2, JG, GRING], I32)
        dst_all = sb("dst_all", [P, GRING, EG])
        sel = sb("sel", [P, RING, JG, P])
        sel_t = sb("sel_t", [P, RING, EG])
        wx = sb("wx", [P, RING, JG, ROW])
        z = sb("z", [P, RING, 4, JG, GH])
        ps_am = [own.enter_context(nc.psum_tensor(f"ps_am{i}", [P, JG, 2 * GH], F32)) for i in range(RING)]
        ps_sum = [own.enter_context(nc.psum_tensor(f"ps_sum{i}", [P, ROW], F32)) for i in range(RING)]

        s_row = [sem(f"s_row{i}") for i in range(GRING)]
        s_dst = [sem(f"s_dst{i}") for i in range(GRING)]
        s_turn_sp = sem("s_turn_sp")
        s_index, s_rows_in, s_dst_in = sem("s_index"), sem("s_rows_in"), sem("s_dst_in")
        s_sel, s_sel_t, s_abs, s_am, s_link, s_z, s_w, s_wx, s_sum, s_add = (
            sem(n) for n in ("s_sel", "s_sel_t", "s_abs", "s_am", "s_link", "s_z", "s_w", "s_wx", "s_sum", "s_add"))

        def groups(eng, passed, begin, issue, landed):
            def turn(m, par, slots=GRING, first=False):
                if not first:
                    word = eng.value_load(k.need[0:1, bass.ds(m, 1)], min_val=0, max_val=(1 << NEED_BITS * NEED_PER) - 1)
                for slot in range(slots):
                    if not first:
                        eng.wait_ge(s_wx, (word >> (NEED_BITS * slot)) & ((1 << NEED_BITS) - 1))
                        eng.sem_inc(passed, 1)
                    if slot == 0:
                        begin(m, par)
                    issue(m * GRING + slot, slot, par)
                    if slot or not first:
                        landed((slot - 1) % GRING, m - (slot == 0))
            turns = GROUPS // GRING
            turn(0, 0, first=True)
            by_pairs(eng, 1, turns, turn)
            turn(turns, turns % 2, GROUPS % GRING)
            landed((GROUPS - 1) % GRING, (GROUPS - 1) // GRING)

        @block.gpsimd
        def _(pool):
            def indices(m, par):
                n = GROUPS % GRING if isinstance(m, int) and m == GROUPS // GRING else GRING
                nc.gpsimd.tensor_copy(index[:, par, :, 0:n], k.src_i[:, :, bass.ds(m * GRING, n)]).then_inc(s_index, 1)
                pool.wait_ge(s_index, m + 1)
                pool.sem_inc(k.s_passed, 1)

            def gather(g, slot, par):
                for j in range(JG):
                    nc.gpsimd.indirect_dma_start(rows[:, slot, j, :], None, k.table, bass.IndirectOffsetOnAxis(
                        ap=index[:, par, j, slot:slot + 1], axis=0)).then_inc(s_row[slot], 16)
            groups(pool, k.s_passed, indices, gather, lambda slot, turn: None)

        @block.sync
        def _(sp):
            def spread(g, slot, _):
                sp.dma_start(dst_all[:, slot, :], k.dst_f[bass.ds(g, 1), :].to_broadcast([P, EG])).then_inc(s_dst[slot], 16)

            def landed(slot, turn):
                sp.wait_ge(s_dst[slot], (turn + 1) * 16)
                sp.sem_inc(s_dst_in, 1)
                sp.wait_ge(s_row[slot], (turn + 1) * (16 * JG))
                sp.sem_inc(s_rows_in, 1)
            groups(sp, s_turn_sp, lambda m, par: None, spread, landed)

        def blocks(eng, i, lo):
            words, found = {}, {}

            def block(n):
                at = (n - lo) // FIELDS
                if at not in words:
                    words[at] = eng.value_load(k.items[0:1, bass.ds(i + (lo + at * FIELDS + BACK + 1), 1)], min_val=0,
                                               max_val=(1 << BLOCK_BITS * FIELDS) - 1)
                if n not in found:
                    found[n] = field(nc, eng, words[at], BLOCK_BITS * ((n - lo) % FIELDS), TILES - 1)
                return found[n]
            return block

        def group(eng, i, b):
            return within(nc, eng, (i - b) & ((1 << GROUPS.bit_length()) - 1), GROUPS - 1)

        @block.vector
        def _(dve):
            def select_t(i, s, g, slot, b):
                dve.wait_ge(s_dst_in, g + 1)
                after(dve, s_am, i - 2)
                nc.vector.tensor_scalar(sel_t[:, s, :], dst_all[:, slot, :], k.node_id[:, bass.ds(b, 1)], None,
                                        ALU.is_equal).then_inc(s_sel_t, 1)

            def weigh(i, s, slot):
                dve.wait_ge(s_w, i + 1)
                nc.vector.tensor_tensor(
                    wx[:, s, :, 0:D].rearrange("p j (h d) -> p j h d", h=GH),
                    rows[:, slot, :, 0:D].rearrange("p j (h d) -> p j h d", h=GH),
                    wx[:, s, :, D:ROW].unsqueeze(3).to_broadcast([P, JG, GH, GHD]), ALU.mult).then_inc(s_wx, 1)

            def add(i, s, b):
                dve.wait_ge(s_sum, i + 1)
                after(dve, s_add, i)
                nc.vector.tensor_tensor(k.agg[:, b, :], k.agg[:, b, :], ps_sum[s][:], ALU.add).then_inc(s_add, 1)

            def step(i, s, b, back=BACK, ahead=True):
                g = group(dve, i, b(0))
                zz = z[:, s]
                dve.wait_ge(s_rows_in, g + 1)
                dve.wait_ge(s_am, i + 1)
                nc.vector.tensor_tensor(zz[:, 0], rows[:, g & (GRING - 1), :, D:ROW], ps_am[s][:, :, 0:GH],
                                        ALU.add).then_inc(s_link, 1)
                dve.wait_ge(s_link, i * 3 + 1)
                nc.vector.scalar_tensor_tensor(out=zz[:, 1], in0=zz[:, 0], scalar=SLOPE, in1=zz[:, 0], op0=ALU.mult,
                                               op1=ALU.max).then_inc(s_link, 1)
                dve.wait_ge(s_link, i * 3 + 2)
                nc.vector.tensor_tensor(zz[:, 2], zz[:, 1], ps_am[s][:, :, GH:2 * GH], ALU.subtract).then_inc(s_link, 1)
                dve.wait_ge(s_link, i * 3 + 3)
                nc.vector.tensor_scalar(zz[:, 3], zz[:, 2], 0.0, None, ALU.min).then_inc(s_z, 1)
                if back:
                    weigh(i - 1, (s - 1) % RING, group(dve, i - 1, b(-1)) & (GRING - 1))
                if back == BACK:
                    add(i - 2, (s - 2) % RING, b(-2))
                if ahead:
                    g = group(dve, i + 2, b(2))
                    select_t(i + 2, (s + 2) % RING, g, g & (GRING - 1), b(2))

            def turn(m):
                b = blocks(dve, m, -BACK)
                for n in range(UNROLL):
                    step(m + n, n % RING, lambda at: b(n + at))
            b = blocks(dve, 0, -1)
            select_t(0, 0, 0, 0, 0)
            g = group(dve, 1, b(1))
            select_t(1, 1, g, g & (GRING - 1), b(1))
            for i in range(UNROLL):
                step(i, i % RING, lambda at: b(i + at), back=min(i, BACK))
            by_turns(dve, turn)
            end = ITEMS - BACK
            b = blocks(dve, end, -BACK)
            for n in range(BACK):
                step(end + n, n, lambda at: b(n + at), ahead=False)
            weigh(end + 1, 1, group(dve, end + 1, b(1)) & (GRING - 1))
            add(end, 0, b(0))
            add(end + 1, 1, TILES - 1)

        @block.scalar
        def _(act):
            def select(i, s, g, b):
                after(act, s_sum, i - 2)
                for j in range(JG):
                    m = nc.scalar.activation(sel[:, s, j, :], k.iota_n[:, bass.ds(b * P, P)], ACT.Abs, scale=-1.0,
                                             bias=k.dst_e[:, j, bass.ds(g, 1)])
                m.then_inc(s_abs, 1)
                act.wait_ge(s_abs, i + 1)
                nc.scalar.activation(sel[:, s], sel[:, s], ACT.Relu, scale=-1.0, bias=k.ones[:, 0:1]).then_inc(s_sel, 1)

            def weights(i, s):
                act.wait_ge(s_z, i + 1)
                nc.scalar.activation(wx[:, s, :, D:ROW], z[:, s, 3], ACT.Exp).then_inc(s_w, 1)

            def step(i, s, b):
                weights(i, s)
                select(i + 2, (s + 2) % RING, group(act, i + 2, b(2)), b(2))

            def turn(m):
                b = blocks(act, m, BACK)
                for n in range(UNROLL):
                    step(m + n, n % RING, lambda at: b(n + at))
            b = blocks(act, 0, 1)
            select(0, 0, 0, 0)
            select(1, 1, group(act, 1, b(1)), b(1))
            for i in range(UNROLL):
                step(i, i % RING, lambda at: b(i + at))
            by_turns(act, turn)
            for i in range(ITEMS - BACK, ITEMS):
                weights(i, i % RING)

        @block.tensor
        def _(pe):
            def shares(i, s, b):
                pe.wait_ge(s_sel_t, i + 1)
                after(pe, s_z, i - 2)
                for j in range(JG):
                    m = nc.tensor.matmul(ps_am[s][:, j, :], sel_t[:, s, j * P:(j + 1) * P], k.node_am[:, b, :], start=True,
                                         stop=True)
                m.then_inc(s_am, 1)

            def sums(i, s):
                pe.wait_ge(s_wx, i + 1)
                pe.wait_ge(s_sel, i + 1)
                after(pe, s_add, i - 2)
                for j in range(JG):
                    m = nc.tensor.matmul(ps_sum[s][:], sel[:, s, j, :], wx[:, s, j, :], start=(j == 0), stop=(j == JG - 1))
                m.then_inc(s_sum, 1)

            def step(i, s, b):
                sums(i - 1, (s - 1) % RING)
                shares(i + 2, (s + 2) % RING, b(2))

            def turn(m):
                b = blocks(pe, m, BACK)
                for n in range(UNROLL):
                    step(m + n, n % RING, lambda at: b(n + at))
            b = blocks(pe, 0, 1)
            shares(0, 0, 0)
            shares(1, 1, b(1))
            shares(2, 2, b(2))
            for i in range(1, UNROLL):
                step(i, i % RING, lambda at: b(i + at))
            by_turns(pe, turn)
            for i in range(ITEMS - BACK - 1, ITEMS):
                sums(i, i % RING)


def feed_forward(nc, sb, ps, sem, n, width, name, gelu, weights, b1, xin, s_xin, gain, words=None):
    f = Names()
    step_rows = width * P
    half = HB // 2
    xe = sb(name + "_xe", [P, KT, step_rows])
    xh, xl = (sb(name + v, [P, 2, KT, step_rows], BF16) for v in ("_xh", "_xl"))
    hf = sb(name + "_hf", [P, 2, half, step_rows])
    hh, hl = (sb(name + v, [P, 2, HB, step_rows], BF16) for v in ("_hh", "_hl"))
    ps_x = ps(name + "_ps_x", [P, KT, step_rows])
    f.ps_h = ps_h = [ps(f"{name}_ps_h{i}", [P, half, step_rows]) for i in range(2)]
    f.ps_y = [ps(f"{name}_ps_y{i}", [P, width, D]) for i in range(2)]
    s_turned, s_gained, s_xhi, s_x, s_up, s_gelu, s_hhi, s_h = (
        sem(name + v) for v in ("_turned", "_gained", "_xhi", "_x", "_up", "_gelu", "_hhi", "_h"))
    f.s_down, f.s_y, f.s_turned = sem(name + "_down"), sem(name + "_y"), s_turned

    def word(eng, i):
        return None if words is None else words(eng, i)

    def turn(pe, i, par):
        pe.wait_ge(s_xin, i + 1)
        after(pe, s_x, i)
        for kt in range(KT):
            for w in range(width):
                m = nc.tensor.transpose(ps_x[:, kt, w * P:(w + 1) * P], xin[:, par, w, kt * P:(kt + 1) * P], f.ident)
        m.then_inc(s_turned, 1)

    def up(pe, i, par, w):
        pe.wait_ge(s_x, i + 1)
        for q in range(2):
            after(pe, s_gelu, i * 2 + (q - 1))
            for b in range(q * half, (q + 1) * half):
                steps = [(w.w1h, xh, kt) for kt in range(KT)] + [(w.w1h, xl, kt) for kt in range(KT)] + [
                    (w.w1l, xh, kt) for kt in range(KT)]
                for c, (w1, xx, kt) in enumerate(steps):
                    m = nc.tensor.matmul(ps_h[q][:, b - q * half, :], w1[:, kt, b, :], xx[:, par, kt, :], start=(c == 0),
                                         stop=(c == len(steps) - 1))
            m.then_inc(s_up, 1)

    def down(pe, i, par, w):
        after(pe, f.s_y, i - 1)
        pe.wait_ge(s_h, i * 2 + 2)
        steps = [(hx, w2, b) for b in range(HB) for hx, w2 in ((hh, w.w2h), (hh, w.w2l), (hl, w.w2h))]
        for v in range(width):
            for c, (hx, w2, b) in enumerate(steps):
                m = nc.tensor.matmul(f.ps_y[par][:, v, :], hx[:, par, b, v * P:(v + 1) * P], w2[:, b, :], start=(c == 0),
                                     stop=(c == len(steps) - 1))
        m.then_inc(f.s_down, 1)

    def pe_program(pe):
        def step(i, par, own, last):
            turn(pe, i + 1, 1 - par)
            up(pe, i, par, own)
            down(pe, i - 1, 1 - par, last)

        def steps(i, par, count):
            by_step = weights(pe, word(pe, i))
            for c in range(count):
                step(i + c, (par + c) % 2, by_step[OWN + c], by_step[LAST + c])
        turn(pe, 0, 0)
        turn(pe, 1, 1)
        up(pe, 0, 0, weights(pe, word(pe, 0))[OWN])
        steps(1, 1, 2)
        with pe.Fori(1, (n - 2) // 2) as m:
            steps(m * 2 + 1, 1, 2)
        if n % 2:
            steps(n - 2, 1, 1)
        by_step = weights(pe, word(pe, n - 1))
        up(pe, n - 1, (n - 1) % 2, by_step[OWN])
        down(pe, n - 2, n % 2, by_step[LAST])
        down(pe, n - 1, (n - 1) % 2, by_step[OWN])

    def act_program(act):
        def step(i, par):
            bias = b1(act, word(act, i))
            for q in range(2):
                act.wait_ge(s_up, i * 2 + (1 + q))
                after(act, s_h, i * 2 + (q - 1))
                for b in range(half):
                    m = nc.scalar.activation(hf[:, q, b, :], ps_h[q][:, b, :], gelu, bias=bias[:, q * half + b:q * half + b + 1])
                m.then_inc(s_gelu, 1)
                act.wait_ge(s_gelu, i * 2 + (1 + q))
                if q == 0:
                    after(act, f.s_down, i - 1)
                nc.scalar.copy(hh[:, par, q * half:(q + 1) * half], hf[:, q]).then_inc(s_hhi, 1)
        for i in range(3):
            step(i, i % 2)
        by_pairs(act, 3, n, step)

    def split_x(dve, i, par, w, which=NEXT):
        dve.wait_ge(s_turned, i + 1)
        after(dve, s_up, i * 2 - 2)
        from_ = ps_x
        if gain is not None:
            g, b = gain(dve, w, which)
            for kt in range(KT):
                m = nc.vector.tensor_scalar(xe[:, kt, :], ps_x[:, kt, :], g[:, kt:kt + 1], b[:, kt:kt + 1], ALU.mult, ALU.add)
            m.then_inc(s_gained, 1)
            dve.wait_ge(s_gained, i + 1)
            from_ = xe
        nc.vector.tensor_copy(xh[:, par], from_[:]).then_inc(s_xhi, 1)
        dve.wait_ge(s_xhi, i + 1)
        nc.vector.tensor_tensor(xl[:, par], from_[:], xh[:, par], ALU.subtract).then_inc(s_x, 1)

    def split_h(dve, i, par):
        for q in range(2):
            dve.wait_ge(s_hhi, i * 2 + (1 + q))
            nc.vector.tensor_tensor(hl[:, par, q * half:(q + 1) * half], hf[:, q], hh[:, par, q * half:(q + 1) * half],
                                    ALU.subtract).then_inc(s_h, 1)

    def dve_program(dve, before, leave):
        def step(i, par, ahead=True):
            w = word(dve, i)
            if ahead:
                before(i + 2, par)
            split_x(dve, i + 1, 1 - par, w)
            split_h(dve, i, par)
            leave(i - 1, 1 - par, w, LAST)
        before(0, 0)
        before(1, 1)
        w = word(dve, 0)
        split_x(dve, 0, 0, w, OWN)
        split_x(dve, 1, 1, w)
        before(2, 0)
        split_h(dve, 0, 0)
        for i in (1, 2):
            step(i, i % 2)
        by_pairs(dve, 3, n - 2, step)
        step(n - 2, n % 2, ahead=False)
        w = word(dve, n - 1)
        split_h(dve, n - 1, (n - 1) % 2)
        leave(n - 2, n % 2, w, LAST)
        leave(n - 1, (n - 1) % 2, w, OWN)

    f.pe, f.act, f.dve = pe_program, act_program, dve_program
    return f


def row_sums(nc, dve, link, t, src):
    if src is not None:
        def one(i):
            nc.vector.bn_stats(t.stats[:, i, :], src[:, i, 0:D])
        by_many(dve, 0, TILES - 1, one)
        link(nc.vector.bn_stats(t.stats[:, TILES - 1, :], src[:, TILES - 1, 0:D]))
    link(nc.vector.tensor_tensor(t.a[:], t.stats[:, :, 1], t.stats[:, :, 4], ALU.subtract))
    link(nc.vector.tensor_tensor(t.a[:], t.a[:], t.a[:], ALU.mult))
    link(nc.vector.tensor_tensor(t.b[:], t.stats[:, :, 2], t.stats[:, :, 5], ALU.add))
    link(nc.vector.scalar_tensor_tensor(out=t.sq[:], in0=t.a[:], scalar=D / 4.0, in1=t.b[:], op0=ALU.mult, op1=ALU.add))
    link(nc.vector.tensor_tensor(t.mean[:], t.stats[:, :, 1], t.stats[:, :, 4], ALU.add))
    link(nc.vector.tensor_scalar(t.mean[:], t.mean[:], 0.5, None, ALU.mult))


def row_stats(nc, dve, link, t, src, n):
    row_sums(nc, dve, link, t, src)
    link(nc.vector.tensor_scalar(t.var[:], t.sq[:], 1.0 / D, EPS, ALU.mult, ALU.add))
    nc.vector.tensor_copy(t.root[:], t.var[:]).then_inc(t.s_var, 1)
    dve.wait_ge(t.s_root, n)
    link(nc.vector.reciprocal(t.a[:], t.root[:]))
    link(nc.vector.tensor_tensor(t.a[:], t.a[:], t.var[:], ALU.mult))
    link(nc.vector.tensor_tensor(t.a[:], t.a[:], t.root[:], ALU.add))
    link(nc.vector.reciprocal(t.rstd[:], t.a[:]))
    link(nc.vector.tensor_scalar(t.rstd[:], t.rstd[:], 2.0, None, ALU.mult))


def roots(nc, act, t, first, count):
    for n in range(first, first + count):
        act.wait_ge(t.s_var, n)
        nc.scalar.activation(t.root[:], t.root[:], ACT.Sqrt).then_inc(t.s_root, 1)


def stat_tiles(sb, sem, name, stats=None):
    t = Names()
    t.stats = sb(name + "_stats", [P, TILES, 6]) if stats is None else stats
    t.s_var, t.s_root = sem(name + "_s_var"), sem(name + "_s_root")
    t.a, t.b, t.sq, t.var, t.root, t.mean, t.rstd, t.scale = (
        sb(name + "_" + v, [P, TILES]) for v in ("a", "b", "sq", "var", "root", "mean", "rstd", "scale"))
    return t


def nodes_finish(nc, k, a):
    with ExitStack() as own, nc.Block() as block:
        def sb(name, shape, dt=F32):
            return own.enter_context(nc.sbuf_tensor(name, shape, dt))

        def ps(name, shape):
            return own.enter_context(nc.psum_tensor(name, shape, F32))

        def sem(name):
            return own.enter_context(nc.semaphore(name))

        raw1 = sb("raw1", [P, KT, HID])
        raw2 = sb("raw2", [P, HB, D])
        w = Weights(sb("w1h", [P, KT, HB, P], BF16), sb("w1l", [P, KT, HB, P], BF16),
                    sb("w2h", [P, HB, D], BF16), sb("w2l", [P, HB, D], BF16))
        b1 = sb("fb1", [P, HB])
        t = stat_tiles(sb, sem, "fin")
        xin = sb("xin", [P, 2, 1, D])
        rden = sb("rden", [P, TILES, GH])
        squares = sb("squares", [P, 2, D])
        norm = sb("norm", [P, TILES])
        s_w, s_whi, s_split, s_link, s_xin = (
            sem(n) for n in ("f_w", "f_whi", "f_split", "f_link", "f_xin"))
        s_qcopy, s_qt, s_qt_out, s_mix, s_mix_out, s_norm, s_acc = (
            sem(n) for n in ("f_qcopy", "f_qt", "f_qt_out", "f_mix", "f_mix_out", "f_norm", "f_acc"))
        f = feed_forward(nc, sb, ps, sem, TILES, 1, "g", ACT.Gelu_apprx_tanh, lambda eng, _: (w, w, w), lambda eng, _: b1, xin, s_xin, None)
        f.ident = k.ident[:]
        ps_mix = f.ps_h
        qs, qt = xin, sb("qt", [P, 2, P])

        @block.sync
        def _(sp):
            sp.dma_start(raw1[:], a.f_w1.rearrange("(k p) h -> p k h", p=P)).then_inc(s_w, 16)
            sp.dma_start(raw2[:], a.f_w2.rearrange("(p b) d -> p b d", b=HB)).then_inc(s_w, 16)
            sp.dma_start(b1[:], a.f_b1.rearrange("(p b) -> p b", b=HB)).then_inc(s_w, 16)

        @block.gpsimd
        def _(pool):
            def query(i, par):
                after(pool, s_qt, i - 1)
                pool.sem_inc(k.s_passed, 1)
                nc.gpsimd.tensor_copy(qs[:, par, 0, 0:P], k.q[:, i, :]).then_inc(s_qcopy, 1)
            query(0, 0)
            query(1, 1)
            by_pairs(pool, 2, TILES, query)

        @block.tensor
        def _(pe):
            def turn(i, par):
                pe.wait_ge(s_qcopy, i + 1)
                after(pe, s_qt_out, i - 1)
                nc.tensor.transpose(f.ps_y[par][:, 0, 0:P], qs[:, par, 0, 0:P], k.ident[:]).then_inc(s_qt, 1)

            def mix(i, par):
                pe.wait_ge(s_qt_out, i + 1)
                after(pe, s_mix_out, i - 1)
                nc.tensor.matmul(ps_mix[par][:, 0:KT, :], qt[:, par, :], k.cw[:], start=True, stop=True).then_inc(s_mix, 1)

            def step(i, par):
                turn(i + 1, 1 - par)
                mix(i, par)
            turn(0, 0)
            step(0, 0)
            step(1, 1)
            by_pairs(pe, 2, TILES - 1, step)
            mix(TILES - 1, (TILES - 1) % 2)
            pe.wait_ge(s_mix_out, TILES)
            pe.wait_ge(s_split, 4)
            f.pe(pe)

        @block.scalar
        def _(act):
            def out(i, par):
                act.wait_ge(s_qt, i + 1)
                after(act, s_mix, i - 1)
                nc.scalar.copy(qt[:, par, :], f.ps_y[par][:, 0, 0:P]).then_inc(s_qt_out, 1)

            def mixed(i, par):
                act.wait_ge(s_mix, i + 1)
                rows = ps_mix[par][:, 0:KT, :].rearrange("p a b -> p (a b)")
                nc.scalar.copy(k.xn0[:, i, :], rows)
                after(act, s_mix_out, i - 1)
                nc.scalar.activation(squares[:, par, :], rows, ACT.Square, accum_out=norm[:, bass.ds(i, 1)]).then_inc(s_mix_out, 1)

            def tile(i, par):
                out(i, par)
                mixed(i - 1, 1 - par)
            out(0, 0)
            half = TILES // 4 * 2 + 1
            tile(1, 1)
            tile(2, 0)
            by_pairs(act, 3, half, tile)
            roots(nc, act, t, 1, 1)
            act.wait_ge(s_w, 48)
            nc.scalar.copy(w.w1h[:], raw1[:].rearrange("p k (m b) -> p k b m", b=HB)).then_inc(s_whi, 1)
            nc.scalar.copy(w.w2h[:], raw2[:]).then_inc(s_whi, 1)
            by_pairs(act, half, TILES - 1, tile)
            out(TILES - 1, (TILES - 1) % 2)
            mixed(TILES - 2, TILES % 2)
            mixed(TILES - 1, (TILES - 1) % 2)
            act.wait_ge(s_mix_out, TILES)
            nc.scalar.activation(norm[:], norm[:], ACT.Sqrt).then_inc(s_norm, 1)
            f.act(act)

        @block.vector
        def _(dve):
            link = Chain(dve, s_link)
            link(nc.vector.reciprocal(rden[:], k.agg[:, :, D:ROW]))
            for t0, t1 in ((0, 13), (13, TILES)):
                hv = k.agg[:, t0:t1, 0:D].rearrange("p t (h d) -> p t h d", h=GH)
                link(nc.vector.tensor_tensor(hv, hv, rden[:, t0:t1, :].unsqueeze(3).to_broadcast([P, t1 - t0, GH, GHD]),
                                             ALU.mult))
            link(nc.vector.tensor_tensor(k.agg[:, :, 0:D], k.agg[:, :, 0:D], k.res[:], ALU.add))
            row_stats(nc, dve, link, t, k.agg, 1)

            def graph_norm(i):
                nc.vector.tensor_scalar(k.agg[:, i, 0:D], k.agg[:, i, 0:D], t.mean[:, bass.ds(i, 1)],
                                        t.rstd[:, bass.ds(i, 1)], ALU.subtract, ALU.mult)
            by_many(dve, 0, TILES - 1, graph_norm)
            i = TILES - 1
            link(nc.vector.tensor_scalar(k.agg[:, i, 0:D], k.agg[:, i, 0:D], t.mean[:, i:i + 1], t.rstd[:, i:i + 1],
                                         ALU.subtract, ALU.mult))
            dve.wait_ge(s_whi, 2)
            link(nc.vector.tensor_tensor(w.w1l[:], raw1[:].rearrange("p k (m b) -> p k b m", b=HB), w.w1h[:], ALU.subtract))
            nc.vector.tensor_tensor(w.w2l[:], raw2[:], w.w2h[:], ALU.subtract).then_inc(s_split, 4)

            dve.wait_ge(s_norm, 1)
            link(nc.vector.tensor_scalar(norm[:], norm[:], 1e-12, None, ALU.max))
            link(nc.vector.reciprocal(norm[:], norm[:]))
            link(nc.vector.tensor_scalar(norm[:], norm[:], float(D) ** 0.5, None, ALU.mult))
            dve.wait_ge(s_qt, TILES)

            base = link.n

            def before(i, par):
                link.n = i * 3 + base
                after(dve, f.s_turned, i - 1)
                link(nc.vector.tensor_tensor(k.agg[:, i, 0:D], k.agg[:, i, 0:D], k.g2[:], ALU.mult))
                nc.vector.tensor_tensor(xin[:, par, 0, :], k.agg[:, i, 0:D], k.b2n[:], ALU.add).then_inc(s_xin, 1)
                link(nc.vector.scalar_tensor_tensor(out=k.xn0[:, i, :], in0=k.xn0[:, i, :], scalar=norm[:, bass.ds(i, 1)],
                                                    in1=k.gout[:], op0=ALU.mult, op1=ALU.mult))
                link(nc.vector.tensor_tensor(k.acc[:, i, :], k.acc[:, i, :], k.xn0[:, i, :], ALU.add))
                dve.wait_ge(s_xin, i + 1)
                nc.vector.tensor_tensor(k.acc[:, i, :], k.acc[:, i, :], xin[:, par, 0, :], ALU.add).then_inc(s_acc, 1)

            def leave(i, par, *_):
                dve.wait_ge(f.s_down, i + 1)
                dve.wait_ge(s_acc, i + 1)
                nc.vector.tensor_tensor(k.acc[:, i, :], k.acc[:, i, :], f.ps_y[par][:, 0, :], ALU.add).then_inc(f.s_y, 1)
                if not (isinstance(i, int) and i == 0):
                    stats(i - 1)

            def stats(i):
                dve.wait_ge(f.s_y, i + 1)
                nc.vector.bn_stats(k.acc_stats[:, i, :], k.acc[:, i, :])
            f.dve(dve, before, leave)
            stats(TILES - 1)


def route(nc, k, a):
    with ExitStack() as own, nc.Block() as block:
        def sb(name, shape, dt=F32):
            return own.enter_context(nc.sbuf_tensor(name, shape, dt))

        def ps(name, shape):
            return own.enter_context(nc.psum_tensor(name, shape, F32))

        def sem(name):
            return own.enter_context(nc.semaphore(name))

        raw1 = [sb(f"r_raw1{i}", [P, KT, HID]) for i in range(2)]
        raw2 = [sb(f"r_raw2{i}", [P, HB, D]) for i in range(2)]
        wr = sb("wr", [P, KT, EXP])
        br = sb("br", [P, EXP])
        t = stat_tiles(sb, sem, "r1", k.acc_stats)
        t2 = stat_tiles(sb, sem, "r2")
        xt = sb("xt", [P, 2, D])
        xt_t = sb("xt_t", [P, 2, KT, P])
        xn = sb("xn", [P, 2, D])
        index = sb("r_index", [P, 2, TOPK], I32)
        logit, eq, enc, o1, o2, both, rank, total, incl = (
            sb("r_" + n, [P, TILES, EXP]) for n in ("logit", "eq", "enc", "o1", "o2", "both", "rank", "total", "incl"))
        best = sb("best", [P, 3, TILES])
        rev = sb("rev", [P, EXP])
        lower = sb("lower", [P, P])
        tile_no = sb("tile_no", [P, P])
        per_e = sb("per_e", [P, 6, EXP])
        per_ei = sb("per_ei", [P, EXP], I32)
        cmp = sb("cmp", [1, MOE_STEPS, EXP - 1])
        expert_f = sb("expert_f", [1, MOE_STEPS])
        word_f = sb("word_f", [1, MOE_STEPS])
        place_f = sb("place_f", [P, TILES, TOPK])
        zero = sb("zero", [P, TILES])
        ps_t = [ps(f"r_ps_t{i}", [P, KT, P]) for i in range(2)]
        ps_l = ps("r_ps_l", [P, TILES, EXP])
        ps_r = ps("r_ps_r", [P, TILES, EXP])
        ps_n = ps("r_ps_n", [P, TILES, EXP])

        s_small, s_iota, s_link, s_xt, s_turned, s_xt_t, s_logit, s_exp_in, s_exp, s_both, s_rank = (
            sem(n) for n in ("r_small", "r_iota", "r_link", "r_xt", "r_turned", "r_xt_t", "r_logit", "r_exp_in", "r_exp",
                             "r_both", "r_rank"))
        s_place, s_xn, s_idx = sem("r_place"), sem("r_xn"), sem("r_idx")
        s_put = [sem(f"r_put{i}") for i in range(2)]
        s_raw1 = [sem(f"r_s_raw1{i}") for i in range(2)]
        s_raw2 = [sem(f"r_s_raw2{i}") for i in range(2)]
        s_const = sem("r_const")
        s_hi1, s_hi2, s_lo1, s_lo2 = (sem(n) for n in ("r_hi1", "r_hi2", "r_lo1", "r_lo2"))

        @block.sync
        def _(sp):
            sp.dma_start(wr[:], a.e_Wr.rearrange("(k p) e -> p k e", p=P)).then_inc(s_small, 16)
            sp.dma_start(br[:], row_on_all(a.e_br)).then_inc(s_small, 16)

            def load(e, par):
                after(sp, s_lo1, e - 1)
                sp.dma_start(raw1[par][:], a.e_W1[bass.ds(e, 1), :, :].rearrange("e (k p) h -> p (e k) h", p=P)).then_inc(
                    s_raw1[par], 16)
                after(sp, s_lo2, e - 1)
                sp.dma_start(raw2[par][:], a.e_W2[bass.ds(e, 1), :, :].rearrange("e (p b) d -> p (e b) d", b=HB)).then_inc(
                    s_raw2[par], 16)
            load(0, 0)
            load(1, 1)
            by_pairs(sp, 2, EXP, load)
            for n, v in enumerate((a.e_lng, a.e_lnb)):
                for e in range(EXP):
                    sp.dma_start(k.ln_cols[:, e, n, :], cols(v[e])).then_inc(s_const, 16)
            sp.dma_start(k.b1[:], a.e_b1.rearrange("e (p b) -> p e b", b=HB)).then_inc(s_const, 16)
            sp.wait_ge(s_const, 16 * (2 * EXP + 1))

        @block.gpsimd
        def _(pool):
            nc.gpsimd.iota(tile_no[:], pattern=[[1, P]], base=0, channel_multiplier=0,
                           allow_small_or_imprecise_dtypes=True).then_inc(s_iota, 1)
            nc.gpsimd.iota(rev[:], pattern=[[-1, EXP]], base=EXP, channel_multiplier=0,
                           allow_small_or_imprecise_dtypes=True).then_inc(s_iota, 1)
            nc.gpsimd.memset(zero[:], 0.0).then_inc(s_iota, 1)
            pool.wait_ge(s_place, 1)

            def put(i, par):
                after(pool, s_put[par], i * 16 - 16 * par)
                pool.sem_inc(k.s_passed, 1)
                nc.gpsimd.tensor_copy(index[:, par, :], k.place_i[:, i, :]).then_inc(s_idx, 1)
                pool.wait_ge(s_idx, i + 1)
                pool.sem_inc(k.s_passed, 1)
                pool.wait_ge(s_xn, i + 1)
                pool.sem_inc(k.s_passed, 1)
                for c in range(TOPK):
                    nc.gpsimd.indirect_dma_start(k.rows_in, bass.IndirectOffsetOnAxis(ap=index[:, par, c:c + 1], axis=0),
                                                 xn[:, par, :], None).then_inc(s_put[par], 16)
            put(0, 0)
            put(1, 1)
            by_pairs(pool, 2, TILES, put, per=6)
            pool.wait_ge(s_put[0], 32 * (TILES - TILES // 2))
            pool.wait_ge(s_put[1], 32 * (TILES // 2))

        @block.scalar
        def _(act):
            roots(nc, act, t, 1, 1)

            def out(i, par):
                act.wait_ge(s_turned, i + 1)
                after(act, s_logit, i - 1)
                nc.scalar.copy(xt_t[:, par], ps_t[par][:]).then_inc(s_xt_t, 1)
            out(0, 0)
            out(1, 1)
            by_pairs(act, 2, TILES, out)
            roots(nc, act, t2, 1, 1)

            def high(e, par):
                act.wait_ge(s_raw1[par], e * 8 + (16 - 8 * par))
                nc.scalar.copy(k.w1[:, e, 0], raw1[par][:].rearrange("p k (m b) -> p k b m", b=HB)).then_inc(s_hi1, 1)
                act.wait_ge(s_raw2[par], e * 8 + (16 - 8 * par))
                nc.scalar.copy(k.w2[:, e, 0], raw2[par][:]).then_inc(s_hi2, 1)
            high(0, 0)
            high(1, 1)
            act.wait_ge(s_exp_in, 1)
            nc.scalar.activation(best[:, 2, :], best[:, 2, :], ACT.Exp).then_inc(s_exp, 1)
            by_pairs(act, 2, EXP, high)

        @block.tensor
        def _(pe):
            pe.wait_ge(s_small, 32)

            def turn(i, par):
                pe.wait_ge(s_xt, i + 1)
                after(pe, s_xt_t, i - 1)
                for kt in range(KT):
                    m = nc.tensor.transpose(ps_t[par][:, kt, :], xt[:, par, kt * P:(kt + 1) * P], k.ident[:])
                m.then_inc(s_turned, 1)

            def logits(i, par):
                pe.wait_ge(s_xt_t, i + 1)
                for kt in range(KT):
                    m = nc.tensor.matmul(ps_l[:, i, :], xt_t[:, par, kt, :], wr[:, kt, :], start=(kt == 0),
                                         stop=(kt == KT - 1))
                m.then_inc(s_logit, 1)

            def step(i, par):
                turn(i + 1, 1 - par)
                logits(i, par)
            turn(0, 0)
            step(0, 0)
            step(1, 1)
            by_pairs(pe, 2, TILES - 1, step)
            logits(TILES - 1, (TILES - 1) % 2)
            pe.wait_ge(s_both, 1)
            nc.tensor.matmul(ps_r[:], lower[:], both[:], start=True, stop=True)
            nc.tensor.matmul(ps_n[:], k.ones[:], both[:], start=True, stop=True).then_inc(s_rank, 1)

        @block.vector
        def _(dve):
            link = Chain(dve, s_link)
            row_stats(nc, dve, link, t, None, 1)

            def normed(i, par, to):
                return nc.vector.tensor_scalar(to[:, par, :], k.acc[:, i, :], t.mean[:, bass.ds(i, 1)],
                                               t.rstd[:, bass.ds(i, 1)], ALU.subtract, ALU.mult)

            def tile(i, par):
                after(dve, s_turned, i - 1)
                normed(i, par, xt).then_inc(s_xt, 1)
                dve.wait_ge(s_xt, i + 1)
                nc.vector.bn_stats(t2.stats[:, i, :], xt[:, par, :])
            tile(0, 0)
            tile(1, 1)
            by_pairs(dve, 2, TILES, tile)
            dve.wait_ge(s_iota, 3)
            link(nc.vector.tensor_scalar(lower[:], tile_no[:], k.pidx[:, 0:1], None, ALU.is_gt))
            row_stats(nc, dve, link, t2, None, 1)

            def over_e(v):
                return v.unsqueeze(2).to_broadcast([P, TILES, EXP])

            def over_t(v):
                return v.unsqueeze(1).to_broadcast([P, TILES, EXP])
            dve.wait_ge(s_logit, TILES)
            dve.wait_ge(s_small, 32)
            link(nc.vector.tensor_tensor(logit[:], ps_l[:], over_t(br[:]), ALU.add))
            for c, o in enumerate((o1, o2)):
                link(nc.vector.tensor_reduce(best[:, c, :], logit[:], AX_X, ALU.max))
                link(nc.vector.tensor_tensor(eq[:], logit[:], over_e(best[:, c, :]), ALU.is_equal))
                link(nc.vector.tensor_tensor(enc[:], eq[:], over_t(rev[:]), ALU.mult))
                link(nc.vector.tensor_reduce(best[:, 2, :], enc[:], AX_X, ALU.max))
                link(nc.vector.tensor_tensor(o[:], enc[:], over_e(best[:, 2, :]), ALU.is_equal))
                if c == 0:
                    link(nc.vector.scalar_tensor_tensor(out=logit[:], in0=o[:], scalar=-BIG, in1=logit[:], op0=ALU.mult,
                                                        op1=ALU.add))
            nc.vector.tensor_tensor(both[:], o1[:], o2[:], ALU.add).then_inc(s_both, 1)
            nc.vector.tensor_tensor(best[:, 2, :], best[:, 1, :], best[:, 0, :], ALU.subtract).then_inc(s_exp_in, 1)
            def low1(e, par):
                dve.wait_ge(s_hi1, e + 1)
                nc.vector.tensor_tensor(k.w1[:, e, 1], raw1[par][:].rearrange("p k (m b) -> p k b m", b=HB), k.w1[:, e, 0],
                                        ALU.subtract).then_inc(s_lo1, 1)

            def low2(e, par):
                dve.wait_ge(s_hi2, e + 1)
                nc.vector.tensor_tensor(k.w2[:, e, 1], raw2[par][:], k.w2[:, e, 0], ALU.subtract).then_inc(s_lo2, 1)

            for e in range(2):
                low1(e, e)
                low2(e, e)
            dve.wait_ge(s_exp, 1)
            link(nc.vector.tensor_scalar(best[:, 0, :], best[:, 2, :], 1.0, None, ALU.add))
            link(nc.vector.reciprocal(k.share[:, :, 0], best[:, 0, :]))
            link(nc.vector.tensor_tensor(k.share[:, :, 1], k.share[:, :, 0], best[:, 2, :], ALU.mult))
            dve.wait_ge(s_rank, 1)
            link(nc.vector.tensor_copy(total[:], ps_n[:]))
            for e in range(EXP):
                m = nc.vector.tensor_tensor_scan(incl[:, :, e], total[:, :, e], zero[:], 0.0, ALU.add, ALU.add)
            link(m)
            link(nc.vector.tensor_tensor(rank[:], incl[:], total[:], ALU.subtract))
            link(nc.vector.tensor_tensor(rank[:], rank[:], ps_r[:], ALU.add))
            link(nc.vector.tensor_scalar(per_e[:, 0, :], incl[:, TILES - 1, :], float(MP - 1), None, ALU.add))
            link(nc.vector.tensor_copy(per_ei[:], per_e[:, 0, :]))
            link(nc.vector.tensor_scalar(per_ei[:], per_ei[:], MP.bit_length() - 1, None, ALU.arith_shift_right))
            link(nc.vector.tensor_copy(per_e[:, 1, :], per_ei[:]))
            link(nc.vector.tensor_tensor_scan(per_e[:, 2, :], per_e[:, 1, :], zero[:, 0:EXP], 0.0, ALU.add, ALU.add))
            link(nc.vector.tensor_tensor(per_e[:, 3, :], per_e[:, 2, :], per_e[:, 1, :], ALU.subtract))
            link(nc.vector.tensor_scalar(per_e[:, 4, :], per_e[:, 3, :], float(MP), None, ALU.mult))
            link(nc.vector.tensor_tensor(rank[:], rank[:], over_t(per_e[:, 4, :]), ALU.add))
            for c, o in enumerate((o1, o2)):
                link(nc.vector.tensor_tensor(enc[:], rank[:], o[:], ALU.mult))
                link(nc.vector.tensor_reduce(place_f[:, :, c], enc[:], AX_X, ALU.add))
            nc.vector.tensor_copy(k.place_i[:], place_f[:]).then_inc(s_place, 1)
            link(nc.vector.tensor_tensor(cmp[:], tile_no[0:1, 0:MOE_STEPS].unsqueeze(2).to_broadcast([1, MOE_STEPS, EXP - 1]),
                                         per_e[0:1, 3, 1:EXP].unsqueeze(1).to_broadcast([1, MOE_STEPS, EXP - 1]), ALU.is_ge))
            link(nc.vector.tensor_reduce(expert_f[:], cmp[:], AX_X, ALU.add))
            link(nc.vector.tensor_scalar(word_f[:], expert_f[:], float(1 << EXPERT_BITS), None, ALU.mult))
            link(nc.vector.tensor_tensor(word_f[:, 1:], word_f[:, 1:], expert_f[:, 0:MOE_STEPS - 1], ALU.add))
            link(nc.vector.scalar_tensor_tensor(out=word_f[:, 0:MOE_STEPS - 1], in0=expert_f[:, 1:],
                                                scalar=float(1 << 2 * EXPERT_BITS), in1=word_f[:, 0:MOE_STEPS - 1],
                                                op0=ALU.mult, op1=ALU.add))
            link(nc.vector.tensor_copy(k.step_word[:], word_f[:]))

            def row(i, par):
                after(dve, s_put[par], i * 16 - 16 * par)
                link(normed(i, par, xt))
                nc.vector.tensor_scalar(xn[:, par, :], xt[:, par, :], t2.mean[:, bass.ds(i, 1)], t2.rstd[:, bass.ds(i, 1)],
                                        ALU.subtract, ALU.mult).then_inc(s_xn, 1)
            dve.wait_ge(s_turned, TILES)
            base = link.n
            per_expert = TILES // (EXP - 2)
            assert per_expert >= 2

            def counted(i, par):
                link.n = i + base
                row(i, par)

            def both_experts(pair, first=0):
                for n in range(first, 2 * per_expert):
                    counted(pair * (2 * per_expert) + n - 2 * per_expert, n % 2)
                    if n % per_expert == per_expert // 2 - 1:
                        low1(pair * 2 + n // per_expert, n // per_expert)
                    if n % per_expert == per_expert - 1:
                        low2(pair * 2 + n // per_expert, n // per_expert)
            counted(0, 0)
            both_experts(1, 1)
            with dve.Fori(2, EXP // 2) as pair:
                both_experts(pair)
            by_pairs(dve, (EXP - 2) * per_expert, TILES, counted)
            link.n = base + TILES


def experts(nc, k, a):
    with ExitStack() as own, nc.Block() as block:
        def sb(name, shape, dt=F32):
            return own.enter_context(nc.sbuf_tensor(name, shape, dt))

        def ps(name, shape):
            return own.enter_context(nc.psum_tensor(name, shape, F32))

        def sem(name):
            return own.enter_context(nc.semaphore(name))

        xin = sb("e_xin", [P, 2, WIDE, D])
        y = sb("e_y", [P, 2, WIDE, D])
        b2 = sb("e_b2", [P, EXP, D])
        s_xin, s_b2 = sem("e_xin_s"), sem("e_s_b2")
        s_load = [sem(f"e_load{i}") for i in range(2)]
        s_store = [sem(f"e_store{i}") for i in range(2)]

        def word(eng, i):
            return eng.value_load(k.step_word[0:1, bass.ds(i, 1)], min_val=0, max_val=(1 << 3 * EXPERT_BITS) - 1)

        def expert(eng, w, which):
            return field(nc, eng, w, which * EXPERT_BITS, EXP - 1)

        def weights(pe, w):
            near = (expert(pe, w, which) for which in (LAST, OWN, NEXT))
            return tuple(Weights(k.w1[:, e, 0], k.w1[:, e, 1], k.w2[:, e, 0], k.w2[:, e, 1]) for e in near)

        def gain(dve, w, which):
            e = expert(dve, w, which)
            return k.ln_cols[:, e, 0, :], k.ln_cols[:, e, 1, :]

        f = feed_forward(nc, sb, ps, sem, MOE_STEPS, WIDE, "e", ACT.Gelu, weights, lambda act, w: k.b1[:, expert(act, w, OWN), :], xin,
                         s_xin, gain, word)
        f.ident = k.ident[:]

        @block.gpsimd
        def _(pool):
            def landed(i, par):
                pool.wait_ge(s_load[1 - par], i * 8 + 8 * par)
                pool.sem_inc(s_xin, 1)

            def load(i, par):
                after(pool, f.s_turned, i - 1)
                pool.sem_inc(k.s_passed, 1)
                pool.dma_start(xin[:, par], k.rows_in[bass.ds(i * MP, MP), :].rearrange("(p w) d -> p w d", w=WIDE)).then_inc(s_load[par], 16)
                if not (isinstance(i, int) and i == 0):
                    landed(i, par)
            load(0, 0)
            load(1, 1)
            by_pairs(pool, 2, MOE_STEPS, load)
            landed(MOE_STEPS, MOE_STEPS % 2)

        @block.sync
        def _(sp):
            sp.dma_start(b2[:], a.e_b2.rearrange("e d -> (e d)").rearrange("(a n) -> a n", a=1).to_broadcast([P, EXP * D])
                         ).then_inc(s_b2, 16)

            def store(i, par):
                sp.wait_ge(f.s_y, i + 1)
                sp.dma_start(k.rows_out[bass.ds(i * MP, MP), :].rearrange("(p w) d -> p w d", w=WIDE), y[:, par]).then_inc(s_store[par], 16)
            by_pairs(sp, 0, MOE_STEPS, store)
            sp.wait_ge(s_store[0], 16 * (MOE_STEPS - MOE_STEPS // 2))
            sp.wait_ge(s_store[1], 16 * (MOE_STEPS // 2))

        @block.tensor
        def _(pe):
            f.pe(pe)

        @block.scalar
        def _(act):
            f.act(act)

        @block.vector
        def _(dve):
            def leave(i, par, w, which):
                e = expert(dve, w, which)
                dve.wait_ge(s_b2, 16)
                dve.wait_ge(f.s_down, i + 1)
                after(dve, s_store[par], i * 8 - 8 * par)
                nc.vector.tensor_tensor(y[:, par], f.ps_y[par][:], b2[:, e, :].unsqueeze(1).to_broadcast([P, WIDE, D]),
                                        ALU.add).then_inc(f.s_y, 1)
            f.dve(dve, lambda i, par: None, leave)


def combine(nc, k, a):
    with ExitStack() as own, nc.Block() as block:
        def sb(name, shape, dt=F32):
            return own.enter_context(nc.sbuf_tensor(name, shape, dt))

        def sem(name):
            return own.enter_context(nc.semaphore(name))

        slots = 4
        got = sb("got", [P, slots, TOPK, D])
        index = sb("c_index", [P, slots, TOPK], I32)
        s_idx, s_sum, s_out, s_first = (sem(n) for n in ("c_idx", "c_sum", "c_out", "c_first"))
        s_get = [sem(f"c_get{i}") for i in range(slots)]

        @block.gpsimd
        def _(pool):
            def get(i, slot):
                if not (isinstance(i, int) and i < slots):
                    pool.wait_ge(s_sum, i - (slots - 1))
                    pool.sem_inc(k.s_passed, 1)
                nc.gpsimd.tensor_copy(index[:, slot, :], k.place_i[:, i, :]).then_inc(s_idx, 1)
                pool.wait_ge(s_idx, i + 1)
                pool.sem_inc(k.s_passed, 1)
                for c in range(TOPK):
                    nc.gpsimd.indirect_dma_start(got[:, slot, c, :], None, k.rows_out, bass.IndirectOffsetOnAxis(
                        ap=index[:, slot, c:c + 1], axis=0)).then_inc(s_get[slot], 16)
            for i in range(slots):
                get(i, i)
            by_slots(pool, slots, TILES, slots, get)

        @block.vector
        def _(dve):
            def total(i, slot):
                per_tile = 16 * TOPK // slots
                dve.wait_ge(s_get[slot], i * per_tile + (slots - slot) * per_tile)
                nc.vector.scalar_tensor_tensor(out=k.acc[:, i, :], in0=got[:, slot, 0, :], scalar=k.share[:, i, 0:1],
                                               in1=k.acc[:, i, :], op0=ALU.mult, op1=ALU.add).then_inc(s_first, 1)
                dve.wait_ge(s_first, i + 1)
                nc.vector.scalar_tensor_tensor(out=k.acc[:, i, :], in0=got[:, slot, 1, :], scalar=k.share[:, i, 1:2],
                                               in1=k.acc[:, i, :], op0=ALU.mult, op1=ALU.add).then_inc(s_sum, 1)
            by_slots(dve, 0, TILES, slots, total)

        @block.sync
        def _(sp):
            def store(i, par):
                sp.wait_ge(s_sum, i + 1)
                sp.dma_start(a.out[bass.ds(i * P, P), :], k.acc[:, i, :]).then_inc(s_out, 16)
            by_pairs(sp, 0, FULL, store)
            sp.wait_ge(s_sum, TILES)
            sp.dma_start(a.out[FULL * P:N, :], k.acc[0:REST, FULL, :]).then_inc(s_out, 16)
            sp.wait_ge(s_out, 16 * TILES)


def gnn_moe_layer(nc, x, src, dst, g_W, g_as, g_ad, g_bias, g_Wres, ln1_g, ln1_b, ln2_g, ln2_b, f_w1, f_b1,
                  f_w2, f_b2, m_qkv, m_mem, m_wout, m_bout, m_gout, m_gpre, e_Wr, e_br, e_lng, e_lnb, e_W1,
                  e_b1, e_W2, e_b2, out):
    a = Names()
    a.x = x
    a.src = src
    a.dst = dst
    a.g_W = g_W
    a.g_as = g_as
    a.g_ad = g_ad
    a.g_bias = g_bias
    a.g_Wres = g_Wres
    a.ln1_g = ln1_g
    a.ln1_b = ln1_b
    a.ln2_g = ln2_g
    a.ln2_b = ln2_b
    a.f_w1 = f_w1
    a.f_b1 = f_b1
    a.f_w2 = f_w2
    a.f_b2 = f_b2
    a.m_qkv = m_qkv
    a.m_mem = m_mem
    a.m_wout = m_wout
    a.m_bout = m_bout
    a.m_gout = m_gout
    a.m_gpre = m_gpre
    a.e_Wr = e_Wr
    a.e_br = e_br
    a.e_lng = e_lng
    a.e_lnb = e_lnb
    a.e_W1 = e_W1
    a.e_b1 = e_b1
    a.e_W2 = e_W2
    a.e_b2 = e_b2
    a.out = out
    k = Names()
    with ExitStack() as top, nc.allow_non_contiguous_dma(reason="a few hundred small constants"):
        def keep(stack, name, shape, dt=F32):
            return stack.enter_context(nc.sbuf_tensor(name, shape, dt))

        def scratch(name, shape):
            return nc.dram_tensor(name, shape, F32, kind="Internal").ap()

        k.table = scratch("table", (NP, ROW))
        k.dst_f = scratch("dst_f", (GROUPS, EG))
        k.rows_in = scratch("rows_in", (MOE_STEPS * MP, D))
        k.rows_out = scratch("rows_out", (MOE_STEPS * MP, D))
        k.s_passed = top.enter_context(nc.semaphore("s_passed"))
        k.ident = keep(top, "ident", [P, P])
        k.ones = keep(top, "ones", [P, P])
        k.pidx = keep(top, "pidx", [P, 1])
        k.acc = keep(top, "acc", [P, TILES, D])
        k.acc_stats = keep(top, "acc_stats", [P, TILES, 6])
        with ExitStack() as graph:
            k.agg = keep(graph, "agg", [P, TILES, ROW])
            k.res = keep(graph, "res", [P, TILES, D])
            k.q = keep(graph, "q", [P, TILES, MC])
            k.xn0 = keep(graph, "xn0", [P, TILES, D])
            k.cw = keep(graph, "cw", [P, D])
            k.node_am = keep(graph, "node_am", [P, TILES, 2 * GH])
            k.bout, k.gout, k.g2, k.b2n, k.fb2 = (keep(graph, n, [P, D]) for n in ("bout", "gout", "g2", "b2n", "fb2"))
            k.iota_n = keep(graph, "iota_n", [P, NP])
            k.src_i = keep(graph, "src_i", [P, JG, GROUPS], I32)
            k.dst_e = keep(graph, "dst_e", [P, JG, GROUPS])
            k.node_id = keep(graph, "node_id", [P, TILES])
            k.items = keep(graph, "items", [1, WORDS], I32)
            k.need = keep(graph, "need", [1, NEED // NEED_PER], I32)
            k.far = keep(graph, "far", [1, 1], I32)
            setup_and_nodes(nc, k, a)
            exact_maxima(nc, k, a)
            graph_items(nc, k, a)
            nodes_finish(nc, k, a)
        k.w1 = keep(top, "w1", [P, EXP, 2, KT, HB, P], BF16)
        k.w2 = keep(top, "w2", [P, EXP, 2, HB, D], BF16)
        k.place_i = keep(top, "place_i", [P, TILES, TOPK], I32)
        k.share = keep(top, "share", [P, TILES, TOPK])
        k.step_word = keep(top, "step_word", [1, MOE_STEPS], I32)
        k.ln_cols = keep(top, "ln_cols", [P, EXP, 2, KT])
        k.b1 = keep(top, "e_b1", [P, EXP, HB])
        route(nc, k, a)
        experts(nc, k, a)
        combine(nc, k, a)


_INS = {
    "x": "x", "src": "src", "dst": "dst", "L0_gnn_W": "g_W", "L0_gnn_att_src": "g_as", "L0_gnn_att_dst": "g_ad",
    "L0_gnn_bias": "g_bias", "L0_gnn_W_res": "g_Wres", "L0_gnn_ln1_g": "ln1_g", "L0_gnn_ln1_b": "ln1_b",
    "L0_gnn_ln2_g": "ln2_g", "L0_gnn_ln2_b": "ln2_b", "L0_gnn_ffn_w1": "f_w1", "L0_gnn_ffn_b1": "f_b1",
    "L0_gnn_ffn_w2": "f_w2", "L0_gnn_ffn_b2": "f_b2", "L0_mix_w_qkv": "m_qkv", "L0_mix_mem_kv": "m_mem",
    "L0_mix_w_out": "m_wout", "L0_mix_b_out": "m_bout", "L0_mix_g_out": "m_gout", "L0_mix_g_pre": "m_gpre",
    "L0_ffn_Wr": "e_Wr", "L0_ffn_br": "e_br", "L0_ffn_ln_g": "e_lng", "L0_ffn_ln_b": "e_lnb", "L0_ffn_W1": "e_W1",
    "L0_ffn_b1": "e_b1", "L0_ffn_W2": "e_W2", "L0_ffn_b2": "e_b2",
}


def kernel(**inputs):
    import numpy as _np
    import concourse.bacc as _bacc
    from concourse import mybir as _mybir
    from concourse.bass_utils import run_bass_kernel_spmd as _run

    nc = _bacc.Bacc("TRN2", target_bir_lowering=False, num_devices=1)
    arrays, args = {}, {}
    for name, short in _INS.items():
        v = _np.ascontiguousarray(inputs[name])
        arrays[f"in_{name}_dram"] = v
        args[short] = nc.dram_tensor(f"in_{name}_dram", v.shape, _mybir.dt.from_np(v.dtype), kind="ExternalInput").ap()
    args["out"] = nc.dram_tensor("out_0_dram", (N, D), F32, kind="ExternalOutput").ap()
    gnn_moe_layer(nc, **args)
    r = _run(nc, [arrays], core_ids=[0])
    return r.results[0]["out_0_dram"]
```
